# Optimizing a Trainium2 kernel written in Bass

```python
import numpy as np
import jax
import jax.numpy as jnp

def _softmax(x, axis=-1):
    return jax.nn.softmax(x, axis=axis)

def _gelu(x):
    return jax.nn.gelu(x, approximate=True)

def _silu(x):
    return jax.nn.silu(x)

def _sigmoid(x):
    return jax.nn.sigmoid(x)

def _layernorm(x, axis=-1, eps=1e-05):
    m = jnp.mean(x, axis=axis, keepdims=True)
    v = jnp.var(x, axis=axis, keepdims=True)
    return (x - m) / jnp.sqrt(v + eps)

def _scatter_add(tgt, idx, src, axis=0):
    return tgt.at[idx].add(src)

def _segment_sum(src, seg, n):
    return jax.ops.segment_sum(src, seg, n)
kernel_name = 'mk_gnn_resnorm_d1_gnn_r32_787cc8'

def setup_inputs(seed: int=0):
    np.random.seed(seed)
    _w = jnp.asarray

    def _rec_inputs():
        import jax
        import jax.numpy as jnp
        _gk = jax.random.key(seed)
        x = -0.0004942 + 1 * jax.random.normal(jax.random.fold_in(_gk, 1), (3125, 128), jnp.float32)
        _s = jax.random.randint(jax.random.fold_in(_gk, 2), (50000,), 0, 3125, jnp.int32)
        _d = jax.random.randint(jax.random.fold_in(_gk, 3), (50000,), 0, 3125, jnp.int32)
        _loop = jnp.arange(3125, dtype=jnp.int32)
        src = jnp.concatenate([_s, _d, _loop])
        dst = jnp.concatenate([_d, _s, _loop])
        _o = jnp.argsort(dst, stable=True)
        src = src[_o]
        dst = dst[_o]
        edge_type_16 = jax.random.randint(jax.random.fold_in(_gk, 12), (103125,), 0, 16, jnp.int32)
        edge_weight = jax.random.uniform(jax.random.fold_in(_gk, 13), (103125,), jnp.float32, 0.0, 0.999998)
        return (x, src, dst, edge_type_16, edge_weight)
    x, src, dst, edge_type_16, edge_weight = _rec_inputs()

    def _L0_gnn_setup():
        import jax, jax.numpy as jnp
        import numpy as np
        N, E, D, R, H, L = (30000, 15000, 128, 16, 4, 3)
        DH = D // H
        key = jax.random.key(seed)
        ks = jax.random.split(key, 16)
        s = 1.0 / np.sqrt(D)
        return {'feat': jax.random.normal(ks[0], (N, D), jnp.float32), 'src': jax.random.randint(ks[1], (E,), 0, N, jnp.int32), 'dst': jax.random.randint(ks[2], (E,), 0, N, jnp.int32), 'etype': jax.random.randint(ks[3], (E,), 0, R, jnp.int32), 'temporal_weight': jax.random.uniform(ks[4], (E,), jnp.float32), 'W_rel': jax.random.normal(ks[5], (L, R, D, D), jnp.float32) * s, 'b_rel': jnp.zeros((L, D), jnp.float32), 'W_loop': jax.random.normal(ks[6], (L, D, D), jnp.float32) * s, 'W_gat': jax.random.normal(ks[7], (L, D, D), jnp.float32) * s, 'attn_l': jax.random.normal(ks[8], (L, H, DH), jnp.float32) * s, 'attn_r': jax.random.normal(ks[9], (L, H, DH), jnp.float32) * s, 'b_gat': jnp.zeros((L, D), jnp.float32), 'W_fuse': jax.random.normal(ks[10], (2 * D, D), jnp.float32) * (1.0 / np.sqrt(2 * D)), 'b_fuse': jnp.zeros((D,), jnp.float32), 'W_gate': jax.random.normal(ks[11], (D + 1, D), jnp.float32) * s, 'b_gate': jnp.zeros((D,), jnp.float32)}
    _L0_gnn_all = _L0_gnn_setup()
    _L0_gnn_in = {k: v for k, v in _L0_gnn_all.items() if k in ('W_rel', 'b_rel', 'W_loop', 'W_gat', 'attn_l', 'attn_r', 'b_gat', 'W_fuse', 'b_fuse', 'W_gate', 'b_gate')}
    del _L0_gnn_all
    return {'x': x, 'src': src, 'dst': dst, 'edge_type_16': edge_type_16, 'edge_weight': edge_weight, 'L0_gnn_W_rel': _L0_gnn_in['W_rel'], 'L0_gnn_b_rel': _L0_gnn_in['b_rel'], 'L0_gnn_W_loop': _L0_gnn_in['W_loop'], 'L0_gnn_W_gat': _L0_gnn_in['W_gat'], 'L0_gnn_attn_l': _L0_gnn_in['attn_l'], 'L0_gnn_attn_r': _L0_gnn_in['attn_r'], 'L0_gnn_b_gat': _L0_gnn_in['b_gat'], 'L0_gnn_W_fuse': _L0_gnn_in['W_fuse'], 'L0_gnn_b_fuse': _L0_gnn_in['b_fuse'], 'L0_gnn_W_gate': _L0_gnn_in['W_gate'], 'L0_gnn_b_gate': _L0_gnn_in['b_gate']}

def reference(x, src, dst, edge_type_16, edge_weight, L0_gnn_W_rel, L0_gnn_b_rel, L0_gnn_W_loop, L0_gnn_W_gat, L0_gnn_attn_l, L0_gnn_attn_r, L0_gnn_b_gat, L0_gnn_W_fuse, L0_gnn_b_fuse, L0_gnn_W_gate, L0_gnn_b_gate):
    import jax
    import jax.numpy as jnp

    def _L0_gnn_ref(feat, src, dst, etype, temporal_weight, W_rel, b_rel, W_loop, W_gat, attn_l, attn_r, b_gat, W_fuse, b_fuse, W_gate, b_gate):
        import jax, jax.numpy as jnp
        import numpy as np
        N, E, D, R, H, L = (30000, 15000, 128, 16, 4, 3)
        DH = D // H
        n = feat.shape[0]
        h = feat
        tw_mean = jnp.mean(temporal_weight)
        for l in range(L):
            ht = jnp.einsum('nd,rdo->nro', h, W_rel[l])
            msg = ht[src, etype]
            h_rel = jax.ops.segment_sum(msg, dst, num_segments=n)
            h_rel = h_rel + h @ W_loop[l] + b_rel[l]
            z = (h @ W_gat[l]).reshape(n, H, DH)
            el = jnp.sum(z * attn_l[l], axis=-1)
            er = jnp.sum(z * attn_r[l], axis=-1)
            e = jax.nn.leaky_relu(el[src] + er[dst], 0.2)
            m = jax.ops.segment_max(e, dst, num_segments=n)
            ex = jnp.exp(e - m[dst])
            denom = jax.ops.segment_sum(ex, dst, num_segments=n)
            alpha = ex / denom[dst]
            h_gat = jax.ops.segment_sum(alpha[:, :, None] * z[src], dst, num_segments=n)
            h_gat = h_gat.reshape(n, D) + b_gat[l]
            hc = jnp.concatenate([h_rel, h_gat], axis=1) @ W_fuse + b_fuse
            if l == 0:
                avg = jnp.full((n, 1), tw_mean, dtype=hc.dtype)
                gate = jax.nn.sigmoid(jnp.concatenate([hc, avg], axis=1) @ W_gate + b_gate)
                hc = hc * gate
            h = jax.nn.relu(hc)
        return h
    x = _layernorm(x + _L0_gnn_ref(x, src, dst, edge_type_16, edge_weight, L0_gnn_W_rel, L0_gnn_b_rel, L0_gnn_W_loop, L0_gnn_W_gat, L0_gnn_attn_l, L0_gnn_attn_r, L0_gnn_b_gat, L0_gnn_W_fuse, L0_gnn_b_fuse, L0_gnn_W_gate, L0_gnn_b_gate), axis=-1)
    return x

_drawn_inputs = setup_inputs


def setup_inputs(seed=0):
    import zlib

    import numpy as np

    out = dict(_drawn_inputs(seed))
    spreads = {'L0_gnn_b_rel': (0.0, 0.302),
     'L0_gnn_b_gat': (0.0, 0.327),
     'L0_gnn_b_fuse': (0.0, 0.1),
     'L0_gnn_b_gate': (0.0, 0.497)}
    factors = {'L0_gnn_attn_r': 2.929}
    for name, (base, spread) in spreads.items():
        noise = np.random.default_rng([zlib.crc32(name.encode()), seed]).standard_normal(out[name].shape)
        drawn = base * np.exp(spread * noise) if base else spread * noise
        out[name] = jnp.asarray(drawn.astype(out[name].dtype))
    for name, factor in factors.items():
        out[name] = (out[name] * factor).astype(out[name].dtype)
    return out
```

```python
from contextlib import ExitStack

import concourse.bass as bass
from concourse import mybir

ALU = mybir.AluOpType
ACT = mybir.ActivationFunctionType
AX = mybir.AxisListType
F32 = mybir.dt.float32
BF16 = mybir.dt.bfloat16
I32 = mybir.dt.int32
U32 = mybir.dt.uint32

P = 128
PAIR = 16
BLOCK = 64
ELL = BLOCK + PAIR
NEG = -1.0e30
SLOPE = 0.2
EPS = 1e-5


def gnn_kernel(nc, x, src, dst, etype, eweight, W_rel, b_rel, W_loop, W_gat, attn_l, attn_r, b_gat,
               W_fuse, b_fuse, W_gate, b_gate, out):
    N, D = x.shape
    E = src.shape[0]
    L, R = W_rel.shape[0], W_rel.shape[1]
    H, DH = attn_l.shape[1], attn_l.shape[2]
    assert D == P and H * DH == D
    T = -(-N // P)
    NP_ = T * P
    EP = 125
    EC = E // EP
    assert EP * EC == E
    ROW = 2 * D + H
    NULL = NP_ * R
    EX = DH + 1
    M_START, M_CNT, M_ID, M_ER = 0, 1, 2, 4
    M_LOOP = M_ER + H
    M_X = M_LOOP + D
    META = M_X + D
    ZW = D + H + H + D
    HB = 25
    assert EC % (3 * HB) == 0 and T % 2 == 1
    RC = R // 4
    assert RC * D == 512
    TAILS = (8, 4, 2, 1)
    RANKED_BY_VECTOR = T // 2 + 1
    KEYMAX = 4095
    assert NP_ <= KEYMAX + 1

    with ExitStack() as ctx:
        def sb(name, shape, dt=F32):
            return ctx.enter_context(nc.sbuf_tensor(name, shape, dt))

        def ps(name, shape):
            return ctx.enter_context(nc.psum_tensor(name, shape, F32))

        def sem(name):
            return ctx.enter_context(nc.semaphore(name))

        def dram(name, shape, dt=F32):
            return nc.dram_tensor(name, shape, dt).ap()

        table = [dram(f"table{i}", [NP_ * R + 1, ROW]) for i in range(2)]
        edge_rows = dram("edge_rows", [E + ELL, 1], I32)
        edge_rows_raw = dram("edge_rows_raw", [E, 1], I32)
        edge_cells = dram("edge_cells", [E, 1], I32)
        cursors = dram("cursors", [NP_, 1])
        keys = dram("keys", [NP_, 1])
        meta_ranked = dram("meta_ranked", [NP_, META])
        plan_dram = dram("plan_dram", [T, 8], I32)

        ident = sb("ident", [P, P])
        ones = sb("ones", [P, P])
        upper = sb("upper", [P, P])
        iota_row = sb("iota_row", [P, P], BF16)
        iota_slot = sb("iota_slot", [P, ELL])
        null_row = sb("null_row", [P, ROW])
        zeros_bf = sb("zeros_bf", [P, P], BF16)
        tail_idx = sb("tail_idx", [P, ELL], I32)

        wrel = sb("wrel", [P, L, R * D])
        wz = sb("wz", [P, L, ZW])
        attn = sb("attn", [P, 2, L, D])
        attn_tmp = sb("attn_tmp", [P, D])
        wfuse = sb("wfuse", [P, 2, D])
        wgate = sb("wgate", [P, D])
        brel = sb("brel", [P, L])
        bgat = sb("bgat", [P, L])
        bfuse = sb("bfuse", [P, 1])
        bfuse_row = sb("bfuse_row", [1, D])
        bgate = sb("bgate", [P, 2])
        gate_bias = sb("gate_bias", [P, 1])
        wsum = sb("wsum", [P, 2])
        tw_mean = sb("tw_mean", [P, 1])

        meta_nat = sb("meta_nat", [P, T, META])
        meta = sb("meta", [P, T, META])
        xin = [sb(f"xin{i}", [P, D]) for i in range(2)]
        hT = [sb(f"hT{i}", [P, P]) for i in range(2)]
        rows = [sb(f"rows{i}", [P, R, ROW]) for i in range(2)]
        degree = sb("degree", [P, T])
        before = sb("before", [P, T])
        key = sb("key", [P, T])
        negkey = sb("negkey", [P, T])
        key_bc = sb("key_bc", [P, NP_])
        assert T * ELL <= NP_
        starts = sb("starts", [P, T])
        rank = sb("rank", [P, T])
        rank_u = sb("rank_u", [P, T], U32)
        start_u = sb("start_u", [P, T], U32)
        cnt_r = sb("cnt_r", [P, T])
        id_u = sb("id_u", [P, T], U32)
        ell = sb("ell", [P, T + 1, ELL], I32)
        ell_valid = key_bc[:, 0:T * ELL].rearrange("p (t j) -> p t j", t=T)
        plan_f = sb("plan_f", [T, 1])
        plan_i = sb("plan_i", [T, 8], I32)
        plan_c = sb("plan_c", [T, 8], I32)
        plan = sb("plan", [1, T * 8], I32)

        dst_i = sb("dst_i", [EP, EC], I32)
        dst_next = sb("dst_next", [EP, EC], I32)
        src_i = sb("src_i", [EP, EC], I32)
        typ_i = sb("typ_i", [EP, EC], I32)
        lo_bf = sb("lo_bf", [EP, EC], BF16)
        hi_bf = sb("hi_bf", [EP, EC], BF16)
        lo_i = sb("lo_i", [EP, EC], I32)
        hi_i = sb("hi_i", [EP, EC], I32)
        ew = sb("ew", [EP, EC])
        oh_lo = [sb(f"oh_lo{i}", [P, HB, P], BF16) for i in range(3)]
        oh_hi = [sb(f"oh_hi{i}", [P, HB, T], BF16) for i in range(3)]
        assert HB * P == NP_
        waste = [oh_lo[i][:].rearrange("p b c -> p (b c)") for i in range(2)]
        sort_key = sb("sort_key", [EP, 1], U32)
        sort_val = sb("sort_val", [EP, 1], I32)
        sort_keys = sb("sort_keys", [EP, EP], U32)
        sort_cur = sb("sort_cur", [EP, 1])
        sort_pos = sb("sort_pos", [EP, 1], U32)
        sort_new = sb("sort_new", [EP, 1])
        sort_cell = sb("sort_cell", [EP, 1], U32)
        sort_f = sb("sort_f", [EP, 4])
        sort_eq = sb("sort_eq", [EP, 2, EP])
        unsorted_f = sb("unsorted_f", [P, 1])
        unsorted_i = sb("unsorted_i", [1, 1], I32)

        GA = ("A", "B", "t4", "t2", "t1")
        GK = dict(A=8, B=8, t4=4, t2=2, t1=1)
        assert sum(GK.values()) * ROW <= T * META
        room = meta_nat[:].rearrange("p t f -> p (t f)")
        slots, used = {}, 0
        for b in GA:
            slots[b] = room[:, used:used + GK[b] * ROW].rearrange("p (k f) -> p k f", k=GK[b])
            used += GK[b] * ROW
        stage = {b: sb(f"stage_{b}", [P, GK[b]], U32) for b in GA}
        stage_id = sb("stage_id", [P, 1], U32)
        tick = sb("tick", [1, 4])
        blk_start = sb("blk_start", [P, 1])
        blk_left = sb("blk_left", [P, 1])
        blk_start_u = sb("blk_start_u", [P, 1], U32)
        blk_f = sb("blk_f", [P, 2, ELL])
        er_cur = sb("er_cur", [P, 1, H])
        raw = sb("raw", [P, 9, H])
        leaky = sb("leaky", [P, 9, H])
        top = sb("top", [P, 1, H])
        peak = sb("peak", [P, 1, H])
        logit = sb("logit", [P, 9, H])
        zx = sb("zx", [P, 9, H, EX])
        acc = sb("acc", [P, H, EX])
        rden = sb("rden", [P, H, 1])
        hg = sb("hg", [P, H, DH])
        hr = sb("hr", [P, D])
        hrT = sb("hrT", [P, P])
        hgT = sb("hgT", [P, P])
        hc = sb("hc", [P, P])
        th = sb("th", [P, P])
        y = sb("y", [P, D])
        yo = sb("yo", [P, D])
        stats = sb("stats", [P, 6])
        mv = sb("mv", [P, 2])
        ve = sb("ve", [P, 1])
        nv = sb("newton", [P, 2])
        nv_i = sb("newton_i", [P, 1], I32)

        ps_rel = ps("ps_rel", [P, 512])
        ps_gat = ps("ps_gat", [P, 512])
        ps_mix = ps("ps_mix", [P, 512])
        ps_z = ps("ps_z", [P, 512])
        ps_tab = [ps(f"ps_tab{i}", [P, 512]) for i in range(2)]
        ps_cnt = ps("ps_cnt", [P, 512])
        mix = [ps_mix[:, 128 * i:128 * i + 128] for i in range(4)]

        s_const = sem("const_ready")
        s_wload = sem("weights_loaded")
        s_bload = sem("biases_loaded")
        s_eload = sem("edges_loaded")
        s_ewload = sem("edge_weights_loaded")
        s_xload = sem("x_loaded_to_meta")
        s_xin = [sem(f"xin{i}_loaded") for i in range(2)]
        s_xin_used = [sem(f"xin{i}_used") for i in range(2)]
        s_xT_ps = sem("xT_in_psum")
        s_hT = [sem(f"hT{i}_ready") for i in range(2)]
        s_z_ps = sem("z_product_ready")
        s_chunk = [sem(f"table_chunk{c}_ready") for c in range(4)]
        s_bank = [sem(f"bank_free_for_chunk{c}") for c in range(4)]
        s_rows = sem("rows_ready")
        s_saved = [sem(f"rows{i}_saved") for i in range(2)]
        s_v = sem("vector_step")
        s_uns_in = sem("order_violations_ready")
        s_fold = sem("attention_fold_step")
        s_wz = sem("wz_ready")
        s_tws = sem("edge_weight_sums_ready")
        s_gbias = sem("gate_bias_ready")
        s_edge_rows = sem("edge_rows_computed")
        s_edge_saved = sem("edge_rows_saved")
        s_oh = [sem(f"onehots{i}_ready") for i in range(3)]
        s_oh_used = [sem(f"onehots{i}_used") for i in range(3)]
        s_hist = sem("histogram_ready")
        s_deg = sem("degrees_ready")
        s_start_ps = sem("starts_and_totals_ready")
        s_key = sem("keys_ready")
        s_key_saved = sem("keys_saved")
        s_key_bc = sem("keys_broadcast")
        s_rank_act = sem("ranks_by_scalar_ready")
        s_rank = sem("ranks_ready")
        s_scatter = sem("meta_scattered")
        s_meta = sem("ranked_meta_loaded")
        s_meta_cols = sem("ranked_columns_ready")
        s_deg_ps = sem("transposed_degrees_ready")
        s_plan_i = sem("plan_computed")
        s_plan_saved = sem("plan_saved")
        s_plan = sem("plan_loaded")
        s_ell = sem("ell_gathered")
        s_ell_ok = sem("ell_ready")
        s_stored = sem("rows_stored")
        s_uns = sem("order_flag_ready")
        s_cur = sem("cursors_saved")
        s_sort_ld = sem("sort_chunk_loaded")
        s_sort_cur = sem("sort_cursors_gathered")
        s_sort_v = sem("sort_positions_ready")
        s_sort_c = sem("sort_vector_step")
        s_sort_st = sem("sort_chunk_stored")
        s_copy = sem("raw_edge_rows_copied")
        s_staged = sem("slot_indices_staged")
        s_blk = sem("block_step")
        s_blk_ld = sem("block_fetched")
        s_landed = {b: sem(f"slots_{b}_landed") for b in GA}
        s_free = {b: sem(f"slots_{b}_free") for b in GA}
        s_tile = sem("tile_started")
        s_raw = sem("raw_logits_ready")
        s_top = sem("running_top_ready")
        s_leaky = sem("leaky_ready")
        s_peak = sem("peak_ready")
        s_keep = sem("top_kept")
        s_logit = sem("logits_ready")
        s_wgt = sem("weights_ready")
        s_zx = sem("weighted_z_ready")
        s_scaled = sem("sums_rescaled")
        s_gat = sem("group_sum_ready")
        s_acc = sem("sums_updated")
        s_rden = sem("denominators_inverted")
        s_h2 = sem("node_sums_ready")
        s_T_ps = sem("node_sums_transposed")
        s_T = sem("transposed_sums_ready")
        s_fuse = sem("fused_in_psum")
        s_hc = sem("fused_ready")
        s_gate_ps = sem("gate_in_psum")
        s_th = sem("gate_ready")
        s_id = sem("ids_staged")
        s_norm = sem("norm_step")
        s_gated = sem("gating_step")
        s_yo = sem("normed_ready")
        s_out = sem("output_saved")

        def bc(ap, n):
            return ap.rearrange("p (o f) -> p o f", o=1).to_broadcast([ap.shape[0], n, ap.shape[1]])

        def bc_last(ap, n):
            return ap.rearrange("p (f o) -> p f o", o=1).to_broadcast([ap.shape[0], ap.shape[1], n])

        def counter(eng, name, value):
            reg = eng.alloc_register(name)
            eng.reg_mov(reg, value)
            return reg

        def load_plan(eng, t, columns):
            limits = [(1, E // PAIR + 1), (0, 1), (0, 1), (0, 1), (0, 1), (1, E // BLOCK + 1)]
            return [eng.value_load(plan[0:1, bass.ds(t * 8 + c, 1)], min_val=limits[c][0], max_val=limits[c][1])
                    for c in columns]

        block = ctx.enter_context(nc.Block())

        @block.sync
        def _(sp):
            sp.dma_start(dst_i[:], dst.rearrange("(p c) -> p c", p=EP)).then_inc(s_eload, 16)
            sp.dma_start(dst_next[0:EP - 1, :], dst[1:1 + (EP - 1) * EC].rearrange("(p c) -> p c", p=EP - 1)
                         ).then_inc(s_eload, 16)
            sp.dma_start(dst_next[EP - 1:EP, 0:EC - 1],
                         dst[(EP - 1) * EC + 1:E].rearrange("(p c) -> p c", p=1)).then_inc(s_eload, 16)
            sp.dma_start(dst_next[EP - 1:EP, EC - 1:EC],
                         dst[E - 1:E].rearrange("(p c) -> p c", p=1)).then_inc(s_eload, 16)
            sp.dma_start(src_i[:], src.rearrange("(p c) -> p c", p=EP)).then_inc(s_eload, 16)
            sp.dma_start(typ_i[:], etype.rearrange("(p c) -> p c", p=EP)).then_inc(s_eload, 16)
            for i in range(2):
                sp.dma_start(xin[i][:], x[i * P:(i + 1) * P, :]).then_inc(s_xin[i], 16)
            sp.dma_start(ew[:], eweight.rearrange("(p c) -> p c", p=EP)).then_inc(s_ewload, 16)
            sp.dma_start(wz[:, :, 0:D], W_gat.rearrange("l d o -> d l o")).then_inc(s_wload, 16)
            sp.dma_start(wz[:, :, D + 2 * H:ZW], W_loop.rearrange("l d o -> d l o")).then_inc(s_wload, 16)
            for i, a in enumerate((attn_l, attn_r)):
                sp.dma_start(attn[:, i].rearrange("p l d -> p (l d)"),
                             a.rearrange("(o l) h c -> o (l h c)", o=1).to_broadcast([P, L * D])
                             ).then_inc(s_wload, 16)
            sp.dma_start(wrel[:, 0].rearrange("p (r o) -> p r o", r=R), W_rel[0].rearrange("r d o -> d r o")
                         ).then_inc(s_wload, 16)
            sp.dma_start(wfuse[:], W_fuse.rearrange("(k d) o -> d k o", k=2)).then_inc(s_bload, 16)
            sp.dma_start(wgate[:], W_gate[0:D, :]).then_inc(s_bload, 16)
            for l in range(L):
                sp.dma_start(brel[:, l:l + 1], b_rel[l].rearrange("(p o) -> p o", o=1)).then_inc(s_bload, 16)
                sp.dma_start(bgat[:, l:l + 1], b_gat[l].rearrange("(p o) -> p o", o=1)).then_inc(s_bload, 16)
            sp.dma_start(bfuse[:], b_fuse.rearrange("(p o) -> p o", o=1)).then_inc(s_bload, 16)
            sp.dma_start(bfuse_row[:], b_fuse.rearrange("(o p) -> o p", o=1)).then_inc(s_bload, 16)
            sp.dma_start(bgate[:, 0:1], b_gate.rearrange("(p o) -> p o", o=1)).then_inc(s_bload, 16)
            sp.dma_start(bgate[:, 1:2], W_gate[D].rearrange("(p o) -> p o", o=1)).then_inc(s_bload, 16)
            for l in range(1, L):
                sp.dma_start(wrel[:, l].rearrange("p (r o) -> p r o", r=R), W_rel[l].rearrange("r d o -> d r o")
                             ).then_inc(s_bload, 16)
            sp.wait_ge(s_const, 2)
            sp.dma_start(meta_nat[:, 0:T - 1, M_X:META], x[0:(T - 1) * P, :].rearrange("(t p) d -> p t d", p=P)
                         ).then_inc(s_xload, 16)
            sp.dma_start(meta_nat[0:N - (T - 1) * P, T - 1, M_X:META], x[(T - 1) * P:N, :]).then_inc(s_xload, 16)
            n = counter(sp, "sp_pair", 1)
            n_rows = counter(sp, "sp_rows", 1)

            def save_rows(t, k):
                sp.reg_add(n_rows, n_rows, 1)
                sp.wait_ge(s_rows, n_rows)
                sp.dma_start(table[0][bass.ds(t * (P * R), P * R), :].rearrange("(p r) f -> p (r f)", r=R),
                             rows[k][:].rearrange("p r f -> p (r f)")).then_inc(s_saved[k], 16)

            with sp.Fori(0, (T - 3) // 2) as i:
                for k in range(2):
                    sp.wait_ge(s_xin_used[k], n)
                    sp.dma_start(xin[k][:], x[bass.ds((i * 2 + 2 + k) * P, P), :]).then_inc(s_xin[k], 16)
                    save_rows(i * 2 + k, k)
                sp.reg_add(n, n, 1)
            sp.wait_ge(s_xin_used[0], n)
            sp.dma_start(xin[0][0:N - (T - 1) * P, :], x[(T - 1) * P:N, :]).then_inc(s_xin[0], 16)
            save_rows(T - 3, 0)
            save_rows(T - 2, 1)
            sp.reg_add(n, n, 1)
            save_rows(T - 1, 0)

        @block.gpsimd
        def _(pool):
            g = nc.gpsimd
            g.memset(meta_nat[:, T - 1, :], 0.0).then_inc(s_const, 1)
            g.memset(ones[:], 1.0).then_inc(s_const, 1)
            pool.wait_ge(s_const, 2)
            g.affine_select(out=ident[:], in_=ones[:], pattern=[[-1, P]], compare_op=ALU.is_equal, fill=0.0,
                            base=0, channel_multiplier=1).then_inc(s_const, 1)
            g.affine_select(out=upper[:], in_=ones[:], pattern=[[1, P]], compare_op=ALU.is_gt, fill=0.0,
                            base=0, channel_multiplier=-1).then_inc(s_const, 1)
            g.iota(iota_row[:], [[1, P]], base=0, channel_multiplier=0,
                   allow_small_or_imprecise_dtypes=True).then_inc(s_const, 1)
            g.iota(iota_slot[:], [[1, ELL]], base=0, channel_multiplier=0,
                   allow_small_or_imprecise_dtypes=True).then_inc(s_const, 1)
            g.memset(zeros_bf[:], 0.0).then_inc(s_const, 1)
            g.memset(tail_idx[:], 0).then_inc(s_const, 1)
            g.memset(tick[:], 0.0)
            g.memset(null_row[:, 0:2 * D], 0.0).then_inc(s_const, 1)
            g.memset(null_row[:, 2 * D:ROW], NEG).then_inc(s_const, 1)
            g.iota(meta_nat[:, :, M_ID], [[P, T]], base=0, channel_multiplier=1,
                   allow_small_or_imprecise_dtypes=True).then_inc(s_const, 1)
            g.memset(meta_nat[:, 0:T - 1, 3], 0.0).then_inc(s_const, 1)
            pool.wait_ge(s_const, 12)
            pool.dma_start(table[0][NULL:NULL + 1, :], null_row[0:1, :]).then_inc(s_stored, 16)
            pool.dma_start(table[1][NULL:NULL + 1, :], null_row[0:1, :]).then_inc(s_out, 16)
            pool.dma_start(edge_rows[E:E + ELL, :].rearrange("(o c) k -> o (c k)", o=1), tail_idx[0:1, :]
                           ).then_inc(s_edge_saved, 16)
            pool.wait_ge(s_edge_rows, 1)
            pool.dma_start(edge_rows[0:E, :].rearrange("(p c) o -> p (c o)", p=EP), src_i[:]
                           ).then_inc(s_edge_saved, 16)
            pool.wait_ge(s_edge_rows, 2)
            pool.dma_start(edge_cells[:].rearrange("(p c) o -> p (c o)", p=EP), typ_i[:]
                           ).then_inc(s_edge_saved, 16)
            pool.wait_ge(s_key, 1)
            pool.dma_start(keys[:].rearrange("(p t) o -> p (t o)", t=T), key[:]).then_inc(s_key_saved, 16)
            pool.dma_start(cursors[:].rearrange("(p t) o -> p (t o)", t=T), starts[:]).then_inc(s_cur, 16)
            pool.wait_ge(s_key_saved, 16)
            pool.dma_start(key_bc[:], keys[:].rearrange("k o -> o k").to_broadcast([P, NP_])
                           ).then_inc(s_key_bc, 16)
            pool.wait_ge(s_uns, 1)
            pool.wait_ge(s_edge_saved, 48)
            pool.wait_ge(s_cur, 16)
            bad = pool.value_load(unsorted_i[0:1, 0:1], min_val=0, max_val=1)
            with pool.If(bad > 0):
                pool.dma_start(edge_rows_raw[:].rearrange("(p c) o -> p (c o)", p=EP),
                               edge_rows[0:E, :].rearrange("(p c) o -> p (c o)", p=EP)).then_inc(s_copy, 16)
                pool.wait_ge(s_copy, 16)
                n_ld, n_v, n_st = (counter(pool, f"pool_sort{i}", v) for i, v in enumerate((48, 1, 32)))
                n_cur = counter(pool, "pool_sort3", 16)
                with pool.Fori(0, EC) as c:
                    at = c * EP
                    pool.dma_start(sort_key[:], edge_cells[bass.ds(at, EP), :].bitcast(U32)).then_inc(s_sort_ld, 16)
                    pool.dma_start(sort_val[:], edge_rows_raw[bass.ds(at, EP), :]).then_inc(s_sort_ld, 16)
                    pool.dma_start(sort_keys[:], edge_cells[bass.ds(at, EP), :].bitcast(U32).rearrange("c o -> o c")
                                   .to_broadcast([EP, EP])).then_inc(s_sort_ld, 16)
                    pool.wait_ge(s_sort_ld, n_ld)
                    pool.reg_add(n_ld, n_ld, 48)
                    pool.indirect_dma_start(
                        out=sort_cur[:], out_offset=None, in_=cursors[:],
                        in_offset=bass.IndirectOffsetOnAxis(ap=sort_key[:], axis=0)
                    ).then_inc(s_sort_cur, 16)
                    pool.wait_ge(s_sort_cur, n_cur)
                    pool.reg_add(n_cur, n_cur, 16)
                    pool.wait_ge(s_sort_v, n_v)
                    pool.reg_add(n_v, n_v, 1)
                    pool.indirect_dma_start(
                        out=edge_rows[:], out_offset=bass.IndirectOffsetOnAxis(ap=sort_pos[:], axis=0),
                        in_=sort_val[:], in_offset=None).then_inc(s_sort_st, 16)
                    pool.indirect_dma_start(
                        out=cursors[:], out_offset=bass.IndirectOffsetOnAxis(ap=sort_cell[:], axis=0),
                        in_=sort_new[:], in_offset=None, bounds_check=NP_ - 1, oob_is_err=False
                    ).then_inc(s_sort_st, 16)
                    pool.wait_ge(s_sort_st, n_st)
                    pool.reg_add(n_st, n_st, 32)
            pool.wait_ge(s_rank, 1)
            pool.wait_ge(s_rows, T + 1)
            pool.wait_ge(s_xload, 32)
            for t in range(T):
                pool.indirect_dma_start(
                    out=meta_ranked[:], out_offset=bass.IndirectOffsetOnAxis(ap=rank_u[:, t:t + 1], axis=0),
                    in_=meta_nat[:, t, :], in_offset=None).then_inc(s_scatter, 16)
            pool.wait_ge(s_scatter, 16 * T)
            pool.dma_start(meta[:], meta_ranked[:].rearrange("(t p) f -> p t f", p=P)).then_inc(s_meta, 16)
            pool.wait_ge(s_meta_cols, 3)
            for t in range(T):
                pool.indirect_dma_start(
                    out=ell[:, t, :], out_offset=None, in_=edge_rows[:],
                    in_offset=bass.IndirectOffsetOnAxis(ap=start_u[:, t:t + 1], axis=0)).then_inc(s_ell, 16)
            pool.wait_ge(s_plan_i, 1)
            pool.dma_start(plan_dram[:], plan_i[:]).then_inc(s_plan_saved, 16)
            pool.wait_ge(s_plan_saved, 16)
            pool.dma_start(plan[:], plan_dram[:].rearrange("(o t) c -> o (t c)", o=1)).then_inc(s_plan, 16)
            pool.wait_ge(s_plan, 16)

            pool.wait_ge(s_ell_ok, 1)
            pool.wait_ge(s_stored, 16)
            pool.wait_ge(s_out, 16)
            n_staged = counter(pool, "pool_staged", 1)
            n_blk = counter(pool, "pool_blk", 1)
            n_blk_ld = counter(pool, "pool_blk_ld", 16)
            n_free = {b: counter(pool, f"pool_free_{b}", 1) for b in GA}
            n_epi = counter(pool, "pool_epi", 1)
            at = counter(pool, "pool_at", 0)
            left = counter(pool, "pool_left", 0)
            ell_flat = ell[:].rearrange("p t j -> p (t j)")

            def gather(l, b):
                K = GK[b]
                pool.wait_ge(s_free[b], n_free[b])
                pool.reg_add(n_free[b], n_free[b], 1)
                here = pool.snap(at, min_val=0, max_val=(T + 1) * ELL - K)
                g.tensor_copy(stage[b][:].bitcast(I32), ell_flat[:, bass.ds(here, K)]).then_inc(s_staged, 1)
                pool.reg_add(at, at, K)
                pool.wait_ge(s_staged, n_staged)
                pool.reg_add(n_staged, n_staged, 1)
                for k in range(K):
                    pool.indirect_dma_start(
                        out=slots[b][:, k, :], out_offset=None, in_=table[l % 2],
                        in_offset=bass.IndirectOffsetOnAxis(ap=stage[b][:, k:k + 1], axis=0)
                    ).then_inc(s_landed[b], 16)

            def next_block(t, first):
                def done():
                    pool.wait_ge(s_blk, n_blk)
                    pool.reg_add(n_blk, n_blk, 1)

                with pool.If(first):
                    g.tensor_copy(blk_start[:], meta[:, bass.ds(t, 1), M_START]).then_inc(s_blk, 1)
                    done()
                    g.tensor_copy(blk_left[:], meta[:, bass.ds(t, 1), M_CNT]).then_inc(s_blk, 1)
                    done()
                g.tensor_scalar(blk_start[:], blk_start[:], float(BLOCK), float(E), ALU.add, ALU.min
                                ).then_inc(s_blk, 1)
                done()
                g.tensor_scalar(blk_left[:], blk_left[:], -float(BLOCK), None, ALU.add).then_inc(s_blk, 1)
                done()
                g.tensor_copy(blk_start_u[:], blk_start[:]).then_inc(s_blk, 1)
                done()
                pool.indirect_dma_start(
                    out=ell[:, T, :], out_offset=None, in_=edge_rows[:],
                    in_offset=bass.IndirectOffsetOnAxis(ap=blk_start_u[:], axis=0)).then_inc(s_blk_ld, 16)
                pool.wait_ge(s_blk_ld, n_blk_ld)
                pool.reg_add(n_blk_ld, n_blk_ld, 16)
                g.tensor_scalar(blk_f[:, 0], iota_slot[:], blk_left[:], None, ALU.is_lt).then_inc(s_blk, 1)
                done()
                g.tensor_scalar(blk_f[:, 1], ell[:, T, :], -float(NULL), None, ALU.add).then_inc(s_blk, 1)
                done()
                g.tensor_tensor(blk_f[:, 0], blk_f[:, 0], blk_f[:, 1], ALU.mult).then_inc(s_blk, 1)
                done()
                g.tensor_scalar(ell[:, T, :], blk_f[:, 0], float(NULL), None, ALU.add).then_inc(s_blk, 1)
                done()

            def store_tile(l, t):
                if l < L - 1:
                    pool.wait_ge(s_rows, n_rows_pool)
                    pool.reg_add(n_rows_pool, n_rows_pool, 1)
                else:
                    pool.wait_ge(s_yo, n_yo)
                    pool.reg_add(n_yo, n_yo, 1)
                g.tensor_tensor(tick[:, 1:2], tick[:, 0:1], tick[:, 0:1], ALU.add)
                g.tensor_copy(stage_id[:].bitcast(I32), id_u[:, bass.ds(t, 1)].bitcast(I32)).then_inc(s_id, 1)
                pool.wait_ge(s_id, n_epi)
                pool.reg_add(n_epi, n_epi, 2)
                g.tensor_tensor(tick[:, 2:3], tick[:, 0:1], tick[:, 0:1], ALU.add).then_inc(s_id, 1)
                if l < L - 1:
                    pool.indirect_dma_start(
                        out=table[(l + 1) % 2][0:NP_ * R, :].rearrange("(n r) f -> n (r f)", r=R),
                        out_offset=bass.IndirectOffsetOnAxis(ap=stage_id[:], axis=0),
                        in_=rows[0][:].rearrange("p r f -> p (r f)"), in_offset=None).then_inc(s_stored, 16)
                else:
                    pool.indirect_dma_start(
                        out=out, out_offset=bass.IndirectOffsetOnAxis(ap=stage_id[:], axis=0),
                        in_=yo[:], in_offset=None, bounds_check=N - 1, oob_is_err=False).then_inc(s_out, 16)

            n_rows_pool = counter(pool, "pool_rows", T + 2)
            n_yo = counter(pool, "pool_yo", 1)

            def tile(l, t):
                pairs, *has, blocks = load_plan(pool, t, range(6))
                pool.reg_mov(at, t * ELL)
                pool.reg_mov(left, pairs)
                with pool.Fori(0, blocks) as b:
                    with pool.If(b >= 1):
                        next_block(t, b < 2)
                        pool.reg_mov(at, T * ELL)
                    now = counter(pool, f"pool_now{l}_{nc.next_id()}", 0)
                    pool.reg_alu(now, left, BLOCK // PAIR, ALU.min)
                    pool.reg_sub(left, left, now)
                    with pool.Fori(0, pool.snap(now, min_val=1, max_val=BLOCK // PAIR)):
                        gather(l, "A")
                        gather(l, "B")
                for h, b in zip(has, ("A", "t4", "t2", "t1")):
                    with pool.If(h > 0):
                        gather(l, b)

            for l in range(L):
                if l == 0:
                    pool.wait_ge(s_saved[0], 16 * ((T + 1) // 2))
                    pool.wait_ge(s_saved[1], 16 * ((T - 1) // 2))
                else:
                    pool.wait_ge(s_stored, 16 * (1 + l * T))
                tile(l, 0)
                with pool.Fori(1, T) as t:
                    tile(l, t)
                    store_tile(l, t - 1)
                store_tile(l, T - 1)
            pool.wait_ge(s_out, 16 * (1 + T))

        @block.scalar
        def _(act):
            s = nc.scalar
            n_tab = counter(act, "act_tab", 1)
            n_saved = [counter(act, f"act_saved{k}", 16) for k in range(2)]

            def evacuate_table(k, meta_col):
                act.wait_ge(s_z_ps, n_tab)
                s.activation(rows[k][:, :, D:ROW], bc(ps_z[:, 0:D + H], R), ACT.Copy)
                for c in range(4):
                    act.wait_ge(s_chunk[c], n_tab)
                    s.activation(rows[k][:, c * RC:(c + 1) * RC, 0:D],
                                     ps_tab[c % 2][:].rearrange("p (r f) -> p r f", r=RC), ACT.Copy
                                 ).then_inc(s_bank[(c + 2) % 4], 1)
                s.activation(meta_col, ps_z[:, D + H:ZW].rearrange("p (o f) -> p o f", o=1), ACT.Copy
                             ).then_inc(s_rows, 1)
                act.reg_add(n_tab, n_tab, 1)

            act.sem_inc(s_bank[0], 1)
            act.sem_inc(s_bank[1], 1)
            act.sem_inc(s_rows, 1)

            def natural_tile(t, k, first):
                act.wait_ge(s_xT_ps, n_tab)
                s.activation(hT[k][:], mix[0], ACT.Copy).then_inc(s_hT[k], 1)
                if not first:
                    act.wait_ge(s_saved[k], n_saved[k])
                    act.reg_add(n_saved[k], n_saved[k], 16)
                evacuate_table(k, meta_nat[:, bass.ds(t, 1), M_ER:M_X])

            act.wait_ge(s_const, 12)
            natural_tile(0, 0, True)
            natural_tile(1, 1, True)
            with act.Fori(1, (T - 1) // 2) as i:
                natural_tile(2 * i, 0, False)
                natural_tile(2 * i + 1, 1, False)
            natural_tile(T - 1, 0, False)

            act.wait_ge(s_key_bc, 16)
            act.wait_ge(s_key, 1)
            for t in range(RANKED_BY_VECTOR, T):
                if t > RANKED_BY_VECTOR:
                    act.wait_ge(s_rank_act, t - RANKED_BY_VECTOR)
                s.activation(waste[1], key_bc[:], ACT.Sign, bias=negkey[:, t:t + 1],
                             accum_out=rank[:, t:t + 1]).then_inc(s_rank_act, 1)

            n_g = counter(act, "act_group", 1)
            n_e = counter(act, "act_epi", 1)

            def group(K):
                act.wait_ge(s_logit, n_g)
                s.activation(zx[:, 8 - K:9, :, DH], logit[:, 8 - K:9, :], ACT.Exp).then_inc(s_wgt, 1)
                act.reg_add(n_g, n_g, 1)

            def transposed(l):
                act.wait_ge(s_T_ps, n_e)
                s.activation(hrT[:], mix[0], ACT.Identity, bias=brel[:, l:l + 1])
                s.activation(hgT[:], mix[1], ACT.Identity, bias=bgat[:, l:l + 1]).then_inc(s_T, 1)

            def fused(l):
                if l < L - 1:
                    act.wait_ge(s_fuse, n_e)
                if l == 0:
                    s.activation(hc[:], mix[2], ACT.Identity, bias=bfuse[:]).then_inc(s_hc, 1)
                elif l < L - 1:
                    s.activation(hT[0][:], mix[2], ACT.Relu, bias=bfuse[:]).then_inc(s_hT[0], 1)

            def gate_and_table(l, t):
                if l == 0:
                    act.wait_ge(s_gate_ps, n_e0)
                    s.activation(th[:], mix[3], ACT.Tanh, bias=gate_bias[:], scale=0.5).then_inc(s_th, 1)
                    act.reg_add(n_e0, n_e0, 1)
                if l < L - 1:
                    act.wait_ge(s_stored, n_stored)
                    act.reg_add(n_stored, n_stored, 16)
                    evacuate_table(0, meta[:, bass.ds(t, 1), M_ER:M_X])
                act.reg_add(n_e, n_e, 1)

            n_e0 = counter(act, "act_epi0", 1)
            n_stored = counter(act, "act_stored", 16)

            def tile(l, t, previous):
                pairs, *has = load_plan(act, t, range(5))
                for b in ("A", "B"):
                    group(8)
                    if previous is not None and b == "A":
                        transposed(l)
                        fused(l)
                    if previous is not None and b == "B":
                        gate_and_table(l, previous)
                with act.If(pairs > 1):
                    with act.Fori(1, pairs):
                        group(8)
                        group(8)
                for h, K in zip(has, TAILS):
                    with act.If(h > 0):
                        group(K)

            act.wait_ge(s_bload, 16 * (5 + 3 * L))
            act.wait_ge(s_plan, 16)
            act.wait_ge(s_gbias, 1)
            act.wait_ge(s_saved[0], 16 * ((T + 1) // 2))
            for l in range(L):
                tile(l, 0, None)
                with act.Fori(1, T) as t:
                    tile(l, t, t - 1)
                transposed(l)
                fused(l)
                gate_and_table(l, T - 1)

        @block.tensor
        def _(pe):
            n_tab = counter(pe, "pe_tab", 1)

            def table_products(l, k, hT_count):
                pe.wait_ge(s_hT[k], hT_count)
                pe.wait_ge(s_rows, n_tab)
                pe.matmul(ps_z[:, 0:ZW], hT[k][:], wz[:, l], start=True, stop=True).then_inc(s_z_ps, 1)
                for c in range(4):
                    pe.wait_ge(s_bank[c], n_tab)
                    pe.matmul(ps_tab[c % 2][:], hT[k][:], wrel[:, l, c * RC * D:(c + 1) * RC * D],
                              start=True, stop=True).then_inc(s_chunk[c], 1)
                pe.reg_add(n_tab, n_tab, 1)

            pe.wait_ge(s_const, 12)
            pe.wait_ge(s_wload, 16 * 5)
            pe.wait_ge(s_wz, 1)
            n_xin = [counter(pe, f"pe_xin{k}", 16) for k in range(2)]
            n_hT = [counter(pe, f"pe_hT{k}", 1) for k in range(2)]

            def natural_tile(k):
                pe.wait_ge(s_xin[k], n_xin[k])
                pe.reg_add(n_xin[k], n_xin[k], 16)
                pe.transpose(mix[0], xin[k][:], ident[:]).then_inc(s_xT_ps, 1)
                pe.wait_ge(s_hT[k], n_hT[k])
                pe.sem_inc(s_xin_used[k], 1)
                table_products(0, k, n_hT[k])
                pe.reg_add(n_hT[k], n_hT[k], 1)

            for j in range(3):
                pe.sem_inc(s_oh_used[j], 1)
            pe.matmul(ps_cnt[:, 0:T], zeros_bf[0:EP, :], zeros_bf[0:EP, 0:T], start=True, stop=False,
                      skip_group_check=True)
            n_oh = counter(pe, "pe_oh", 1)

            def count_batch(j):
                pe.wait_ge(s_oh[j], n_oh)
                for c in range(HB):
                    mm = pe.matmul(ps_cnt[:, 0:T], oh_lo[j][0:EP, c, :], oh_hi[j][0:EP, c, :], start=False,
                                   stop=False, skip_group_check=True)
                mm.then_inc(s_oh_used[j], 1)

            with pe.Fori(0, EC // (3 * HB)):
                count_batch(0)
                natural_tile(0)
                count_batch(1)
                natural_tile(1)
                count_batch(2)
                pe.reg_add(n_oh, n_oh, 1)
            pe.matmul(ps_cnt[:, 0:T], zeros_bf[0:EP, :], zeros_bf[0:EP, 0:T], start=False, stop=True,
                      skip_group_check=True).then_inc(s_hist, 1)
            pe.wait_ge(s_deg, 1)
            pe.matmul(ps_cnt[:, 128:128 + T], upper[:], degree[:], start=True, stop=False)
            pe.matmul(ps_cnt[:, 128:128 + T], ones[:], before[:], start=False, stop=True)
            pe.wait_ge(s_uns_in, 1)
            pe.matmul(ps_cnt[:, 256:257], ones[0:EP, :], unsorted_f[0:EP, :], start=True, stop=True)
            pe.wait_ge(s_tws, 1)
            pe.matmul(ps_cnt[:, 260:261], ones[0:EP, :], wsum[0:EP, 0:1], start=True, stop=True
                      ).then_inc(s_start_ps, 1)
            for i in range(2 * (EC // (3 * HB)), T):
                natural_tile(i % 2)
            pe.wait_ge(s_meta_cols, 3)
            pe.transpose(mix[3][0:T, :], cnt_r[:], ident[:]).then_inc(s_deg_ps, 1)

            pe.wait_ge(s_bload, 16 * (5 + 3 * L))
            pe.wait_ge(s_plan, 16)
            n_land = {b: counter(pe, f"pe_land_{b}", 16 * GK[b]) for b in GA}
            n_g = counter(pe, "pe_group", 1)
            n_e = counter(pe, "pe_epi", 1)
            n_e0 = counter(pe, "pe_epi0", 1)
            for b in GA:
                pe.sem_inc(s_free[b], 1)

            def group(b, first=False, mid=None):
                K = GK[b]
                pe.wait_ge(s_landed[b], n_land[b])
                pe.reg_add(n_land[b], n_land[b], 16 * K)
                if first:
                    pe.wait_ge(s_h2, n_h)
                for k in range(K):
                    mm = pe.matmul(ps_rel[:, 0:D], ident[:], slots[b][:, k, 0:D], start=first and k == 0,
                                   stop=True, skip_group_check=True)
                if mid:
                    mid()
                pe.wait_ge(s_zx, n_g)
                zs = zx[:].rearrange("p k h e -> p k (h e)")
                W = H * EX
                if K == 1:
                    pe.matmul(ps_gat[:, 0:W // 2], ident[:], zs[:, 7, 0:W // 2], start=True, stop=True,
                              skip_group_check=True).then_inc(s_free[b], 1)
                    pe.matmul(ps_gat[:, W // 2:W], ident[:], zs[:, 7, W // 2:W], start=True, stop=True,
                              skip_group_check=True).then_inc(s_gat, 1)
                else:
                    for k in range(K):
                        mm = pe.matmul(ps_gat[:, 0:W], ident[:], zs[:, 8 - K + k, :], start=(k == 0),
                                       stop=(k == K - 1))
                        if k == 0:
                            mm.then_inc(s_free[b], 1)
                    mm.then_inc(s_gat, 1)
                pe.reg_add(n_g, n_g, 1)

            def transpose_sums(l):
                pe.wait_ge(s_h2, n_h)
                pe.transpose(mix[0], hr[:], ident[:])
                pe.transpose(mix[1], hg[:].rearrange("p h c -> p (h c)"), ident[:]).then_inc(s_T_ps, 1)

            def fuse(l):
                pe.wait_ge(s_T, n_e)
                if l < L - 1:
                    pe.matmul(mix[2], wfuse[:, 0], hrT[:], start=True, stop=False)
                    pe.matmul(mix[2], wfuse[:, 1], hgT[:], start=False, stop=True).then_inc(s_fuse, 1)
                else:
                    pe.matmul(mix[2], ones[0:1, :], bfuse_row[:], start=True, stop=False)
                    pe.matmul(mix[2], hrT[:], wfuse[:, 0], start=False, stop=False)
                    pe.matmul(mix[2], hgT[:], wfuse[:, 1], start=False, stop=True).then_inc(s_fuse, 1)

            def gate(l):
                if l == 0:
                    pe.wait_ge(s_hc, n_e0)
                    pe.matmul(mix[3], wgate[:], hc[:], start=True, stop=True).then_inc(s_gate_ps, 1)

            def table_of(l):
                if l < L - 1:
                    table_products(l + 1, 0, n_hT[0])
                    pe.reg_add(n_hT[0], n_hT[0], 1)
                if l == 0:
                    pe.reg_add(n_e0, n_e0, 1)
                pe.reg_add(n_e, n_e, 1)

            n_h = counter(pe, "pe_h2", 1)

            def tile(l, t, previous):
                pairs, *has = load_plan(pe, t, range(5))
                if previous:
                    group("A", first=True, mid=lambda: transpose_sums(l))
                    fuse(l)
                    group("B", mid=lambda: gate(l))
                    table_of(l)
                else:
                    group("A", first=True)
                    group("B")
                with pe.If(pairs > 1):
                    with pe.Fori(1, pairs):
                        group("A")
                        group("B")
                for h, b in zip(has, ("A", "t4", "t2", "t1")):
                    with pe.If(h > 0):
                        group(b)
                pe.reg_add(n_h, n_h, 1)

            for l in range(L):
                tile(l, 0, False)
                with pe.Fori(1, T) as t:
                    tile(l, t, True)
                transpose_sums(l)
                fuse(l)
                gate(l)
                table_of(l)

        @block.vector
        def _(dve):
            v = nc.vector
            done = 0

            def step(ins):
                nonlocal done
                done += 1
                ins.then_inc(s_v, 1)
                dve.wait_ge(s_v, done)

            dve.wait_ge(s_eload, 16 * 6)
            v.tensor_scalar(lo_i[:], dst_i[:], P - 1, None, ALU.bitwise_and)
            step(v.tensor_scalar(hi_i[:], dst_i[:], P.bit_length() - 1, None, ALU.logical_shift_right))
            v.tensor_copy(lo_bf[:], lo_i[:])
            step(v.tensor_copy(hi_bf[:], hi_i[:]))
            v.scalar_tensor_tensor(src_i[:], src_i[:], float(R), typ_i[:], ALU.mult, ALU.add).then_inc(s_edge_rows, 1)

            dve.wait_ge(s_const, 12)
            n = counter(dve, "v_oh", 1)

            def onehots(batch, j):
                dve.wait_ge(s_oh_used[j], n)
                at = batch * HB
                v.tensor_tensor(oh_hi[j][0:EP], bc_last(hi_bf[:, bass.ds(at, HB)], T),
                                bc(iota_row[0:EP, 0:T], HB), ALU.is_equal)
                v.tensor_tensor(oh_lo[j][0:EP], bc_last(lo_bf[:, bass.ds(at, HB)], P),
                                bc(iota_row[0:EP, :], HB), ALU.is_equal).then_inc(s_oh[j], 1)

            def fold(l):
                nonlocal folded
                for i in range(2):
                    folded += 1
                    v.tensor_tensor(attn_tmp[:], wz[:, l, 0:D], attn[:, i, l], ALU.mult).then_inc(s_fold, 1)
                    dve.wait_ge(s_fold, folded)
                    r = v.tensor_reduce(wz[:, l, D + i * H:D + (i + 1) * H],
                                        attn_tmp[:].rearrange("p (h c) -> p h c", h=H), AX.X, ALU.add)
                    if i == 0:
                        folded += 1
                        r.then_inc(s_fold, 1)
                        dve.wait_ge(s_fold, folded)
                    else:
                        r.then_inc(s_wz, 1)
                        dve.wait_ge(s_wz, l + 1)

            folded = 0
            dve.wait_ge(s_wload, 16 * 5)
            fold(0)
            with dve.Fori(0, EC // (3 * HB)) as i:
                for j in range(3):
                    onehots(i * 3 + j, j)
                dve.reg_add(n, n, 1)
            for l in range(1, L):
                fold(l)

            dve.wait_ge(s_edge_rows, 1)
            v.scalar_tensor_tensor(typ_i[:], lo_i[:], float(T), hi_i[:], ALU.mult, ALU.add).then_inc(s_edge_rows, 1)
            step(v.tensor_tensor(dst_next[:], dst_i[:], dst_next[:], ALU.is_gt))
            v.tensor_reduce(unsorted_f[0:EP, :], dst_next[:], AX.X, ALU.add).then_inc(s_uns_in, 1)
            dve.wait_ge(s_ewload, 16)
            v.tensor_reduce(wsum[0:EP, 0:1], ew[:], AX.X, ALU.add).then_inc(s_tws, 1)

            dve.wait_ge(s_hist, 1)
            step(v.tensor_copy(degree[:], ps_cnt[:, 0:T]))
            v.memset(before[:, 0:1], 0.0)
            v.tensor_tensor_scan(before[:, 1:T], ones[:, 0:T - 1], degree[:, 0:T - 1], 0.0, ALU.mult, ALU.add
                                 ).then_inc(s_deg, 1)
            step(v.tensor_scalar(key[:], degree[:], float(KEYMAX), float(KEYMAX + 1), ALU.min, ALU.mult))
            step(v.tensor_tensor(key[:], key[:], meta_nat[:, :, M_ID], ALU.subtract))
            step(v.tensor_scalar(key[:], key[:], float(KEYMAX), None, ALU.add))
            v.tensor_copy(meta_nat[:, :, M_CNT], degree[:])
            step(v.tensor_scalar(negkey[:], key[:], -1.0, None, ALU.mult))
            dve.wait_ge(s_start_ps, 1)
            step(v.tensor_copy(starts[:], ps_cnt[:, 128:128 + T]))
            v.tensor_copy(meta_nat[:, :, M_START], starts[:]).then_inc(s_key, 1)

            v.tensor_scalar(unsorted_i[:], ps_cnt[0:1, 256:257], 1.0, None, ALU.min).then_inc(s_uns, 1)
            step(v.tensor_scalar(tw_mean[:], ps_cnt[:, 260:261], 1.0 / E, None, ALU.mult))
            dve.wait_ge(s_bload, 16 * (5 + 3 * L))
            step(v.tensor_scalar(gate_bias[:], bgate[:, 1:2], tw_mean[:], bgate[:, 0:1], ALU.mult, ALU.add))
            v.tensor_scalar(gate_bias[:], gate_bias[:], 0.5, None, ALU.mult).then_inc(s_gbias, 1)

            dve.wait_ge(s_key_bc, 16)
            for t in range(RANKED_BY_VECTOR):
                step(v.tensor_scalar(waste[0], key_bc[:], key[:, t:t + 1], None, ALU.is_gt, ALU.add,
                                     accum_out=rank[:, t:t + 1]))
            dve.wait_ge(s_rank_act, T - RANKED_BY_VECTOR)
            step(v.tensor_scalar(rank[:, RANKED_BY_VECTOR:T], rank[:, RANKED_BY_VECTOR:T], float(NP_ - 1), 0.5,
                                 ALU.add, ALU.mult))
            v.tensor_copy(rank_u[:], rank[:]).then_inc(s_rank, 1)

            dve.wait_ge(s_uns, 1)
            bad = dve.value_load(unsorted_i[0:1, 0:1], min_val=0, max_val=1)
            with dve.If(bad > 0):
                n_ld = counter(dve, "v_sort_ld", 48)
                n_cur = counter(dve, "v_sort_cur", 16)
                n_c = counter(dve, "v_sort_c", 1)

                def sort_step(ins):
                    ins.then_inc(s_sort_c, 1)
                    dve.wait_ge(s_sort_c, n_c)
                    dve.reg_add(n_c, n_c, 1)

                with dve.Fori(0, EC):
                    dve.wait_ge(s_sort_ld, n_ld)
                    dve.wait_ge(s_sort_cur, n_cur)
                    dve.reg_add(n_ld, n_ld, 48)
                    dve.reg_add(n_cur, n_cur, 16)
                    sort_step(v.tensor_copy(sort_f[:, 0:1], sort_key[:]))
                    sort_step(v.tensor_scalar(sort_eq[:, 0], sort_keys[:], sort_f[:, 0:1], None, ALU.is_equal))
                    sort_step(v.tensor_tensor(sort_eq[:, 1], sort_eq[:, 0], upper[0:EP, 0:EP], ALU.mult))
                    v.tensor_reduce(sort_f[:, 2:3], sort_eq[:, 1], AX.X, ALU.add)
                    sort_step(v.tensor_reduce(sort_f[:, 1:2], sort_eq[:, 0], AX.X, ALU.add))
                    sort_step(v.tensor_tensor(sort_f[:, 1:2], sort_f[:, 1:2], sort_f[:, 2:3], ALU.subtract))
                    sort_step(v.tensor_tensor(sort_new[:], sort_f[:, 1:2], sort_cur[:], ALU.add))
                    v.tensor_scalar(sort_pos[:], sort_new[:], -1.0, None, ALU.add)
                    sort_step(v.tensor_scalar(sort_f[:, 3:4], sort_f[:, 2:3], 0.0, float(NP_), ALU.is_gt, ALU.mult))
                    v.tensor_tensor(sort_cell[:], sort_f[:, 3:4], sort_f[:, 0:1], ALU.add).then_inc(s_sort_v, 1)

            dve.wait_ge(s_meta, 16)
            v.tensor_copy(start_u[:], meta[:, :, M_START]).then_inc(s_meta_cols, 1)
            v.tensor_copy(id_u[:], meta[:, :, M_ID]).then_inc(s_meta_cols, 1)
            v.tensor_copy(cnt_r[:], meta[:, :, M_CNT]).then_inc(s_meta_cols, 1)
            dve.wait_ge(s_deg_ps, 1)
            step(v.tensor_reduce(plan_f[:], mix[3][0:T, :], AX.X, ALU.max))
            for c in range(8):
                ins = v.tensor_scalar(plan_c[:, c:c + 1], plan_f[:], float(PAIR), None, ALU.max)
            step(ins)
            step(v.tensor_scalar(plan_c[:, 5:6], plan_f[:], float(PAIR), float(BLOCK - PAIR), ALU.max, ALU.add))
            v.tensor_scalar(plan_i[:, 0:1], plan_c[:, 0:1], 4, None, ALU.logical_shift_right)
            for c in range(1, 5):
                v.tensor_scalar(plan_i[:, c:c + 1], plan_c[:, c:c + 1], 4 - c, 1, ALU.logical_shift_right,
                                ALU.bitwise_and)
            v.tensor_scalar(plan_i[:, 6:8], plan_c[:, 6:8], 0, None, ALU.bitwise_and)
            v.tensor_scalar(plan_i[:, 5:6], plan_c[:, 5:6], 6, None, ALU.logical_shift_right).then_inc(s_plan_i, 1)
            dve.wait_ge(s_meta_cols, 3)
            step(v.tensor_tensor(ell_valid, bc(iota_slot[:], T), bc_last(cnt_r[:], ELL), ALU.is_lt))
            dve.wait_ge(s_ell, 16 * T)
            step(v.scalar_tensor_tensor(ell_valid, ell[:, 0:T], -float(NULL), ell_valid, ALU.add, ALU.mult))
            v.tensor_scalar(ell[:, 0:T], ell_valid, float(NULL), None, ALU.add).then_inc(s_ell_ok, 1)

            v.memset(acc[:], 0.0).then_inc(s_acc, 1)
            dve.wait_ge(s_plan, 16)
            dve.sem_inc(s_h2, 1)
            n_land = {b: counter(dve, f"v_land_{b}", 16 * GK[b]) for b in GA}
            n_g = counter(dve, "v_group", 1)
            n_t = counter(dve, "v_tile", 1)
            n_norm = counter(dve, "v_norm", 1)
            n_e = counter(dve, "v_epi", 1)
            n_out = counter(dve, "v_out", 16)

            def group(b):
                K = GK[b]
                lo = 8 - K
                dve.wait_ge(s_landed[b], n_land[b])
                dve.reg_add(n_land[b], n_land[b], 16 * K)
                dve.wait_ge(s_acc, n_g)
                v.tensor_tensor(raw[:, lo:8], slots[b][:, :, 2 * D:ROW], er_cur[:].to_broadcast([P, K, H]), ALU.add
                                ).then_inc(s_raw, 1)
                dve.wait_ge(s_raw, n_g)
                v.tensor_reduce(top[:, 0], raw[:, lo:9].rearrange("p k h -> p h k"), AX.X, ALU.max
                                ).then_inc(s_top, 1)
                v.scalar_tensor_tensor(leaky[:, lo:9], raw[:, lo:9], SLOPE, raw[:, lo:9], ALU.mult, ALU.max
                                       ).then_inc(s_leaky, 1)
                dve.wait_ge(s_top, n_g)
                v.scalar_tensor_tensor(peak[:], top[:], SLOPE, top[:], ALU.mult, ALU.max).then_inc(s_peak, 1)
                dve.wait_ge(s_leaky, n_g)
                v.tensor_copy(raw[:, 8:9], top[:]).then_inc(s_keep, 1)
                dve.wait_ge(s_peak, n_g)
                v.tensor_tensor(logit[:, lo:9], leaky[:, lo:9], peak[:].to_broadcast([P, K + 1, H]), ALU.subtract
                                ).then_inc(s_logit, 1)
                dve.wait_ge(s_keep, n_g)
                dve.wait_ge(s_wgt, n_g)
                v.tensor_tensor(zx[:, lo:8, :, 0:DH], slots[b][:, :, D:2 * D].rearrange("p k (h c) -> p k h c", h=H),
                                zx[:, lo:8, :, DH:EX].to_broadcast([P, K, H, DH]), ALU.mult).then_inc(s_zx, 1)
                v.tensor_tensor(acc[:], acc[:], zx[:, 8, :, DH:EX].to_broadcast([P, H, EX]), ALU.mult
                                ).then_inc(s_scaled, 1)
                dve.wait_ge(s_scaled, n_g)
                dve.wait_ge(s_gat, n_g)
                v.tensor_tensor(acc[:], acc[:], ps_gat[:, 0:H * EX].rearrange("p (h e) -> p h e", h=H), ALU.add
                                ).then_inc(s_acc, 1)
                dve.reg_add(n_g, n_g, 1)

            def start_tile(t):
                v.tensor_copy(er_cur[:], meta[:, bass.ds(t, 1), M_ER:M_LOOP])
                v.memset(raw[:, 8:9], NEG).then_inc(s_tile, 1)
                dve.wait_ge(s_tile, n_t)
                dve.reg_add(n_t, n_t, 1)

            def end_tile(t):
                dve.wait_ge(s_acc, n_g)
                v.reciprocal(rden[:], acc[:, :, DH:EX]).then_inc(s_rden, 1)
                v.tensor_tensor(hr[:], ps_rel[:, 0:D], meta[:, bass.ds(t, 1), M_LOOP:M_X].rearrange("p o f -> p (o f)"),
                                ALU.add)
                dve.wait_ge(s_rden, n_rd)
                dve.reg_add(n_rd, n_rd, 1)
                v.tensor_tensor(hg[:], acc[:, :, 0:DH], rden[:].to_broadcast([P, H, DH]), ALU.mult
                                ).then_inc(s_h2, 1)

            n_rd = counter(dve, "v_rden", 1)

            def norm_step(ins):
                ins.then_inc(s_norm, 1)
                dve.wait_ge(s_norm, n_norm)
                dve.reg_add(n_norm, n_norm, 1)

            def epilogue(l, t):
                if l == 0:
                    dve.wait_ge(s_th, n_e)
                    v.scalar_tensor_tensor(th[:], th[:], 1.0, hc[:], ALU.add, ALU.mult).then_inc(s_gated, 1)
                    dve.wait_ge(s_gated, n_e)
                    v.tensor_scalar(hT[0][:], th[:], 0.5, 0.0, ALU.mult, ALU.max).then_inc(s_hT[0], 1)
                    dve.reg_add(n_e, n_e, 1)
                elif l == L - 1:
                    dve.wait_ge(s_fuse, n_f)
                    norm_step(v.scalar_tensor_tensor(y[:], mix[2], 0.0, meta[:, bass.ds(t, 1), M_X:META]
                                                     .rearrange("p o f -> p (o f)"), ALU.max, ALU.add))
                    norm_step(v.bn_stats(stats[:], y[:]))
                    norm_step(v.bn_aggr(mv[:], stats[:]))
                    norm_step(v.tensor_scalar(ve[:], mv[:, 1:2], EPS, None, ALU.add))
                    norm_step(v.tensor_scalar(nv_i[:], ve[:].bitcast(I32), 1, None, ALU.logical_shift_right))
                    norm_step(v.tensor_scalar(nv[:, 0:1].bitcast(I32), nv_i[:], -1.0, float(0x5f3759df),
                                              ALU.mult, ALU.add))
                    for _ in range(4):
                        norm_step(v.tensor_scalar(nv[:, 1:2], nv[:, 0:1], nv[:, 0:1], ve[:], ALU.mult, ALU.mult))
                        norm_step(v.tensor_scalar(nv[:, 1:2], nv[:, 1:2], -0.5, 1.5, ALU.mult, ALU.add))
                        norm_step(v.tensor_tensor(nv[:, 0:1], nv[:, 0:1], nv[:, 1:2], ALU.mult))
                    dve.wait_ge(s_out, n_out)
                    dve.reg_add(n_out, n_out, 16)
                    v.tensor_scalar(yo[:], y[:], mv[:, 0:1], nv[:, 0:1], ALU.subtract, ALU.mult).then_inc(s_yo, 1)
                    dve.reg_add(n_f, n_f, 1)

            n_f = counter(dve, "v_fuse", (L - 1) * T + 1)

            def tile(l, t, previous):
                pairs, *has = load_plan(dve, t, range(5))
                start_tile(t)
                group("A")
                group("B")
                if previous is not None:
                    epilogue(l, previous)
                with dve.If(pairs > 1):
                    with dve.Fori(1, pairs):
                        group("A")
                        group("B")
                for h, b in zip(has, ("A", "t4", "t2", "t1")):
                    with dve.If(h > 0):
                        group(b)
                end_tile(t)

            for l in range(L):
                dve.wait_ge(s_rows, T + 1 + l * T)
                tile(l, 0, None)
                with dve.Fori(1, T) as t:
                    tile(l, t, t - 1)
                epilogue(l, T - 1)


_INS = ['x', 'src', 'dst', 'edge_type_16', 'edge_weight', 'L0_gnn_W_rel', 'L0_gnn_b_rel', 'L0_gnn_W_loop',
        'L0_gnn_W_gat', 'L0_gnn_attn_l', 'L0_gnn_attn_r', 'L0_gnn_b_gat', 'L0_gnn_W_fuse', 'L0_gnn_b_fuse',
        'L0_gnn_W_gate', 'L0_gnn_b_gate']


def kernel(**inputs):
    import numpy as _np
    import concourse.bacc as _bacc
    from concourse.bass_utils import run_bass_kernel_spmd as _run

    nc = _bacc.Bacc("TRN2", target_bir_lowering=False, num_devices=1)
    arrays, args = {}, []
    for name in _INS:
        a = _np.ascontiguousarray(inputs[name])
        arrays[f"in_{name}"] = a
        args.append(nc.dram_tensor(f"in_{name}", a.shape, mybir.dt.from_np(a.dtype), kind="ExternalInput").ap())
    out = nc.dram_tensor("out", inputs["x"].shape, F32, kind="ExternalOutput").ap()
    gnn_kernel(nc, *args, out)
    r = _run(nc, [arrays], core_ids=[0])
    return r.results[0]["out"]
```

```python
from contextlib import ExitStack

import concourse.bass as bass
from concourse import mybir

ALU = mybir.AluOpType
ACT = mybir.ActivationFunctionType
AX = mybir.AxisListType
F32 = mybir.dt.float32
BF16 = mybir.dt.bfloat16
I32 = mybir.dt.int32
U32 = mybir.dt.uint32

P = 128
PAIR = 16
BLOCK = 64
ELL = BLOCK + PAIR
NEG = -1.0e30
LEAST = -1.0e37
SLOPE = 0.2
EPS = 1e-5


def gnn_kernel(nc, x, src, dst, etype, eweight, W_rel, b_rel, W_loop, W_gat, attn_l, attn_r, b_gat,
               W_fuse, b_fuse, W_gate, b_gate, out):
    N, D = x.shape
    E = src.shape[0]
    L, R = W_rel.shape[0], W_rel.shape[1]
    H, DH = attn_l.shape[1], attn_l.shape[2]
    assert D == P and H * DH == D
    T = -(-N // P)
    NP_ = T * P
    EP = 125
    EC = E // EP
    assert EP * EC == E
    ROW = 2 * D + H
    NULL = NP_ * R
    EX = DH + 1
    M_START, M_CNT, M_ID, M_ER = 0, 1, 2, 4
    M_LOOP = M_ER + H
    M_X = M_LOOP + D
    META = M_X + D
    ZW = D + H + H + D
    HB = 25
    assert EC % (3 * HB) == 0 and T % 2 == 1
    RC = R // 4
    assert RC * D == 512
    TAILS = (8, 4, 2, 1)
    LOWER_BY = 16 * BLOCK // 2
    LO = 64
    HI = NP_ // LO
    CLS = P
    CONSTS = 14
    ROUNDS = EC // (3 * HB)
    ER_AHEAD = T - 2 * ROUNDS
    assert ER_AHEAD == 3 and ROUNDS % 2 == 1 and T > ROUNDS + 8
    assert HI == 2 * T and T <= HB

    with ExitStack() as ctx:
        def sb(name, shape, dt=F32):
            return ctx.enter_context(nc.sbuf_tensor(name, shape, dt))

        def ps(name, shape):
            return ctx.enter_context(nc.psum_tensor(name, shape, F32))

        def sem(name):
            return ctx.enter_context(nc.semaphore(name))

        def dram(name, shape, dt=F32):
            return nc.dram_tensor(name, shape, dt).ap()

        table = [dram(f"table{i}", [NP_ * R + 1, ROW]) for i in range(2)]
        edge_rows = dram("edge_rows", [E + ELL, 1], I32)
        edge_rows_raw = dram("edge_rows_raw", [E, 1], I32)
        edge_cells = dram("edge_cells", [E, 1], I32)
        cursors = dram("cursors", [NP_, 1])
        meta_ranked = dram("meta_ranked", [NP_, META])
        tile_slots_dram = dram("tile_slots_dram", [T, 1], I32)

        ident = sb("ident", [P, P])
        ones = sb("ones", [P, P])
        upper = sb("upper", [P, P])
        lower = sb("lower", [P, P])
        shift = sb("shift", [LO, P])
        upper_bf = sb("upper_bf", [P, P], BF16)
        values = sb("values", [P, CLS, HB], BF16)
        iota_row = sb("iota_row", [P, P], BF16)
        iota_slot = sb("iota_slot", [P, ELL])
        null_row = sb("null_row", [P, ROW])
        zeros_bf = sb("zeros_bf", [P, P], BF16)
        tail_idx = sb("tail_idx", [P, ELL], I32)

        wrel = sb("wrel", [P, L, R * D])
        wz = sb("wz", [P, L, ZW])
        attn = sb("attn", [P, 2, L, D])
        attn_tmp = sb("attn_tmp", [P, D])
        wfuse = sb("wfuse", [P, 2, D])
        wgate = sb("wgate", [P, D])
        brel = sb("brel", [P, L])
        bgat = sb("bgat", [P, L])
        bfuse = sb("bfuse", [P, 1])
        bfuse_row = sb("bfuse_row", [1, D])
        bgate = sb("bgate", [P, 2])
        gate_bias = sb("gate_bias", [P, 1])
        wsum = sb("wsum", [P, 2])
        tw_mean = sb("tw_mean", [P, 1])

        meta_nat = sb("meta_nat", [P, T, META])
        meta = sb("meta", [P, T, META])
        xin = [sb(f"xin{i}", [P, D]) for i in range(4)]
        hT = [sb(f"hT{i}", [P, P]) for i in range(4)]
        rows = [sb(f"rows{i}", [P, R, ROW]) for i in range(2)]
        degree = sb("degree", [P, T])
        before = sb("before", [P, T])
        counts = sb("counts", [LO, HI])
        cls = sb("cls", [P, T], BF16)
        cls_count = sb("cls_count", [P, T])
        cls_cum = sb("cls_cum", [P, T])
        cls_above = sb("cls_above", [P, 1])
        cls_base = sb("cls_base", [P, T])
        starts = sb("starts", [P, T])
        rank = sb("rank", [P, T])
        rank_u = sb("rank_u", [P, T], U32)
        start_u = sb("start_u", [P, T], U32)
        cnt_r = sb("cnt_r", [P, T])
        id_u = sb("id_u", [P, T], U32)
        ell = sb("ell", [P, T + 1, ELL], I32)
        tile_slots_f = sb("tile_slots_f", [T, 1])
        tile_slots_col = sb("tile_slots_col", [T, 1], I32)
        tile_slots = sb("tile_slots", [1, T], I32)

        dst_i = sb("dst_i", [EP, EC], I32)
        dst_next = sb("dst_next", [EP, EC], I32)
        src_i = sb("src_i", [EP, EC], I32)
        typ_i = sb("typ_i", [EP, EC], I32)
        lo_bf = sb("lo_bf", [EP, EC], BF16)
        hi_bf = sb("hi_bf", [EP, EC], BF16)
        lo_i = sb("lo_i", [EP, EC], I32)
        hi_i = sb("hi_i", [EP, EC], I32)
        ew = sb("ew", [EP, EC])
        W = (LO + HI) * HB // 2
        assert (LO + HI) * HB % 2 == 0 and CLS * T % 2 == 0
        scratch = sb("scratch", [P, 3 * W])
        oh = [scratch[:, j * W:(j + 1) * W].bitcast(BF16).rearrange("p (v c) -> p v c", c=HB) for j in range(3)]
        oh_cls = scratch[:, 0:CLS * T // 2].bitcast(BF16).rearrange("p (v t) -> p v t", t=T)
        diag, picked = ([scratch[:, CLS * T // 2 + (2 * i + j) * 512:][:, 0:512].rearrange("p (t v) -> p t v", t=4)
                         for j in range(2)] for i in range(2))
        assert CLS * T // 2 + 4 * 512 <= 3 * W
        ell_valid = scratch[:, 0:T * ELL].rearrange("p (t j) -> p t j", t=T)
        sort_key = sb("sort_key", [EP, 1], U32)
        sort_val = sb("sort_val", [EP, 1], I32)
        sort_keys = sb("sort_keys", [EP, EP], U32)
        sort_cur = sb("sort_cur", [EP, 1])
        sort_pos = sb("sort_pos", [EP, 1], U32)
        sort_new = sb("sort_new", [EP, 1])
        sort_cell = sb("sort_cell", [EP, 1], U32)
        sort_f = sb("sort_f", [EP, 4])
        sort_eq = sb("sort_eq", [EP, 2, EP])
        unsorted_f = sb("unsorted_f", [P, 1])
        unsorted_i = sb("unsorted_i", [1, 1], I32)

        GA = ("A", "B", "t4", "t2", "t1")
        GK = dict(A=8, B=8, t4=4, t2=2, t1=1)
        assert sum(GK.values()) * ROW <= T * META
        room = meta_nat[:].rearrange("p t f -> p (t f)")
        slots, used = {}, 0
        for b in GA:
            slots[b] = room[:, used:used + GK[b] * ROW].rearrange("p (k f) -> p k f", k=GK[b])
            used += GK[b] * ROW
        stage = {b: sb(f"stage_{b}", [P, GK[b]], U32) for b in GA}
        stage_id = sb("stage_id", [P, 1], U32)
        tick = sb("tick", [1, 4])
        blk_start = sb("blk_start", [P, 1])
        blk_left = sb("blk_left", [P, 1])
        blk_start_u = sb("blk_start_u", [P, 1], U32)
        blk_f = sb("blk_f", [P, 2, ELL])
        er_cur = sb("er_cur", [P, 1, H])
        raw = sb("raw", [P, 9, H])
        leaky = sb("leaky", [P, 9, H])
        top = sb("top", [P, 1, H])
        peak = sb("peak", [P, 1, H])
        logit = sb("logit", [P, 9, H])
        zx = sb("zx", [P, 9, H, EX])
        acc = sb("acc", [P, H, EX])
        rden = sb("rden", [P, H, 1])
        hg = sb("hg", [P, H, DH])
        hr = sb("hr", [P, D])
        hrT = sb("hrT", [P, P])
        hgT = sb("hgT", [P, P])
        hc = sb("hc", [P, P])
        th = sb("th", [P, P])
        y = sb("y", [P, D])
        yo = sb("yo", [P, D])
        stats = sb("stats", [P, 6])
        mv = sb("mv", [P, 2])
        ve = sb("ve", [P, 1])
        nv = sb("newton", [P, 2])
        nv_i = sb("newton_i", [P, 1], I32)

        ps_rel = ps("ps_rel", [P, 512])
        ps_gat = ps("ps_gat", [P, 512])
        ps_mix = ps("ps_mix", [P, 512])
        ps_z = ps("ps_z", [P, 512])
        ps_tab = [ps(f"ps_tab{i}", [P, 512]) for i in range(2)]
        ps_cnt = ps("ps_cnt", [P, 512])
        ps_xT = [ps_rel[:, 0:P]] * 2 + [ps_mix[:, 0:P]] * 2
        mix = [ps_mix[:, 128 * i:128 * i + 128] for i in range(4)]

        s_const = sem("const_ready")
        s_wload = sem("weights_loaded")
        s_wrload = sem("first_relation_weights_loaded")
        s_bload = sem("biases_loaded")
        s_dload = sem("dst_loaded")
        s_eload = sem("edges_loaded")
        s_ewload = sem("edge_weights_loaded")
        s_xload = sem("x_loaded_to_meta")
        s_xin = [sem(f"xin{i}_loaded") for i in range(4)]
        s_xin_used = [sem(f"xin{i}_used") for i in range(4)]
        s_xT_ps = sem("xT_in_psum")
        s_hT = [sem(f"hT{i}_ready") for i in range(4)]
        s_er_ps = sem("er_product_ready")
        s_er = sem("er_and_loop_of_natural_tile_ready")
        s_z_ps = sem("z_product_ready")
        s_chunk = [sem(f"table_chunk{c}_ready") for c in range(4)]
        s_bank = [sem(f"bank_free_for_chunk{c}") for c in range(4)]
        s_rows = sem("rows_ready")
        s_half = sem("first_half_of_rows_ready")
        s_saved = [[sem(f"rows{i}_half{j}_saved") for j in range(2)] for i in range(2)]
        s_v = sem("vector_step")
        s_uns_in = sem("order_violations_ready")
        s_fold = sem("attention_fold_step")
        s_wz = sem("wz_ready")
        s_tws = sem("edge_weight_sums_ready")
        s_gbias = sem("gate_bias_ready")
        s_edge_rows = sem("edge_rows_computed")
        s_edge_saved = sem("edge_rows_saved")
        s_oh = [sem(f"onehots{i}_ready") for i in range(3)]
        s_oh_used = [sem(f"onehots{i}_used") for i in range(3)]
        s_hist = sem("histogram_ready")
        s_deg = sem("degrees_ready")
        s_start_ps = sem("starts_and_totals_ready")
        s_cnt = sem("histogram_copied")
        s_deg_nat = sem("degrees_by_node_in_psum")
        s_cls = sem("class_onehots_ready")
        s_cls_ps = sem("class_counts_in_psum")
        s_cls_cum = sem("class_counts_summed")
        s_above_ps = sem("higher_classes_in_psum")
        s_diag = sem("diagonals_ready")
        s_place_ps = sem("places_in_psum")
        s_picked = sem("own_class_picked")
        s_rank = sem("ranks_ready")
        s_scatter = sem("meta_scattered")
        s_meta_head = sem("ranked_starts_degrees_ids_loaded")
        s_deg_ps = sem("degrees_by_tile_in_psum")
        s_meta = sem("ranked_meta_loaded")
        s_meta_cols = sem("ranked_columns_ready")
        s_slots_col = sem("tile_slots_computed")
        s_slots_saved = sem("tile_slots_saved")
        s_slots = sem("tile_slots_loaded")
        s_ell = sem("ell_gathered")
        s_ell_ok = sem("ell_ready")
        s_stored = sem("rows_stored")
        s_uns = sem("order_flag_ready")
        s_cur = sem("cursors_saved")
        s_sort_ld = sem("sort_chunk_loaded")
        s_sort_cur = sem("sort_cursors_gathered")
        s_sort_v = sem("sort_positions_ready")
        s_sort_c = sem("sort_vector_step")
        s_sort_st = sem("sort_chunk_stored")
        s_copy = sem("raw_edge_rows_copied")
        s_staged = sem("slot_indices_staged")
        s_blk = sem("block_step")
        s_landed = {b: sem(f"slots_{b}_landed") for b in GA[:2]}
        s_blk_ld = sem("block_fetched")
        s_landed |= {b: sem(f"slots_{b}_landed") for b in GA[2:]}
        s_lowered = sem("landed_counts_lowered")
        s_free = {b: sem(f"slots_{b}_free") for b in GA}
        s_tile = sem("tile_started")
        s_raw = sem("raw_logits_ready")
        s_top = sem("running_top_ready")
        s_leaky = sem("leaky_ready")
        s_peak = sem("peak_ready")
        s_keep = sem("top_kept")
        s_logit = sem("logits_ready")
        s_wgt = sem("weights_ready")
        s_zx = sem("weighted_z_ready")
        s_scaled = sem("sums_rescaled")
        s_gat = sem("group_sum_ready")
        s_acc = sem("sums_updated")
        s_rden = sem("denominators_inverted")
        s_h2 = sem("node_sums_ready")
        s_T_ps = sem("node_sums_transposed")
        s_T = sem("transposed_sums_ready")
        s_fuse = sem("fused_in_psum")
        s_hc = sem("fused_ready")
        s_gate_ps = sem("gate_in_psum")
        s_th = sem("gate_ready")
        s_id = sem("ids_staged")
        s_norm = sem("norm_step")
        s_gated = sem("gating_step")
        s_yo = sem("normed_ready")
        s_out = sem("output_saved")

        def bc(ap, n):
            return ap.rearrange("p (o f) -> p o f", o=1).to_broadcast([ap.shape[0], n, ap.shape[1]])

        def bc_last(ap, n):
            return ap.rearrange("p (f o) -> p f o", o=1).to_broadcast([ap.shape[0], ap.shape[1], n])

        def counter(eng, name, value):
            reg = eng.alloc_register(name)
            eng.reg_mov(reg, value)
            return reg

        def pair_loops(eng, pairs, in_first, n_lowered, n_land, pair):
            with eng.If(in_first > 1):
                with eng.Fori(1, in_first):
                    pair()
            with eng.If(pairs > BLOCK // PAIR):
                left = counter(eng, f"left_{nc.next_id()}", 0)
                blocks = counter(eng, f"blocks_{nc.next_id()}", 0)
                now = counter(eng, f"now_{nc.next_id()}", 0)
                low = counter(eng, f"low_{nc.next_id()}", 0)
                eng.reg_sub(left, pairs, BLOCK // PAIR)
                eng.reg_sub(blocks, pairs, 1)
                eng.reg_alu(blocks, blocks, (BLOCK // PAIR).bit_length() - 1, ALU.logical_shift_right)
                with eng.Fori(0, eng.snap(blocks, min_val=1, max_val=E // BLOCK)):
                    eng.wait_ge(s_lowered, n_lowered)
                    eng.reg_add(n_lowered, n_lowered, 1)
                    for b in ("A", "B"):
                        eng.reg_sub(low, n_land[b], LOWER_BY)
                        eng.reg_alu(n_land[b], low, 16 * GK[b], ALU.max)
                    eng.reg_alu(now, left, BLOCK // PAIR, ALU.min)
                    eng.reg_sub(left, left, now)
                    with eng.Fori(0, eng.snap(now, min_val=1, max_val=BLOCK // PAIR)):
                        pair()

        def load_slots(eng, t):
            n = eng.value_load(tile_slots[0:1, bass.ds(t, 1)], min_val=PAIR, max_val=E)
            pairs = counter(eng, f"pairs_{nc.next_id()}", 0)
            in_first = counter(eng, f"in_first_{nc.next_id()}", 0)
            eng.reg_alu(pairs, n, PAIR.bit_length() - 1, ALU.logical_shift_right)
            eng.reg_alu(in_first, pairs, BLOCK // PAIR, ALU.min)
            return n, eng.snap(pairs, min_val=1, max_val=E // PAIR), eng.snap(in_first, min_val=1, max_val=BLOCK // PAIR)

        def tail_groups(eng, n, run):
            has = counter(eng, f"has_{nc.next_id()}", 0)
            for b, K in zip(("A", "t4", "t2", "t1"), TAILS):
                eng.reg_alu(has, n, K, ALU.bitwise_and)
                with eng.If(eng.snap(has, min_val=0, max_val=K) > 0):
                    run(b, K)

        block = ctx.enter_context(nc.Block())

        @block.sync
        def _(sp):
            sp.dma_start(dst_i[:], dst.rearrange("(p c) -> p c", p=EP)).then_inc(s_dload, 16)
            for k, i in enumerate((0, 1, 0, 1)):
                sp.dma_start(xin[k][:], x[i * P:(i + 1) * P, :]).then_inc(s_xin[k], 16)
            sp.dma_start(wz[:, :, 0:D], W_gat.rearrange("l d o -> d l o")).then_inc(s_wload, 16)
            sp.dma_start(wz[:, :, D + 2 * H:ZW], W_loop.rearrange("l d o -> d l o")).then_inc(s_wload, 16)
            for i, a in enumerate((attn_l, attn_r)):
                sp.dma_start(attn[:, i].rearrange("p l d -> p (l d)"),
                             a.rearrange("(o l) h c -> o (l h c)", o=1).to_broadcast([P, L * D])
                             ).then_inc(s_wload, 16)
            sp.dma_start(wrel[:, 0].rearrange("p (r o) -> p r o", r=R), W_rel[0].rearrange("r d o -> d r o")
                         ).then_inc(s_wrload, 16)
            sp.dma_start(src_i[:], src.rearrange("(p c) -> p c", p=EP)).then_inc(s_eload, 16)
            sp.dma_start(typ_i[:], etype.rearrange("(p c) -> p c", p=EP)).then_inc(s_eload, 16)
            sp.dma_start(dst_next[0:EP - 1, :], dst[1:1 + (EP - 1) * EC].rearrange("(p c) -> p c", p=EP - 1)
                         ).then_inc(s_eload, 16)
            sp.dma_start(dst_next[EP - 1:EP, 0:EC - 1],
                         dst[(EP - 1) * EC + 1:E].rearrange("(p c) -> p c", p=1)).then_inc(s_eload, 16)
            sp.dma_start(dst_next[EP - 1:EP, EC - 1:EC],
                         dst[E - 1:E].rearrange("(p c) -> p c", p=1)).then_inc(s_eload, 16)
            sp.dma_start(ew[:], eweight.rearrange("(p c) -> p c", p=EP)).then_inc(s_ewload, 16)
            n_used = [counter(sp, f"sp_used{k}", 0) for k in range(4)]
            n_rows = counter(sp, "sp_rows", 0)
            n_both = counter(sp, "sp_both", 1)
            half = R * ROW // 2

            def load_tile(t, k):
                sp.reg_add(n_used[k], n_used[k], 1)
                sp.wait_ge(s_xin_used[k], n_used[k])
                if isinstance(t, int) and t == T - 1:
                    sp.dma_start(xin[k][0:N - t * P, :], x[t * P:N, :]).then_inc(s_xin[k], 16)
                else:
                    sp.dma_start(xin[k][:], x[bass.ds(t * P, P), :]).then_inc(s_xin[k], 16)

            def save_rows(t, k):
                to = table[0][bass.ds(t * (P * R), P * R), :].rearrange("(p r) f -> p (r f)", r=R)
                rows_k = rows[k][:].rearrange("p r f -> p (r f)")
                sp.reg_add(n_rows, n_rows, 1)
                sp.wait_ge(s_half, n_rows)
                sp.dma_start(to[:, 0:half], rows_k[:, 0:half]).then_inc(s_saved[k][0], 16)
                sp.reg_add(n_both, n_rows, 1)
                sp.wait_ge(s_rows, n_both)
                sp.dma_start(to[:, half:2 * half], rows_k[:, half:2 * half]).then_inc(s_saved[k][1], 16)

            def table_turn(t, k):
                if not (isinstance(t, int) and t >= T - 2):
                    load_tile(t + 2, 2 + k)
                save_rows(t, k)

            def round_(i, k):
                if not (isinstance(i, int) and i == ROUNDS - 1):
                    load_tile(2 * i + ER_AHEAD + 2, 1)
                    load_tile(2 * i + ER_AHEAD + 3, 0)
                table_turn(i, k)

            for t in range(2, ER_AHEAD + 2):
                load_tile(t, t % 2)
            with sp.Fori(0, (ROUNDS - 3) // 2) as i:
                round_(2 * i, 0)
                round_(2 * i + 1, 1)
            sp.dma_start(wfuse[:], W_fuse.rearrange("(k d) o -> d k o", k=2)).then_inc(s_bload, 16)
            sp.dma_start(wgate[:], W_gate[0:D, :]).then_inc(s_bload, 16)
            for l in range(L):
                sp.dma_start(brel[:, l:l + 1], b_rel[l].rearrange("(p o) -> p o", o=1)).then_inc(s_bload, 16)
                sp.dma_start(bgat[:, l:l + 1], b_gat[l].rearrange("(p o) -> p o", o=1)).then_inc(s_bload, 16)
            sp.dma_start(bfuse[:], b_fuse.rearrange("(p o) -> p o", o=1)).then_inc(s_bload, 16)
            sp.dma_start(bfuse_row[:], b_fuse.rearrange("(o p) -> o p", o=1)).then_inc(s_bload, 16)
            sp.dma_start(bgate[:, 0:1], b_gate.rearrange("(p o) -> p o", o=1)).then_inc(s_bload, 16)
            sp.dma_start(bgate[:, 1:2], W_gate[D].rearrange("(p o) -> p o", o=1)).then_inc(s_bload, 16)
            for l in range(1, L):
                sp.dma_start(wrel[:, l].rearrange("p (r o) -> p r o", r=R), W_rel[l].rearrange("r d o -> d r o")
                             ).then_inc(s_bload, 16)
            sp.wait_ge(s_const, 2)
            sp.dma_start(meta_nat[:, 0:T - 1, M_X:META], x[0:(T - 1) * P, :].rearrange("(t p) d -> p t d", p=P)
                         ).then_inc(s_xload, 16)
            sp.dma_start(meta_nat[0:N - (T - 1) * P, T - 1, M_X:META], x[(T - 1) * P:N, :]).then_inc(s_xload, 16)
            for i in range(ROUNDS - 3, ROUNDS):
                round_(i, i % 2)
            with sp.Fori(0, (T - 4 - ROUNDS) // 2) as i:
                table_turn(2 * i + ROUNDS, 1)
                table_turn(2 * i + ROUNDS + 1, 0)
            for t in range(T - 4, T):
                table_turn(t, t % 2)

        @block.gpsimd
        def _(pool):
            g = nc.gpsimd
            g.memset(meta_nat[:, T - 1, :], 0.0).then_inc(s_const, 1)
            g.memset(ones[:], 1.0).then_inc(s_const, 1)
            pool.wait_ge(s_const, 2)
            g.affine_select(out=ident[:], in_=ones[:], pattern=[[-1, P]], compare_op=ALU.is_equal, fill=0.0,
                            base=0, channel_multiplier=1).then_inc(s_const, 1)
            g.affine_select(out=upper[:], in_=ones[:], pattern=[[1, P]], compare_op=ALU.is_gt, fill=0.0,
                            base=0, channel_multiplier=-1).then_inc(s_const, 1)
            g.affine_select(out=lower[:], in_=ones[:], pattern=[[-1, P]], compare_op=ALU.is_gt, fill=0.0,
                            base=0, channel_multiplier=1).then_inc(s_const, 1)
            g.affine_select(out=shift[:], in_=ones[0:LO, :], pattern=[[-1, P]], compare_op=ALU.is_equal, fill=0.0,
                            base=LO, channel_multiplier=1).then_inc(s_const, 1)
            g.iota(iota_row[:], [[1, P]], base=0, channel_multiplier=0,
                   allow_small_or_imprecise_dtypes=True).then_inc(s_const, 1)
            g.iota(iota_slot[:], [[1, ELL]], base=0, channel_multiplier=0,
                   allow_small_or_imprecise_dtypes=True).then_inc(s_const, 1)
            g.memset(zeros_bf[:], 0.0).then_inc(s_const, 1)
            g.memset(tail_idx[:], 0).then_inc(s_const, 1)
            g.memset(tick[:], 0.0)
            g.memset(null_row[:, 0:2 * D], 0.0).then_inc(s_const, 1)
            g.memset(null_row[:, 2 * D:ROW], NEG).then_inc(s_const, 1)
            g.iota(meta_nat[:, :, M_ID], [[P, T]], base=0, channel_multiplier=1,
                   allow_small_or_imprecise_dtypes=True).then_inc(s_const, 1)
            g.memset(meta_nat[:, 0:T - 1, 3], 0.0).then_inc(s_const, 1)
            pool.wait_ge(s_const, CONSTS)
            pool.dma_start(table[0][NULL:NULL + 1, :], null_row[0:1, :]).then_inc(s_stored, 16)
            pool.dma_start(table[1][NULL:NULL + 1, :], null_row[0:1, :]).then_inc(s_out, 16)
            pool.dma_start(edge_rows[E:E + ELL, :].rearrange("(o c) k -> o (c k)", o=1), tail_idx[0:1, :]
                           ).then_inc(s_edge_saved, 16)
            pool.wait_ge(s_edge_rows, 1)
            pool.dma_start(edge_rows[0:E, :].rearrange("(p c) o -> p (c o)", p=EP), src_i[:]
                           ).then_inc(s_edge_saved, 16)
            pool.wait_ge(s_uns, 1)
            pool.wait_ge(s_edge_saved, 32)
            bad = pool.value_load(unsorted_i[0:1, 0:1], min_val=0, max_val=1)
            with pool.If(bad > 0):
                pool.wait_ge(s_edge_rows, 2)
                pool.dma_start(edge_cells[:].rearrange("(p c) o -> p (c o)", p=EP), typ_i[:]
                               ).then_inc(s_edge_saved, 16)
                pool.wait_ge(s_edge_saved, 48)
                pool.dma_start(cursors[:].rearrange("(p t) o -> p (t o)", t=T), starts[:]).then_inc(s_cur, 16)
                pool.wait_ge(s_cur, 16)
                pool.dma_start(edge_rows_raw[:].rearrange("(p c) o -> p (c o)", p=EP),
                               edge_rows[0:E, :].rearrange("(p c) o -> p (c o)", p=EP)).then_inc(s_copy, 16)
                pool.wait_ge(s_copy, 16)
                n_ld, n_v, n_st = (counter(pool, f"pool_sort{i}", v) for i, v in enumerate((48, 1, 32)))
                n_cur = counter(pool, "pool_sort3", 16)
                with pool.Fori(0, EC) as c:
                    at = c * EP
                    pool.dma_start(sort_key[:], edge_cells[bass.ds(at, EP), :].bitcast(U32)).then_inc(s_sort_ld, 16)
                    pool.dma_start(sort_val[:], edge_rows_raw[bass.ds(at, EP), :]).then_inc(s_sort_ld, 16)
                    pool.dma_start(sort_keys[:], edge_cells[bass.ds(at, EP), :].bitcast(U32).rearrange("c o -> o c")
                                   .to_broadcast([EP, EP])).then_inc(s_sort_ld, 16)
                    pool.wait_ge(s_sort_ld, n_ld)
                    pool.reg_add(n_ld, n_ld, 48)
                    pool.indirect_dma_start(
                        out=sort_cur[:], out_offset=None, in_=cursors[:],
                        in_offset=bass.IndirectOffsetOnAxis(ap=sort_key[:], axis=0)
                    ).then_inc(s_sort_cur, 16)
                    pool.wait_ge(s_sort_cur, n_cur)
                    pool.reg_add(n_cur, n_cur, 16)
                    pool.wait_ge(s_sort_v, n_v)
                    pool.reg_add(n_v, n_v, 1)
                    pool.indirect_dma_start(
                        out=edge_rows[:], out_offset=bass.IndirectOffsetOnAxis(ap=sort_pos[:], axis=0),
                        in_=sort_val[:], in_offset=None).then_inc(s_sort_st, 16)
                    pool.indirect_dma_start(
                        out=cursors[:], out_offset=bass.IndirectOffsetOnAxis(ap=sort_cell[:], axis=0),
                        in_=sort_new[:], in_offset=None, bounds_check=NP_ - 1, oob_is_err=False
                    ).then_inc(s_sort_st, 16)
                    pool.wait_ge(s_sort_st, n_st)
                    pool.reg_add(n_st, n_st, 32)
            pool.wait_ge(s_rank, 1)
            pool.wait_ge(s_er, T + 1)
            pool.wait_ge(s_xload, 32)
            for t in range(T):
                pool.indirect_dma_start(
                    out=meta_ranked[:], out_offset=bass.IndirectOffsetOnAxis(ap=rank_u[:, t:t + 1], axis=0),
                    in_=meta_nat[:, t, :], in_offset=None).then_inc(s_scatter, 16)
            pool.wait_ge(s_scatter, 16 * T)
            by_rank = meta_ranked[:].rearrange("(t p) f -> p t f", p=P)
            pool.dma_start(meta[:, :, 0:M_ER], by_rank[:, :, 0:M_ER]).then_inc(s_meta_head, 16)
            pool.dma_start(meta[:, :, M_ER:META], by_rank[:, :, M_ER:META]).then_inc(s_meta, 16)
            pool.wait_ge(s_meta_cols, 3)
            for t in range(T):
                pool.indirect_dma_start(
                    out=ell[:, t, :], out_offset=None, in_=edge_rows[:],
                    in_offset=bass.IndirectOffsetOnAxis(ap=start_u[:, t:t + 1], axis=0)).then_inc(s_ell, 16)
            pool.wait_ge(s_slots_col, 1)
            pool.dma_start(tile_slots_dram[:], tile_slots_col[:]).then_inc(s_slots_saved, 16)
            pool.wait_ge(s_slots_saved, 16)
            pool.dma_start(tile_slots[:], tile_slots_dram[:].rearrange("t o -> o t")).then_inc(s_slots, 16)
            pool.wait_ge(s_slots, 16)

            pool.wait_ge(s_ell_ok, 1)
            pool.wait_ge(s_stored, 16)
            pool.wait_ge(s_out, 16)
            n_staged = counter(pool, "pool_staged", 1)
            n_blk = counter(pool, "pool_blk", 1)
            n_stored_pool = counter(pool, "pool_stored", 16)
            n_out_pool = counter(pool, "pool_out", 16)
            n_free = {b: counter(pool, f"pool_free_{b}", 1) for b in GA}
            n_epi = counter(pool, "pool_epi", 1)
            at = counter(pool, "pool_at", 0)
            left = counter(pool, "pool_left", 0)
            ell_flat = ell[:].rearrange("p t j -> p (t j)")

            def gather(l, b):
                K = GK[b]
                pool.wait_ge(s_free[b], n_free[b])
                pool.reg_add(n_free[b], n_free[b], 1)
                here = pool.snap(at, min_val=0, max_val=(T + 1) * ELL - K)
                g.tensor_copy(stage[b][:].bitcast(I32), ell_flat[:, bass.ds(here, K)]).then_inc(s_staged, 1)
                pool.reg_add(at, at, K)
                pool.wait_ge(s_staged, n_staged)
                pool.reg_add(n_staged, n_staged, 1)
                for k in range(K):
                    pool.indirect_dma_start(
                        out=slots[b][:, k, :], out_offset=None, in_=table[l % 2],
                        in_offset=bass.IndirectOffsetOnAxis(ap=stage[b][:, k:k + 1], axis=0)
                    ).then_inc(s_landed[b], 16)

            def next_block(t, first):
                def done():
                    pool.wait_ge(s_blk, n_blk)
                    pool.reg_add(n_blk, n_blk, 1)

                with pool.If(first):
                    g.tensor_copy(blk_start[:], meta[:, bass.ds(t, 1), M_START]).then_inc(s_blk, 1)
                    done()
                    g.tensor_copy(blk_left[:], meta[:, bass.ds(t, 1), M_CNT]).then_inc(s_blk, 1)
                    done()
                g.tensor_scalar(blk_start[:], blk_start[:], float(BLOCK), float(E), ALU.add, ALU.min
                                ).then_inc(s_blk, 1)
                done()
                g.tensor_scalar(blk_left[:], blk_left[:], -float(BLOCK), None, ALU.add).then_inc(s_blk, 1)
                done()
                g.tensor_copy(blk_start_u[:], blk_start[:]).then_inc(s_blk, 1)
                done()
                pool.indirect_dma_start(
                    out=ell[:, T, :], out_offset=None, in_=edge_rows[:],
                    in_offset=bass.IndirectOffsetOnAxis(ap=blk_start_u[:], axis=0)).then_inc(s_blk_ld, 16)
                pool.wait_ge(s_blk_ld, 16)
                pool.wait_ge(s_free["A"], n_free["A"])
                pool.wait_ge(s_free["B"], n_free["B"])
                pool.wait_ge(s_stored, n_stored_pool)
                pool.wait_ge(s_out, n_out_pool)
                pool.inc_swdge_sem([s_landed["A"], s_landed["B"], s_blk_ld], [LOWER_BY, LOWER_BY, 16], mode="sub")
                pool.sem_inc(s_lowered, 1)
                g.tensor_scalar(blk_f[:, 0], iota_slot[:], blk_left[:], None, ALU.is_lt).then_inc(s_blk, 1)
                done()
                g.tensor_scalar(blk_f[:, 1], ell[:, T, :], -float(NULL), None, ALU.add).then_inc(s_blk, 1)
                done()
                g.tensor_tensor(blk_f[:, 0], blk_f[:, 0], blk_f[:, 1], ALU.mult).then_inc(s_blk, 1)
                done()
                g.tensor_scalar(ell[:, T, :], blk_f[:, 0], float(NULL), None, ALU.add).then_inc(s_blk, 1)
                done()

            def store_tile(l, t):
                if l < L - 1:
                    pool.wait_ge(s_rows, n_rows_pool)
                    pool.reg_add(n_rows_pool, n_rows_pool, 1)
                else:
                    pool.wait_ge(s_yo, n_yo)
                    pool.reg_add(n_yo, n_yo, 1)
                g.tensor_tensor(tick[:, 1:2], tick[:, 0:1], tick[:, 0:1], ALU.add)
                g.tensor_copy(stage_id[:].bitcast(I32), id_u[:, bass.ds(t, 1)].bitcast(I32)).then_inc(s_id, 1)
                pool.wait_ge(s_id, n_epi)
                pool.reg_add(n_epi, n_epi, 2)
                g.tensor_tensor(tick[:, 2:3], tick[:, 0:1], tick[:, 0:1], ALU.add).then_inc(s_id, 1)
                if l < L - 1:
                    pool.indirect_dma_start(
                        out=table[(l + 1) % 2][0:NP_ * R, :].rearrange("(n r) f -> n (r f)", r=R),
                        out_offset=bass.IndirectOffsetOnAxis(ap=stage_id[:], axis=0),
                        in_=rows[0][:].rearrange("p r f -> p (r f)"), in_offset=None).then_inc(s_stored, 16)
                    pool.reg_add(n_stored_pool, n_stored_pool, 16)
                else:
                    pool.indirect_dma_start(
                        out=out, out_offset=bass.IndirectOffsetOnAxis(ap=stage_id[:], axis=0),
                        in_=yo[:], in_offset=None, bounds_check=N - 1, oob_is_err=False).then_inc(s_out, 16)
                    pool.reg_add(n_out_pool, n_out_pool, 16)

            n_rows_pool = counter(pool, "pool_rows", T + 2)
            n_yo = counter(pool, "pool_yo", 1)

            def tile(l, t):
                n, pairs, in_first = load_slots(pool, t)
                pool.reg_mov(at, t * ELL)
                with pool.Fori(0, in_first):
                    gather(l, "A")
                    gather(l, "B")
                with pool.If(pairs > BLOCK // PAIR):
                    now = counter(pool, f"pool_now{nc.next_id()}", 0)
                    blocks = counter(pool, f"pool_blocks{nc.next_id()}", 0)
                    pool.reg_sub(left, pairs, BLOCK // PAIR)
                    pool.reg_sub(blocks, pairs, 1)
                    pool.reg_alu(blocks, blocks, (BLOCK // PAIR).bit_length() - 1, ALU.logical_shift_right)
                    with pool.Fori(0, pool.snap(blocks, min_val=1, max_val=E // BLOCK)) as b:
                        next_block(t, b < 1)
                        pool.reg_mov(at, T * ELL)
                        pool.reg_alu(now, left, BLOCK // PAIR, ALU.min)
                        pool.reg_sub(left, left, now)
                        with pool.Fori(0, pool.snap(now, min_val=1, max_val=BLOCK // PAIR)):
                            gather(l, "A")
                            gather(l, "B")
                tail_groups(pool, n, lambda b, K: gather(l, b))

            for l in range(L):
                if l == 0:
                    for k, j in ((0, 0), (0, 1), (1, 0), (1, 1)):
                        pool.wait_ge(s_saved[k][j], 16 * (T // 2 + 2 - k))
                else:
                    pool.wait_ge(s_stored, 16 * (1 + l * T))
                tile(l, 0)
                with pool.Fori(1, T) as t:
                    tile(l, t)
                    store_tile(l, t - 1)
                store_tile(l, T - 1)
            pool.wait_ge(s_out, 16 * (1 + T))

        @block.scalar
        def _(act):
            s = nc.scalar
            n_tab = counter(act, "act_tab", 1)
            n_saved = [counter(act, f"act_saved{k}", 16) for k in range(2)]

            def evacuate_chunk(k, c):
                act.wait_ge(s_chunk[c], n_tab)
                s.activation(rows[k][:, c * RC:(c + 1) * RC, 0:D],
                             ps_tab[c % 2][:].rearrange("p (r f) -> p r f", r=RC), ACT.Copy
                             ).then_inc(s_bank[(c + 2) % 4], 1)

            def evacuate_table(k, meta_col):
                for c in range(4):
                    evacuate_chunk(k, c)
                act.wait_ge(s_z_ps, n_tab)
                s.activation(rows[k][:, :, D:ROW], bc(ps_z[:, 0:D + H], R), ACT.Copy)
                s.activation(meta_col, ps_z[:, D + H:ZW].rearrange("p (o f) -> p o f", o=1), ACT.Copy
                             ).then_inc(s_rows, 1)
                act.reg_add(n_tab, n_tab, 1)

            act.sem_inc(s_bank[0], 1)
            act.sem_inc(s_bank[1], 1)
            act.sem_inc(s_rows, 1)
            act.sem_inc(s_er, 1)
            n_xT = counter(act, "act_xT", 1)
            n_er = counter(act, "act_er", 1)

            def transposed_x(k):
                act.wait_ge(s_xT_ps, n_xT)
                s.activation(hT[k][:], ps_xT[k], ACT.Copy).then_inc(s_hT[k], 1)
                act.reg_add(n_xT, n_xT, 1)

            def natural_er(t, k):
                transposed_x(k)
                act.wait_ge(s_er_ps, n_er)
                s.activation(meta_nat[:, bass.ds(t, 1), M_ER:M_X],
                             ps_gat[:, 0:H + D].rearrange("p (o f) -> p o f", o=1), ACT.Copy).then_inc(s_er, 1)
                act.reg_add(n_er, n_er, 1)

            def natural_rows(k, next_x=False):
                for j in range(2):
                    if j == 1 and next_x:
                        transposed_x(3 - k)
                    act.wait_ge(s_saved[k][j], n_saved[k])
                    for c in (2 * j, 2 * j + 1):
                        evacuate_chunk(k, c)
                    if j == 0:
                        act.wait_ge(s_z_ps, n_tab)
                    s.activation(rows[k][:, j * R // 2:(j + 1) * R // 2, D:ROW], bc(ps_z[:, 0:D + H], R // 2),
                                 ACT.Copy).then_inc((s_half, s_rows)[j], 1)
                act.reg_add(n_saved[k], n_saved[k], 16)
                act.reg_add(n_tab, n_tab, 1)

            def round_(i, k):
                natural_er(2 * i + ER_AHEAD, 1)
                transposed_x(2 + k)
                natural_er(2 * i + ER_AHEAD + 1, 0)
                natural_rows(k)

            for k in range(2):
                for j in range(2):
                    act.sem_inc(s_saved[k][j], 16)
            act.wait_ge(s_const, CONSTS)
            for t in range(ER_AHEAD):
                natural_er(t, t % 2)
            with act.Fori(0, (ROUNDS - 1) // 2) as i:
                round_(2 * i, 0)
                round_(2 * i + 1, 1)
            round_(ROUNDS - 1, 0)
            transposed_x(3)
            with act.Fori(0, (T - ROUNDS - 2) // 2):
                natural_rows(1, next_x=True)
                natural_rows(0, next_x=True)
            natural_rows(1, next_x=True)
            natural_rows(0)

            n_g = counter(act, "act_group", 1)
            n_e = counter(act, "act_epi", 1)

            def group(K):
                act.wait_ge(s_logit, n_g)
                s.activation(zx[:, 8 - K:9, :, DH], logit[:, 8 - K:9, :], ACT.Exp).then_inc(s_wgt, 1)
                act.reg_add(n_g, n_g, 1)

            def transposed(l):
                act.wait_ge(s_T_ps, n_e)
                s.activation(hrT[:], mix[0], ACT.Identity, bias=brel[:, l:l + 1])
                s.activation(hgT[:], mix[1], ACT.Identity, bias=bgat[:, l:l + 1]).then_inc(s_T, 1)

            def fused(l):
                if l < L - 1:
                    act.wait_ge(s_fuse, n_e)
                if l == 0:
                    s.activation(hc[:], mix[2], ACT.Identity, bias=bfuse[:]).then_inc(s_hc, 1)
                elif l < L - 1:
                    s.activation(hT[0][:], mix[2], ACT.Relu, bias=bfuse[:]).then_inc(s_hT[0], 1)

            def gate_and_table(l, t):
                if l == 0:
                    act.wait_ge(s_gate_ps, n_e0)
                    s.activation(th[:], mix[3], ACT.Tanh, bias=gate_bias[:], scale=0.5).then_inc(s_th, 1)
                    act.reg_add(n_e0, n_e0, 1)
                if l < L - 1:
                    act.wait_ge(s_stored, n_stored)
                    act.reg_add(n_stored, n_stored, 16)
                    evacuate_table(0, meta[:, bass.ds(t, 1), M_ER:M_X])
                act.reg_add(n_e, n_e, 1)

            n_e0 = counter(act, "act_epi0", 1)
            n_stored = counter(act, "act_stored", 16)

            def tile(l, t, previous):
                n, pairs, _ = load_slots(act, t)
                for b in ("A", "B"):
                    group(8)
                    if previous is not None and b == "A":
                        transposed(l)
                        fused(l)
                    if previous is not None and b == "B":
                        gate_and_table(l, previous)
                with act.If(pairs > 1):
                    with act.Fori(1, pairs):
                        group(8)
                        group(8)
                tail_groups(act, n, lambda b, K: group(K))

            act.wait_ge(s_bload, 16 * (5 + 3 * L))
            act.wait_ge(s_slots, 16)
            act.wait_ge(s_gbias, 1)
            for j in range(2):
                act.wait_ge(s_saved[0][j], 16 * (T // 2 + 2))
            act.wait_ge(s_meta, 16)
            for l in range(L):
                tile(l, 0, None)
                with act.Fori(1, T) as t:
                    tile(l, t, t - 1)
                transposed(l)
                fused(l)
                gate_and_table(l, T - 1)

        @block.tensor
        def _(pe):
            n_tab = counter(pe, "pe_tab", 1)

            def table_products(l, k, hT_count, width=ZW, mid=None):
                pe.wait_ge(s_hT[k], hT_count)
                for c in range(4):
                    pe.wait_ge(s_bank[c], n_tab)
                    pe.matmul(ps_tab[c % 2][:], hT[k][:], wrel[:, l, c * RC * D:(c + 1) * RC * D],
                              start=True, stop=True).then_inc(s_chunk[c], 1)
                    if c == 0:
                        pe.wait_ge(s_rows, n_tab)
                        pe.matmul(ps_z[:, 0:width], hT[k][:], wz[:, l, 0:width], start=True, stop=True
                                  ).then_inc(s_z_ps, 1)
                    if c == 1 and mid:
                        mid()
                pe.reg_add(n_tab, n_tab, 1)

            pe.wait_ge(s_const, CONSTS)
            pe.wait_ge(s_wload, 16 * 4)
            pe.wait_ge(s_wz, 1)
            n_xin = [counter(pe, f"pe_xin{k}", 16) for k in range(4)]
            n_hT = [counter(pe, f"pe_hT{k}", 1) for k in range(4)]
            n_er = counter(pe, "pe_er", 1)

            def transpose_x(k):
                pe.wait_ge(s_xin[k], n_xin[k])
                pe.reg_add(n_xin[k], n_xin[k], 16)
                pe.transpose(ps_xT[k], xin[k][:], ident[:]).then_inc(s_xT_ps, 1)

            def transposed_x(k):
                pe.wait_ge(s_hT[k], n_hT[k])
                pe.sem_inc(s_xin_used[k], 1)

            def natural_er(k):
                transposed_x(k)
                pe.wait_ge(s_er, n_er)
                pe.reg_add(n_er, n_er, 1)
                pe.matmul(ps_gat[:, 0:H + D], hT[k][:], wz[:, 0, D + H:ZW], start=True, stop=True
                          ).then_inc(s_er_ps, 1)
                pe.reg_add(n_hT[k], n_hT[k], 1)

            def natural_rows(k, next_x=False):
                transposed_x(2 + k)
                table_products(0, 2 + k, n_hT[2 + k], D + H, mid=(lambda: transpose_x(3 - k)) if next_x else None)
                pe.reg_add(n_hT[2 + k], n_hT[2 + k], 1)

            for j in range(3):
                pe.sem_inc(s_oh_used[j], 1)
            hist = ps_cnt[0:LO, 0:HI]
            pe.matmul(hist, zeros_bf[0:EP, 0:LO], zeros_bf[0:EP, 0:HI], start=True, stop=False,
                      skip_group_check=True)
            n_oh = counter(pe, "pe_oh", 1)

            def count_batch(j):
                pe.wait_ge(s_oh[j], n_oh)
                for c in range(HB):
                    mm = pe.matmul(hist, oh[j][0:EP, 0:LO, c], oh[j][0:EP, LO:LO + HI, c], start=False,
                                   stop=False, skip_group_check=True)
                mm.then_inc(s_oh_used[j], 1)

            for t in range(ER_AHEAD):
                transpose_x(t % 2)
                natural_er(t % 2)
            pe.wait_ge(s_wrload, 16)

            def round_(k):
                transpose_x(1)
                count_batch(0)
                natural_er(1)
                transpose_x(2 + k)
                transpose_x(0)
                count_batch(1)
                natural_er(0)
                natural_rows(k)
                count_batch(2)
                pe.reg_add(n_oh, n_oh, 1)

            with pe.Fori(0, (ROUNDS - 1) // 2):
                round_(0)
                round_(1)
            round_(0)
            transpose_x(3)
            pe.matmul(hist, zeros_bf[0:EP, 0:LO], zeros_bf[0:EP, 0:HI], start=False, stop=True,
                      skip_group_check=True).then_inc(s_hist, 1)
            pe.wait_ge(s_cnt, 1)
            halves = counts[:].rearrange("p (t o) -> p o t", o=2)
            pe.matmul(ps_rel[:, 0:T], ident[0:LO, :], halves[:, 0], start=True, stop=False)
            pe.matmul(ps_rel[:, 0:T], shift[:], halves[:, 1], start=False, stop=True).then_inc(s_deg_nat, 1)
            pe.wait_ge(s_cls, 1)
            pe.wait_ge(s_er, T + 1)
            for t in range(T):
                mm = pe.matmul(ps_gat[:, t:t + 1], oh_cls[:, :, t], values[:, 1, 0:1], start=True, stop=True)
            mm.then_inc(s_cls_ps, 1)
            natural_rows(1, next_x=True)
            pe.wait_ge(s_deg, 1)
            pe.matmul(ps_cnt[:, 128:128 + T], upper[:], degree[:], start=True, stop=False)
            pe.matmul(ps_cnt[:, 128:128 + T], ones[:], before[:], start=False, stop=True)
            pe.wait_ge(s_cls_cum, 1)
            pe.matmul(ps_gat[:, 64:65], lower[:], cls_cum[:, T - 1:T], start=True, stop=True
                      ).then_inc(s_above_ps, 1)
            pe.wait_ge(s_uns_in, 1)
            pe.matmul(ps_cnt[:, 256:257], ones[0:EP, :], unsorted_f[0:EP, :], start=True, stop=True)
            pe.wait_ge(s_tws, 1)
            pe.matmul(ps_cnt[:, 260:261], ones[0:EP, :], wsum[0:EP, 0:1], start=True, stop=True
                      ).then_inc(s_start_ps, 1)
            natural_rows(0, next_x=True)
            for c in range(-(-T // 4)):
                tiles = range(4 * c, min(4 * c + 4, T))
                place = (ps_rel, ps_gat)[c % 2][:, 0:len(tiles) * CLS].rearrange("p (t v) -> p t v", v=CLS)
                pe.wait_ge(s_diag, c + 1)
                if c >= 2:
                    pe.wait_ge(s_picked, c - 1)
                pe.matmul(place, upper_bf[:], oh_cls[:, :, tiles[0]:tiles[-1] + 1].rearrange("p v t -> p t v"),
                          start=True, stop=False, skip_group_check=True)
                pe.matmul(place, ones[:], diag[c % 2][:, 0:len(tiles)], start=False, stop=True,
                          skip_group_check=True).then_inc(s_place_ps, 1)
            LAST = 4
            with pe.Fori(0, (T - ROUNDS - 2 - LAST) // 2):
                natural_rows(1, next_x=True)
                natural_rows(0, next_x=True)
            pe.wait_ge(s_meta_cols, 3)
            pe.transpose(ps_cnt[0:T, 0:P], cnt_r[:], ident[:]).then_inc(s_deg_ps, 1)
            with pe.Fori(0, (LAST - 2) // 2):
                natural_rows(1, next_x=True)
                natural_rows(0, next_x=True)
            natural_rows(1, next_x=True)
            natural_rows(0)

            pe.wait_ge(s_bload, 16 * (5 + 3 * L))
            pe.wait_ge(s_slots, 16)
            n_land = {b: counter(pe, f"pe_land_{b}", 16 * GK[b]) for b in GA}
            n_g = counter(pe, "pe_group", 1)
            n_e = counter(pe, "pe_epi", 1)
            n_e0 = counter(pe, "pe_epi0", 1)
            n_lowered = counter(pe, "pe_lowered", 1)
            for b in GA:
                pe.sem_inc(s_free[b], 1)

            def group(b, first=False, mid=None):
                K = GK[b]
                pe.wait_ge(s_landed[b], n_land[b])
                pe.reg_add(n_land[b], n_land[b], 16 * K)
                if first:
                    pe.wait_ge(s_h2, n_h)
                for k in range(K):
                    mm = pe.matmul(ps_rel[:, 0:D], ident[:], slots[b][:, k, 0:D], start=first and k == 0,
                                   stop=True, skip_group_check=True)
                if mid:
                    mid()
                pe.wait_ge(s_zx, n_g)
                zs = zx[:].rearrange("p k h e -> p k (h e)")
                W = H * EX
                if K == 1:
                    pe.matmul(ps_gat[:, 0:W // 2], ident[:], zs[:, 7, 0:W // 2], start=True, stop=True,
                              skip_group_check=True).then_inc(s_free[b], 1)
                    pe.matmul(ps_gat[:, W // 2:W], ident[:], zs[:, 7, W // 2:W], start=True, stop=True,
                              skip_group_check=True).then_inc(s_gat, 1)
                else:
                    for k in range(K):
                        mm = pe.matmul(ps_gat[:, 0:W], ident[:], zs[:, 8 - K + k, :], start=(k == 0),
                                       stop=(k == K - 1))
                        if k == 0:
                            mm.then_inc(s_free[b], 1)
                    mm.then_inc(s_gat, 1)
                pe.reg_add(n_g, n_g, 1)

            def transpose_sums(l):
                pe.wait_ge(s_h2, n_h)
                pe.transpose(mix[0], hr[:], ident[:])
                pe.transpose(mix[1], hg[:].rearrange("p h c -> p (h c)"), ident[:]).then_inc(s_T_ps, 1)

            def fuse(l):
                pe.wait_ge(s_T, n_e)
                if l < L - 1:
                    pe.matmul(mix[2], wfuse[:, 0], hrT[:], start=True, stop=False)
                    pe.matmul(mix[2], wfuse[:, 1], hgT[:], start=False, stop=True).then_inc(s_fuse, 1)
                else:
                    pe.matmul(mix[2], ones[0:1, :], bfuse_row[:], start=True, stop=False)
                    pe.matmul(mix[2], hrT[:], wfuse[:, 0], start=False, stop=False)
                    pe.matmul(mix[2], hgT[:], wfuse[:, 1], start=False, stop=True).then_inc(s_fuse, 1)

            def gate(l):
                if l == 0:
                    pe.wait_ge(s_hc, n_e0)
                    pe.matmul(mix[3], wgate[:], hc[:], start=True, stop=True).then_inc(s_gate_ps, 1)

            def table_of(l):
                if l < L - 1:
                    table_products(l + 1, 0, n_hT[0])
                    pe.reg_add(n_hT[0], n_hT[0], 1)
                if l == 0:
                    pe.reg_add(n_e0, n_e0, 1)
                pe.reg_add(n_e, n_e, 1)

            n_h = counter(pe, "pe_h2", 1)

            def tile(l, t, previous):
                n, pairs, in_first = load_slots(pe, t)
                if previous:
                    group("A", first=True, mid=lambda: transpose_sums(l))
                    fuse(l)
                    group("B", mid=lambda: gate(l))
                    table_of(l)
                else:
                    group("A", first=True)
                    group("B")
                pair_loops(pe, pairs, in_first, n_lowered, n_land, lambda: (group("A"), group("B")))
                tail_groups(pe, n, lambda b, K: group(b))
                pe.reg_add(n_h, n_h, 1)

            for l in range(L):
                tile(l, 0, False)
                with pe.Fori(1, T) as t:
                    tile(l, t, True)
                transpose_sums(l)
                fuse(l)
                gate(l)
                table_of(l)

        @block.vector
        def _(dve):
            v = nc.vector
            done = 0

            def step(ins):
                nonlocal done
                done += 1
                ins.then_inc(s_v, 1)
                dve.wait_ge(s_v, done)

            dve.wait_ge(s_const, CONSTS)
            v.tensor_copy(upper_bf[:], upper[:])
            v.tensor_copy(values[:], bc_last(iota_row[:], HB))
            dve.wait_ge(s_dload, 16)
            v.tensor_scalar(lo_i[:], dst_i[:], LO - 1, None, ALU.bitwise_and)
            step(v.tensor_scalar(hi_i[:], dst_i[:], LO.bit_length() - 1, None, ALU.logical_shift_right))
            v.tensor_copy(lo_bf[:], lo_i[:])
            step(v.tensor_copy(hi_bf[:], hi_i[:]))

            n = counter(dve, "v_oh", 1)

            def onehots(batch, j):
                dve.wait_ge(s_oh_used[j], n)
                at = batch * HB
                v.tensor_tensor(oh[j][0:EP, LO:LO + HI, :], bc(hi_bf[:, bass.ds(at, HB)], HI), values[0:EP, 0:HI, :],
                                ALU.is_equal)
                v.tensor_tensor(oh[j][0:EP, 0:LO, :], bc(lo_bf[:, bass.ds(at, HB)], LO), values[0:EP, 0:LO, :],
                                ALU.is_equal).then_inc(s_oh[j], 1)

            def fold(l):
                nonlocal folded
                for i in range(2):
                    folded += 1
                    v.tensor_tensor(attn_tmp[:], wz[:, l, 0:D], attn[:, i, l], ALU.mult).then_inc(s_fold, 1)
                    dve.wait_ge(s_fold, folded)
                    r = v.tensor_reduce(wz[:, l, D + i * H:D + (i + 1) * H],
                                        attn_tmp[:].rearrange("p (h c) -> p h c", h=H), AX.X, ALU.add)
                    if i == 0:
                        folded += 1
                        r.then_inc(s_fold, 1)
                        dve.wait_ge(s_fold, folded)
                    else:
                        r.then_inc(s_wz, 1)
                        dve.wait_ge(s_wz, l + 1)

            folded = 0
            dve.wait_ge(s_wload, 16 * 4)
            fold(0)
            with dve.Fori(0, EC // (3 * HB)) as i:
                for j in range(3):
                    onehots(i * 3 + j, j)
                dve.reg_add(n, n, 1)

            dve.wait_ge(s_hist, 1)
            v.tensor_copy(counts[:], ps_cnt[0:LO, 0:HI]).then_inc(s_cnt, 1)
            dve.wait_ge(s_eload, 16 * 5)
            v.scalar_tensor_tensor(src_i[:], src_i[:], float(R), typ_i[:], ALU.mult, ALU.add).then_inc(s_edge_rows, 1)
            dve.wait_ge(s_deg_nat, 1)
            step(v.tensor_copy(degree[:], ps_rel[:, 0:T]))
            step(v.tensor_scalar(cls[:], degree[:], float(CLS - 1), None, ALU.min))
            v.tensor_tensor(oh_cls, bc(cls[:], CLS), values[:, :, 0:T], ALU.is_equal).then_inc(s_cls, 1)
            v.memset(before[:, 0:1], 0.0)
            v.tensor_tensor_scan(before[:, 1:T], ones[:, 0:T - 1], degree[:, 0:T - 1], 0.0, ALU.mult, ALU.add
                                 ).then_inc(s_deg, 1)
            v.tensor_copy(meta_nat[:, :, M_CNT], degree[:])
            step(v.tensor_tensor(dst_next[:], dst_i[:], dst_next[:], ALU.is_gt))
            v.tensor_reduce(unsorted_f[0:EP, :], dst_next[:], AX.X, ALU.add).then_inc(s_uns_in, 1)

            dve.wait_ge(s_cls_ps, 1)
            step(v.tensor_copy(cls_count[:], ps_gat[:, 0:T]))
            v.tensor_tensor_scan(cls_cum[:], ones[:, 0:T], cls_count[:], 0.0, ALU.mult, ALU.add
                                 ).then_inc(s_cls_cum, 1)
            dve.wait_ge(s_ewload, 16)
            v.tensor_reduce(wsum[0:EP, 0:1], ew[:], AX.X, ALU.add).then_inc(s_tws, 1)
            dve.wait_ge(s_above_ps, 1)
            step(v.tensor_copy(cls_above[:], ps_gat[:, 64:65]))
            v.tensor_copy(cls_base[:, 0:1], cls_above[:])
            step(v.tensor_scalar(cls_base[:, 1:T], cls_cum[:, 0:T - 1], cls_above[:], None, ALU.add))

            chunks = [range(4 * c, min(4 * c + 4, T)) for c in range(-(-T // 4))]

            def diagonals(c):
                tiles = chunks[c]
                v.tensor_tensor(diag[c % 2][:, 0:len(tiles)], bc(ident[:], len(tiles)),
                                bc_last(cls_base[:, tiles[0]:tiles[-1] + 1], CLS), ALU.mult).then_inc(s_diag, 1)

            diagonals(0)
            diagonals(1)
            for c, tiles in enumerate(chunks):
                dve.wait_ge(s_place_ps, c + 1)
                place = (ps_rel, ps_gat)[c % 2][:, 0:len(tiles) * CLS].rearrange("p (t v) -> p t v", v=CLS)
                v.tensor_tensor(picked[c % 2][:, 0:len(tiles)], place,
                                oh_cls[:, :, tiles[0]:tiles[-1] + 1].rearrange("p v t -> p t v"), ALU.mult
                                ).then_inc(s_picked, 1)
                if c + 2 < len(chunks):
                    diagonals(c + 2)
                dve.wait_ge(s_picked, c + 1)
                step(v.tensor_reduce(rank[:, tiles[0]:tiles[-1] + 1], picked[c % 2][:, 0:len(tiles)], AX.X, ALU.add))
            dve.wait_ge(s_start_ps, 1)
            step(v.tensor_copy(starts[:], ps_cnt[:, 128:128 + T]))
            v.tensor_copy(meta_nat[:, :, M_START], starts[:])
            v.tensor_copy(rank_u[:], rank[:]).then_inc(s_rank, 1)

            v.tensor_scalar(unsorted_i[:], ps_cnt[0:1, 256:257], 1.0, None, ALU.min).then_inc(s_uns, 1)
            step(v.tensor_scalar(tw_mean[:], ps_cnt[:, 260:261], 1.0 / E, None, ALU.mult))
            dve.wait_ge(s_bload, 16 * (5 + 3 * L))
            step(v.tensor_scalar(gate_bias[:], bgate[:, 1:2], tw_mean[:], bgate[:, 0:1], ALU.mult, ALU.add))
            v.tensor_scalar(gate_bias[:], gate_bias[:], 0.5, None, ALU.mult).then_inc(s_gbias, 1)
            for l in range(1, L):
                fold(l)

            dve.wait_ge(s_uns, 1)
            bad = dve.value_load(unsorted_i[0:1, 0:1], min_val=0, max_val=1)
            with dve.If(bad > 0):
                n_ld = counter(dve, "v_sort_ld", 48)
                n_cur = counter(dve, "v_sort_cur", 16)
                n_c = counter(dve, "v_sort_c", 1)

                def sort_step(ins):
                    ins.then_inc(s_sort_c, 1)
                    dve.wait_ge(s_sort_c, n_c)
                    dve.reg_add(n_c, n_c, 1)

                sort_step(v.tensor_scalar(lo_i[:], dst_i[:], P - 1, None, ALU.bitwise_and))
                sort_step(v.tensor_scalar(hi_i[:], dst_i[:], P.bit_length() - 1, None, ALU.logical_shift_right))
                dve.wait_ge(s_edge_rows, 1)
                v.scalar_tensor_tensor(typ_i[:], lo_i[:], float(T), hi_i[:], ALU.mult, ALU.add
                                       ).then_inc(s_edge_rows, 1)

                with dve.Fori(0, EC):
                    dve.wait_ge(s_sort_ld, n_ld)
                    dve.wait_ge(s_sort_cur, n_cur)
                    dve.reg_add(n_ld, n_ld, 48)
                    dve.reg_add(n_cur, n_cur, 16)
                    sort_step(v.tensor_copy(sort_f[:, 0:1], sort_key[:]))
                    sort_step(v.tensor_scalar(sort_eq[:, 0], sort_keys[:], sort_f[:, 0:1], None, ALU.is_equal))
                    sort_step(v.tensor_tensor(sort_eq[:, 1], sort_eq[:, 0], upper[0:EP, 0:EP], ALU.mult))
                    v.tensor_reduce(sort_f[:, 2:3], sort_eq[:, 1], AX.X, ALU.add)
                    sort_step(v.tensor_reduce(sort_f[:, 1:2], sort_eq[:, 0], AX.X, ALU.add))
                    sort_step(v.tensor_tensor(sort_f[:, 1:2], sort_f[:, 1:2], sort_f[:, 2:3], ALU.subtract))
                    sort_step(v.tensor_tensor(sort_new[:], sort_f[:, 1:2], sort_cur[:], ALU.add))
                    v.tensor_scalar(sort_pos[:], sort_new[:], -1.0, None, ALU.add)
                    sort_step(v.tensor_scalar(sort_f[:, 3:4], sort_f[:, 2:3], 0.0, float(NP_), ALU.is_gt, ALU.mult))
                    v.tensor_tensor(sort_cell[:], sort_f[:, 3:4], sort_f[:, 0:1], ALU.add).then_inc(s_sort_v, 1)

            dve.wait_ge(s_meta_head, 16)
            v.tensor_copy(start_u[:], meta[:, :, M_START]).then_inc(s_meta_cols, 1)
            v.tensor_copy(id_u[:], meta[:, :, M_ID]).then_inc(s_meta_cols, 1)
            v.tensor_copy(cnt_r[:], meta[:, :, M_CNT]).then_inc(s_meta_cols, 1)
            dve.wait_ge(s_deg_ps, 1)
            step(v.tensor_reduce(tile_slots_f[:], ps_cnt[0:T, 0:P], AX.X, ALU.max))
            v.tensor_scalar(tile_slots_col[:], tile_slots_f[:], float(PAIR), None, ALU.max).then_inc(s_slots_col, 1)
            dve.wait_ge(s_meta_cols, 3)
            step(v.tensor_tensor(ell_valid, bc(iota_slot[:], T), bc_last(cnt_r[:], ELL), ALU.is_lt))
            dve.wait_ge(s_ell, 16 * T)
            step(v.scalar_tensor_tensor(ell_valid, ell[:, 0:T], -float(NULL), ell_valid, ALU.add, ALU.mult))
            v.tensor_scalar(ell[:, 0:T], ell_valid, float(NULL), None, ALU.add).then_inc(s_ell_ok, 1)

            v.memset(acc[:], 0.0).then_inc(s_acc, 1)
            dve.wait_ge(s_slots, 16)
            dve.wait_ge(s_meta, 16)
            dve.sem_inc(s_h2, 1)
            n_land = {b: counter(dve, f"v_land_{b}", 16 * GK[b]) for b in GA}
            n_g = counter(dve, "v_group", 1)
            n_t = counter(dve, "v_tile", 1)
            n_lowered = counter(dve, "v_lowered", 1)
            n_norm = counter(dve, "v_norm", 1)
            n_e = counter(dve, "v_epi", 1)
            n_out = counter(dve, "v_out", 16)

            def group(b):
                K = GK[b]
                lo = 8 - K
                dve.wait_ge(s_landed[b], n_land[b])
                dve.reg_add(n_land[b], n_land[b], 16 * K)
                dve.wait_ge(s_acc, n_g)
                v.tensor_tensor(raw[:, lo:8], slots[b][:, :, 2 * D:ROW], er_cur[:].to_broadcast([P, K, H]), ALU.add
                                ).then_inc(s_raw, 1)
                dve.wait_ge(s_raw, n_g)
                v.tensor_reduce(top[:, 0], raw[:, lo:9].rearrange("p k h -> p h k"), AX.X, ALU.max
                                ).then_inc(s_top, 1)
                v.scalar_tensor_tensor(leaky[:, lo:9], raw[:, lo:9], SLOPE, raw[:, lo:9], ALU.mult, ALU.max
                                       ).then_inc(s_leaky, 1)
                dve.wait_ge(s_top, n_g)
                v.scalar_tensor_tensor(peak[:], top[:], SLOPE, top[:], ALU.mult, ALU.max).then_inc(s_peak, 1)
                dve.wait_ge(s_leaky, n_g)
                v.tensor_copy(raw[:, 8:9], top[:]).then_inc(s_keep, 1)
                dve.wait_ge(s_peak, n_g)
                v.tensor_tensor(logit[:, lo:9], leaky[:, lo:9], peak[:].to_broadcast([P, K + 1, H]), ALU.subtract
                                ).then_inc(s_logit, 1)
                dve.wait_ge(s_keep, n_g)
                dve.wait_ge(s_wgt, n_g)
                v.tensor_tensor(zx[:, lo:8, :, 0:DH], slots[b][:, :, D:2 * D].rearrange("p k (h c) -> p k h c", h=H),
                                zx[:, lo:8, :, DH:EX].to_broadcast([P, K, H, DH]), ALU.mult).then_inc(s_zx, 1)
                v.tensor_tensor(acc[:], acc[:], zx[:, 8, :, DH:EX].to_broadcast([P, H, EX]), ALU.mult
                                ).then_inc(s_scaled, 1)
                dve.wait_ge(s_scaled, n_g)
                dve.wait_ge(s_gat, n_g)
                v.tensor_tensor(acc[:], acc[:], ps_gat[:, 0:H * EX].rearrange("p (h e) -> p h e", h=H), ALU.add
                                ).then_inc(s_acc, 1)
                dve.reg_add(n_g, n_g, 1)

            def start_tile(t):
                v.tensor_copy(er_cur[:], meta[:, bass.ds(t, 1), M_ER:M_LOOP])
                v.memset(raw[:, 8:9], LEAST).then_inc(s_tile, 1)
                dve.wait_ge(s_tile, n_t)
                dve.reg_add(n_t, n_t, 1)

            def end_tile(t):
                dve.wait_ge(s_acc, n_g)
                v.reciprocal(rden[:], acc[:, :, DH:EX]).then_inc(s_rden, 1)
                v.tensor_tensor(hr[:], ps_rel[:, 0:D], meta[:, bass.ds(t, 1), M_LOOP:M_X].rearrange("p o f -> p (o f)"),
                                ALU.add)
                dve.wait_ge(s_rden, n_rd)
                dve.reg_add(n_rd, n_rd, 1)
                v.tensor_tensor(hg[:], acc[:, :, 0:DH], rden[:].to_broadcast([P, H, DH]), ALU.mult
                                ).then_inc(s_h2, 1)

            n_rd = counter(dve, "v_rden", 1)

            def norm_step(ins):
                ins.then_inc(s_norm, 1)
                dve.wait_ge(s_norm, n_norm)
                dve.reg_add(n_norm, n_norm, 1)

            def epilogue(l, t):
                if l == 0:
                    dve.wait_ge(s_th, n_e)
                    v.scalar_tensor_tensor(th[:], th[:], 1.0, hc[:], ALU.add, ALU.mult).then_inc(s_gated, 1)
                    dve.wait_ge(s_gated, n_e)
                    v.tensor_scalar(hT[0][:], th[:], 0.5, 0.0, ALU.mult, ALU.max).then_inc(s_hT[0], 1)
                    dve.reg_add(n_e, n_e, 1)
                elif l == L - 1:
                    dve.wait_ge(s_fuse, n_f)
                    norm_step(v.scalar_tensor_tensor(y[:], mix[2], 0.0, meta[:, bass.ds(t, 1), M_X:META]
                                                     .rearrange("p o f -> p (o f)"), ALU.max, ALU.add))
                    norm_step(v.bn_stats(stats[:], y[:]))
                    norm_step(v.bn_aggr(mv[:], stats[:]))
                    norm_step(v.tensor_scalar(ve[:], mv[:, 1:2], EPS, None, ALU.add))
                    norm_step(v.tensor_scalar(nv_i[:], ve[:].bitcast(I32), 1, None, ALU.logical_shift_right))
                    norm_step(v.tensor_scalar(nv[:, 0:1].bitcast(I32), nv_i[:], -1.0, float(0x5f3759df),
                                              ALU.mult, ALU.add))
                    for _ in range(4):
                        norm_step(v.tensor_scalar(nv[:, 1:2], nv[:, 0:1], nv[:, 0:1], ve[:], ALU.mult, ALU.mult))
                        norm_step(v.tensor_scalar(nv[:, 1:2], nv[:, 1:2], -0.5, 1.5, ALU.mult, ALU.add))
                        norm_step(v.tensor_tensor(nv[:, 0:1], nv[:, 0:1], nv[:, 1:2], ALU.mult))
                    dve.wait_ge(s_out, n_out)
                    dve.reg_add(n_out, n_out, 16)
                    v.tensor_scalar(yo[:], y[:], mv[:, 0:1], nv[:, 0:1], ALU.subtract, ALU.mult).then_inc(s_yo, 1)
                    dve.reg_add(n_f, n_f, 1)

            n_f = counter(dve, "v_fuse", (L - 1) * T + 1)

            def tile(l, t, previous):
                n, pairs, in_first = load_slots(dve, t)
                start_tile(t)
                group("A")
                group("B")
                if previous is not None:
                    epilogue(l, previous)
                pair_loops(dve, pairs, in_first, n_lowered, n_land, lambda: (group("A"), group("B")))
                tail_groups(dve, n, lambda b, K: group(b))
                end_tile(t)

            for l in range(L):
                if l:
                    dve.wait_ge(s_rows, T + 1 + l * T)
                tile(l, 0, None)
                with dve.Fori(1, T) as t:
                    tile(l, t, t - 1)
                epilogue(l, T - 1)


_INS = ['x', 'src', 'dst', 'edge_type_16', 'edge_weight', 'L0_gnn_W_rel', 'L0_gnn_b_rel', 'L0_gnn_W_loop',
        'L0_gnn_W_gat', 'L0_gnn_attn_l', 'L0_gnn_attn_r', 'L0_gnn_b_gat', 'L0_gnn_W_fuse', 'L0_gnn_b_fuse',
        'L0_gnn_W_gate', 'L0_gnn_b_gate']


def kernel(**inputs):
    import numpy as _np
    import concourse.bacc as _bacc
    from concourse.bass_utils import run_bass_kernel_spmd as _run

    nc = _bacc.Bacc("TRN2", target_bir_lowering=False, num_devices=1)
    arrays, args = {}, []
    for name in _INS:
        a = _np.ascontiguousarray(inputs[name])
        arrays[f"in_{name}"] = a
        args.append(nc.dram_tensor(f"in_{name}", a.shape, mybir.dt.from_np(a.dtype), kind="ExternalInput").ap())
    out = nc.dram_tensor("out", inputs["x"].shape, F32, kind="ExternalOutput").ap()
    gnn_kernel(nc, *args, out)
    r = _run(nc, [arrays], core_ids=[0])
    return r.results[0]["out"]
```

```python
from contextlib import ExitStack

import concourse.bass as bass
from concourse import mybir

ALU = mybir.AluOpType
ACT = mybir.ActivationFunctionType
AX = mybir.AxisListType
F32 = mybir.dt.float32
BF16 = mybir.dt.bfloat16
I32 = mybir.dt.int32
U32 = mybir.dt.uint32

P = 128
PAIR = 16
BLOCK = 64
ELL = BLOCK + PAIR
NEG = -1.0e30
LEAST = -1.0e37
SLOPE = 0.2
EPS = 1e-5


def gnn_kernel(nc, x, src, dst, etype, eweight, W_rel, b_rel, W_loop, W_gat, attn_l, attn_r, b_gat,
               W_fuse, b_fuse, W_gate, b_gate, out):
    N, D = x.shape
    E = src.shape[0]
    L, R = W_rel.shape[0], W_rel.shape[1]
    H, DH = attn_l.shape[1], attn_l.shape[2]
    assert D == P and H * DH == D
    T = -(-N // P)
    NP_ = T * P
    EP = 125
    EC = E // EP
    assert EP * EC == E
    ROW = 2 * D + H
    NULL = NP_ * R
    EX = DH + 1
    M_START, M_CNT, M_ID, M_ER = 0, 1, 2, 4
    M_LOOP = M_ER + H
    M_X = M_LOOP + D
    META = M_X + D
    ZW = D + H + H + D
    HB = 25
    assert EC % (3 * HB) == 0 and T % 2 == 1
    RC = R // 4
    assert RC * D == 512
    LOWER_BY = 16 * BLOCK // 2
    LO = 64
    HI = NP_ // LO
    CLS = P
    CONSTS = 14
    ROUNDS = EC // (3 * HB)
    ER_AHEAD = T - 2 * ROUNDS
    assert ER_AHEAD == 3 and ROUNDS % 2 == 1 and T > ROUNDS + 8
    assert HI == 2 * T and T <= HB

    with ExitStack() as ctx:
        def sb(name, shape, dt=F32):
            return ctx.enter_context(nc.sbuf_tensor(name, shape, dt))

        def ps(name, shape):
            return ctx.enter_context(nc.psum_tensor(name, shape, F32))

        def sem(name):
            return ctx.enter_context(nc.semaphore(name))

        def dram(name, shape, dt=F32):
            return nc.dram_tensor(name, shape, dt).ap()

        table = [dram(f"table{i}", [NP_ * R + 1, ROW]) for i in range(2)]
        edge_rows = dram("edge_rows", [E + ELL, 1], I32)
        edge_rows_raw = dram("edge_rows_raw", [E, 1], I32)
        edge_cells = dram("edge_cells", [E, 1], I32)
        cursors = dram("cursors", [NP_, 1])
        meta_ranked = dram("meta_ranked", [NP_, META])
        tile_slots_dram = dram("tile_slots_dram", [T, 1], I32)

        ident = sb("ident", [P, P])
        ones = sb("ones", [P, P])
        upper = sb("upper", [P, P])
        lower = sb("lower", [P, P])
        shift = sb("shift", [LO, P])
        upper_bf = sb("upper_bf", [P, P], BF16)
        values = sb("values", [P, CLS, HB], BF16)
        iota_row = sb("iota_row", [P, P], BF16)
        iota_slot = sb("iota_slot", [P, ELL])
        null_row = sb("null_row", [P, ROW])
        zeros_bf = sb("zeros_bf", [P, P], BF16)
        tail_idx = sb("tail_idx", [P, ELL], I32)

        wrel = sb("wrel", [P, L, R * D])
        wz = sb("wz", [P, L, ZW])
        attn = sb("attn", [P, 2, L, D])
        attn_tmp = sb("attn_tmp", [P, D])
        wfuse = sb("wfuse", [P, 2, D])
        wgate = sb("wgate", [P, D])
        brel = sb("brel", [P, L])
        bgat = sb("bgat", [P, L])
        bfuse = sb("bfuse", [P, 1])
        bfuse_row = sb("bfuse_row", [1, D])
        bgate = sb("bgate", [P, 2])
        gate_bias = sb("gate_bias", [P, 1])
        wsum = sb("wsum", [P, 2])
        tw_mean = sb("tw_mean", [P, 1])

        meta_nat = sb("meta_nat", [P, T, META])
        meta = sb("meta", [P, T, META])
        xin = [sb(f"xin{i}", [P, D]) for i in range(4)]
        hT = [sb(f"hT{i}", [P, P]) for i in range(4)]
        rows = [sb(f"rows{i}", [P, R, ROW]) for i in range(2)]
        degree = sb("degree", [P, T])
        before = sb("before", [P, T])
        counts = sb("counts", [LO, HI])
        cls = sb("cls", [P, T], BF16)
        cls_count = sb("cls_count", [P, T])
        cls_cum = sb("cls_cum", [P, T])
        cls_above = sb("cls_above", [P, 1])
        cls_base = sb("cls_base", [P, T])
        starts = sb("starts", [P, T])
        rank = sb("rank", [P, T])
        rank_u = sb("rank_u", [P, T], U32)
        start_u = sb("start_u", [P, T], U32)
        cnt_r = sb("cnt_r", [P, T])
        id_u = sb("id_u", [P, T], U32)
        ell = sb("ell", [P, T + 2, ELL], I32)
        HUB = T + 1
        tile_slots_f = sb("tile_slots_f", [T, 1])
        tile_slots_col = sb("tile_slots_col", [T, 1], I32)
        tile_slots = sb("tile_slots", [1, T], I32)

        dst_i = sb("dst_i", [EP, EC], I32)
        dst_next = sb("dst_next", [EP, EC], I32)
        src_i = sb("src_i", [EP, EC], I32)
        typ_i = sb("typ_i", [EP, EC], I32)
        lo_bf = sb("lo_bf", [EP, EC], BF16)
        hi_bf = sb("hi_bf", [EP, EC], BF16)
        lo_i = sb("lo_i", [EP, EC], I32)
        hi_i = sb("hi_i", [EP, EC], I32)
        ew = sb("ew", [EP, EC])
        W = (LO + HI) * HB // 2
        assert (LO + HI) * HB % 2 == 0 and CLS * T % 2 == 0
        scratch = sb("scratch", [P, 3 * W])
        oh = [scratch[:, j * W:(j + 1) * W].bitcast(BF16).rearrange("p (v c) -> p v c", c=HB) for j in range(3)]
        oh_cls = scratch[:, 0:CLS * T // 2].bitcast(BF16).rearrange("p (v t) -> p v t", t=T)
        diag, picked = ([scratch[:, CLS * T // 2 + (2 * i + j) * 512:][:, 0:512].rearrange("p (t v) -> p t v", t=4)
                         for j in range(2)] for i in range(2))
        assert CLS * T // 2 + 4 * 512 <= 3 * W
        ell_valid = scratch[:, 0:T * ELL].rearrange("p (t j) -> p t j", t=T)
        sort_key = sb("sort_key", [EP, 1], U32)
        sort_val = sb("sort_val", [EP, 1], I32)
        sort_keys = sb("sort_keys", [EP, EP], U32)
        sort_cur = sb("sort_cur", [EP, 1])
        sort_pos = sb("sort_pos", [EP, 1], U32)
        sort_new = sb("sort_new", [EP, 1])
        sort_cell = sb("sort_cell", [EP, 1], U32)
        sort_f = sb("sort_f", [EP, 4])
        sort_eq = sb("sort_eq", [EP, 2, EP])
        unsorted_f = sb("unsorted_f", [P, 1])
        unsorted_i = sb("unsorted_i", [1, 1], I32)

        GROUPS = dict(A=8, B=8, t8=8, t7=7)
        PIECES = dict(t4=4, t2=2, t1=1)
        GA = ("A", "B", "t8", *PIECES)
        GK = dict(GROUPS, **PIECES)
        TAIL = GA[2:]
        room = meta_nat[:].rearrange("p t f -> p (t f)")
        slots, used = {}, 0
        slots["t8"] = scratch[:, 0:8 * ROW].rearrange("p (k f) -> p k f", k=8)
        for b in ("A", "B", "t7"):
            slots[b] = room[:, used:used + GK[b] * ROW].rearrange("p (k f) -> p k f", k=GK[b])
            used += GK[b] * ROW
        for b, first in zip(PIECES, (0, 4, 6)):
            slots[b] = slots["t7"][:, first:first + GK[b]]
        assert used <= T * META and 8 * ROW <= 3 * W
        stage_head = sb("stage_head", [P, PAIR], U32)
        stage_mid = {b: sb(f"stage_mid_{b}", [P, 8], U32) for b in "AB"}
        stage_tail = {b: sb(f"stage_{b}", [P, GK[b]], U32) for b in TAIL}
        stage_hub = {b: sb(f"stage_hub_{b}", [P, GK[b]], U32) for b in GA}
        stage_id = [sb(f"stage_id{i}", [P, 1], U32) for i in range(2)]
        blk_start = sb("blk_start", [P, 1])
        blk_left = sb("blk_left", [P, 1])
        blk_start_u = sb("blk_start_u", [P, 1], U32)
        blk_f = sb("blk_f", [P, 2, ELL])
        er_cur = sb("er_cur", [P, 1, H])
        raw = sb("raw", [P, 9, H])
        leaky = sb("leaky", [P, 9, H])
        top = sb("top", [P, 1, H])
        peak = sb("peak", [P, 1, H])
        logit = sb("logit", [P, 9, H])
        zx = sb("zx", [P, 9, H, EX])
        acc = sb("acc", [P, H, EX])
        rden = sb("rden", [P, H, 1])
        hg = sb("hg", [P, H, DH])
        hr = sb("hr", [P, D])
        hrT = sb("hrT", [P, P])
        hgT = sb("hgT", [P, P])
        hc = sb("hc", [P, P])
        th = sb("th", [P, P])
        y = sb("y", [P, D])
        yo = [sb(f"yo{i}", [P, D]) for i in range(2)]
        stats = sb("stats", [P, 6])
        mv = sb("mv", [P, 2])
        ve = sb("ve", [P, 1])
        nv = sb("newton", [P, 2])
        nv_i = sb("newton_i", [P, 1], I32)

        ps_rel = ps("ps_rel", [P, 512])
        ps_gat = ps("ps_gat", [P, 512])
        ps_mix = ps("ps_mix", [P, 512])
        ps_z = ps("ps_z", [P, 512])
        ps_tab = [ps(f"ps_tab{i}", [P, 512]) for i in range(2)]
        ps_cnt = ps("ps_cnt", [P, 512])
        ps_xT = [ps_rel[:, 0:P]] * 2 + [ps_mix[:, 0:P]] * 2
        mix = [ps_mix[:, 128 * i:128 * i + 128] for i in range(4)]

        s_const = sem("const_ready")
        s_wload = sem("weights_loaded")
        s_wrload = sem("first_relation_weights_loaded")
        s_bload = sem("biases_loaded")
        s_dload = sem("dst_loaded")
        s_eload = sem("edges_loaded")
        s_ewload = sem("edge_weights_loaded")
        s_xload = sem("x_loaded_to_meta")
        s_xin = [sem(f"xin{i}_loaded") for i in range(4)]
        s_xin_used = [sem(f"xin{i}_used") for i in range(4)]
        s_xT_ps = sem("xT_in_psum")
        s_hT = [sem(f"hT{i}_ready") for i in range(4)]
        s_er_ps = sem("er_product_ready")
        s_er = sem("er_and_loop_of_natural_tile_ready")
        s_z_ps = sem("z_product_ready")
        s_chunk = [sem(f"table_chunk{c}_ready") for c in range(4)]
        s_bank = [sem(f"bank_free_for_chunk{c}") for c in range(4)]
        s_rows = sem("rows_ready")
        s_half = sem("first_half_of_rows_ready")
        s_saved = [[sem(f"rows{i}_half{j}_saved") for j in range(2)] for i in range(2)]
        s_v = sem("vector_step")
        s_uns_in = sem("order_violations_ready")
        s_fold = sem("attention_fold_step")
        s_wz = sem("wz_ready")
        s_tws = sem("edge_weight_sums_ready")
        s_gbias = sem("gate_bias_ready")
        s_edge_rows = sem("edge_rows_computed")
        s_edge_saved = sem("edge_rows_saved")
        s_oh = [sem(f"onehots{i}_ready") for i in range(3)]
        s_oh_used = [sem(f"onehots{i}_used") for i in range(3)]
        s_hist = sem("histogram_ready")
        s_deg = sem("degrees_ready")
        s_start_ps = sem("starts_and_totals_ready")
        s_cnt = sem("histogram_copied")
        s_deg_nat = sem("degrees_by_node_in_psum")
        s_cls = sem("class_onehots_ready")
        s_cls_ps = sem("class_counts_in_psum")
        s_cls_cum = sem("class_counts_summed")
        s_above_ps = sem("higher_classes_in_psum")
        s_diag = sem("diagonals_ready")
        s_place_ps = sem("places_in_psum")
        s_picked = sem("own_class_picked")
        s_rank = sem("ranks_ready")
        s_scatter = sem("meta_scattered")
        s_meta_head = sem("ranked_starts_degrees_ids_loaded")
        s_deg_ps = sem("degrees_by_tile_in_psum")
        s_meta = sem("ranked_meta_loaded")
        s_meta_cols = sem("ranked_columns_ready")
        s_slots_col = sem("tile_slots_computed")
        s_slots_saved = sem("tile_slots_saved")
        s_slots = sem("tile_slots_loaded")
        s_ell = sem("ell_gathered")
        s_ell_ok = sem("ell_ready")
        s_stored = sem("rows_stored")
        s_uns = sem("order_flag_ready")
        s_cur = sem("cursors_saved")
        s_sort_ld = sem("sort_chunk_loaded")
        s_sort_cur = sem("sort_cursors_gathered")
        s_sort_v = sem("sort_positions_ready")
        s_sort_c = sem("sort_vector_step")
        s_sort_st = sem("sort_chunk_stored")
        s_copy = sem("raw_edge_rows_copied")
        s_head = sem("first_pair_staged")
        s_mid = {b: sem(f"next_{b}_staged") for b in "AB"}
        s_tail = sem("tail_staged")
        s_staged = sem("hub_indices_staged")
        s_blk = sem("block_step")
        s_landed = {b: sem(f"slots_{b}_landed") for b in GA[:2]}
        s_blk_ld = sem("block_fetched")
        s_landed |= {b: sem(f"slots_{b}_landed") for b in GA[2:]}
        s_lowered = sem("landed_counts_lowered")
        s_free = {b: sem(f"slots_{b}_free") for b in GROUPS}
        s_tile = sem("tile_started")
        s_raw = sem("raw_logits_ready")
        s_top = sem("running_top_ready")
        s_leaky = sem("leaky_ready")
        s_peak = sem("peak_ready")
        s_keep = sem("top_kept")
        s_logit = sem("logits_ready")
        s_wgt = sem("weights_ready")
        s_zx = sem("weighted_z_ready")
        s_scaled = sem("sums_rescaled")
        s_gat = sem("group_sum_ready")
        s_acc = sem("sums_updated")
        s_rden = sem("denominators_inverted")
        s_h2 = sem("node_sums_ready")
        s_T_ps = sem("node_sums_transposed")
        s_T = sem("transposed_sums_ready")
        s_fuse = sem("fused_in_psum")
        s_hc = sem("fused_ready")
        s_gate_ps = sem("gate_in_psum")
        s_th = sem("gate_ready")
        s_id = sem("ids_staged")
        s_norm = sem("norm_step")
        s_gated = sem("gating_step")
        s_yo = sem("normed_ready")
        s_out = sem("output_saved")

        def bc(ap, n):
            return ap.rearrange("p (o f) -> p o f", o=1).to_broadcast([ap.shape[0], n, ap.shape[1]])

        def bc_last(ap, n):
            return ap.rearrange("p (f o) -> p f o", o=1).to_broadcast([ap.shape[0], ap.shape[1], n])

        def counter(eng, name, value):
            reg = eng.alloc_register(name)
            eng.reg_mov(reg, value)
            return reg

        def pair_loops(eng, first, pairs, in_first, n_lowered, n_land, pair):
            with eng.If(in_first > first):
                with eng.Fori(first, in_first):
                    pair(hub=False)
            with eng.If(pairs > BLOCK // PAIR):
                left = counter(eng, f"left_{nc.next_id()}", 0)
                blocks = counter(eng, f"blocks_{nc.next_id()}", 0)
                now = counter(eng, f"now_{nc.next_id()}", 0)
                low = counter(eng, f"low_{nc.next_id()}", 0)
                eng.reg_sub(left, pairs, BLOCK // PAIR)
                eng.reg_sub(blocks, pairs, 1)
                eng.reg_alu(blocks, blocks, (BLOCK // PAIR).bit_length() - 1, ALU.logical_shift_right)
                with eng.Fori(0, eng.snap(blocks, min_val=1, max_val=E // BLOCK)):
                    eng.wait_ge(s_lowered, n_lowered)
                    eng.reg_add(n_lowered, n_lowered, 1)
                    for b in ("A", "B"):
                        eng.reg_sub(low, n_land[b], LOWER_BY)
                        eng.reg_alu(n_land[b], low, 16 * GK[b], ALU.max)
                    eng.reg_alu(now, left, BLOCK // PAIR, ALU.min)
                    eng.reg_sub(left, left, now)
                    with eng.Fori(0, eng.snap(now, min_val=1, max_val=BLOCK // PAIR)):
                        pair(hub=True)

        def load_slots(eng, t):
            n = eng.value_load(tile_slots[0:1, bass.ds(t, 1)], min_val=PAIR, max_val=E)
            pairs = counter(eng, f"pairs_{nc.next_id()}", 0)
            in_first = counter(eng, f"in_first_{nc.next_id()}", 0)
            eng.reg_alu(pairs, n, PAIR.bit_length() - 1, ALU.logical_shift_right)
            eng.reg_alu(in_first, pairs, BLOCK // PAIR, ALU.min)
            return n, eng.snap(pairs, min_val=1, max_val=E // PAIR), eng.snap(in_first, min_val=1, max_val=BLOCK // PAIR)

        def tail_groups(eng, n, group):
            for b, mask in (("t8", 8), ("t7", 7)):
                has = counter(eng, f"has_{nc.next_id()}", 0)
                eng.reg_alu(has, n, mask, ALU.bitwise_and)
                with eng.If(eng.snap(has, min_val=0, max_val=mask) > 0):
                    group(b)

        def pieces(eng, n, run):
            for b, K in PIECES.items():
                has = counter(eng, f"has_{nc.next_id()}", 0)
                eng.reg_alu(has, n, K, ALU.bitwise_and)
                with eng.If(eng.snap(has, min_val=0, max_val=K) > 0):
                    run(b)

        block = ctx.enter_context(nc.Block())

        @block.sync
        def _(sp):
            sp.dma_start(dst_i[:], dst.rearrange("(p c) -> p c", p=EP)).then_inc(s_dload, 16)
            for k, i in enumerate((0, 1, 0, 1)):
                sp.dma_start(xin[k][:], x[i * P:(i + 1) * P, :]).then_inc(s_xin[k], 16)
            sp.dma_start(wz[:, :, 0:D], W_gat.rearrange("l d o -> d l o")).then_inc(s_wload, 16)
            sp.dma_start(wz[:, :, D + 2 * H:ZW], W_loop.rearrange("l d o -> d l o")).then_inc(s_wload, 16)
            for i, a in enumerate((attn_l, attn_r)):
                sp.dma_start(attn[:, i].rearrange("p l d -> p (l d)"),
                             a.rearrange("(o l) h c -> o (l h c)", o=1).to_broadcast([P, L * D])
                             ).then_inc(s_wload, 16)
            sp.dma_start(wrel[:, 0].rearrange("p (r o) -> p r o", r=R), W_rel[0].rearrange("r d o -> d r o")
                         ).then_inc(s_wrload, 16)
            sp.dma_start(src_i[:], src.rearrange("(p c) -> p c", p=EP)).then_inc(s_eload, 16)
            sp.dma_start(typ_i[:], etype.rearrange("(p c) -> p c", p=EP)).then_inc(s_eload, 16)
            sp.dma_start(dst_next[0:EP - 1, :], dst[1:1 + (EP - 1) * EC].rearrange("(p c) -> p c", p=EP - 1)
                         ).then_inc(s_eload, 16)
            sp.dma_start(dst_next[EP - 1:EP, 0:EC - 1],
                         dst[(EP - 1) * EC + 1:E].rearrange("(p c) -> p c", p=1)).then_inc(s_eload, 16)
            sp.dma_start(dst_next[EP - 1:EP, EC - 1:EC],
                         dst[E - 1:E].rearrange("(p c) -> p c", p=1)).then_inc(s_eload, 16)
            sp.dma_start(ew[:], eweight.rearrange("(p c) -> p c", p=EP)).then_inc(s_ewload, 16)
            n_used = [counter(sp, f"sp_used{k}", 0) for k in range(4)]
            n_rows = counter(sp, "sp_rows", 0)
            n_both = counter(sp, "sp_both", 1)
            half = R * ROW // 2

            def load_tile(t, k):
                sp.reg_add(n_used[k], n_used[k], 1)
                sp.wait_ge(s_xin_used[k], n_used[k])
                if isinstance(t, int) and t == T - 1:
                    sp.dma_start(xin[k][0:N - t * P, :], x[t * P:N, :]).then_inc(s_xin[k], 16)
                else:
                    sp.dma_start(xin[k][:], x[bass.ds(t * P, P), :]).then_inc(s_xin[k], 16)

            def save_rows(t, k):
                to = table[0][bass.ds(t * (P * R), P * R), :].rearrange("(p r) f -> p (r f)", r=R)
                rows_k = rows[k][:].rearrange("p r f -> p (r f)")
                sp.reg_add(n_rows, n_rows, 1)
                sp.wait_ge(s_half, n_rows)
                sp.dma_start(to[:, 0:half], rows_k[:, 0:half]).then_inc(s_saved[k][0], 16)
                sp.reg_add(n_both, n_rows, 1)
                sp.wait_ge(s_rows, n_both)
                sp.dma_start(to[:, half:2 * half], rows_k[:, half:2 * half]).then_inc(s_saved[k][1], 16)

            def table_turn(t, k):
                if not (isinstance(t, int) and t >= T - 2):
                    load_tile(t + 2, 2 + k)
                save_rows(t, k)

            def round_(i, k):
                if not (isinstance(i, int) and i == ROUNDS - 1):
                    load_tile(2 * i + ER_AHEAD + 2, 1)
                    load_tile(2 * i + ER_AHEAD + 3, 0)
                table_turn(i, k)

            for t in range(2, ER_AHEAD + 2):
                load_tile(t, t % 2)
            with sp.Fori(0, (ROUNDS - 3) // 2) as i:
                round_(2 * i, 0)
                round_(2 * i + 1, 1)
            sp.dma_start(wfuse[:], W_fuse.rearrange("(k d) o -> d k o", k=2)).then_inc(s_bload, 16)
            sp.dma_start(wgate[:], W_gate[0:D, :]).then_inc(s_bload, 16)
            for l in range(L):
                sp.dma_start(brel[:, l:l + 1], b_rel[l].rearrange("(p o) -> p o", o=1)).then_inc(s_bload, 16)
                sp.dma_start(bgat[:, l:l + 1], b_gat[l].rearrange("(p o) -> p o", o=1)).then_inc(s_bload, 16)
            sp.dma_start(bfuse[:], b_fuse.rearrange("(p o) -> p o", o=1)).then_inc(s_bload, 16)
            sp.dma_start(bfuse_row[:], b_fuse.rearrange("(o p) -> o p", o=1)).then_inc(s_bload, 16)
            sp.dma_start(bgate[:, 0:1], b_gate.rearrange("(p o) -> p o", o=1)).then_inc(s_bload, 16)
            sp.dma_start(bgate[:, 1:2], W_gate[D].rearrange("(p o) -> p o", o=1)).then_inc(s_bload, 16)
            for l in range(1, L):
                sp.dma_start(wrel[:, l].rearrange("p (r o) -> p r o", r=R), W_rel[l].rearrange("r d o -> d r o")
                             ).then_inc(s_bload, 16)
            sp.wait_ge(s_const, 2)
            sp.dma_start(meta_nat[:, 0:T - 1, M_X:META], x[0:(T - 1) * P, :].rearrange("(t p) d -> p t d", p=P)
                         ).then_inc(s_xload, 16)
            sp.dma_start(meta_nat[0:N - (T - 1) * P, T - 1, M_X:META], x[(T - 1) * P:N, :]).then_inc(s_xload, 16)
            for i in range(ROUNDS - 3, ROUNDS):
                round_(i, i % 2)
            with sp.Fori(0, (T - 4 - ROUNDS) // 2) as i:
                table_turn(2 * i + ROUNDS, 1)
                table_turn(2 * i + ROUNDS + 1, 0)
            for t in range(T - 4, T):
                table_turn(t, t % 2)

        @block.gpsimd
        def _(pool):
            g = nc.gpsimd
            g.memset(meta_nat[:, T - 1, :], 0.0).then_inc(s_const, 1)
            g.memset(ones[:], 1.0).then_inc(s_const, 1)
            pool.wait_ge(s_const, 2)
            g.affine_select(out=ident[:], in_=ones[:], pattern=[[-1, P]], compare_op=ALU.is_equal, fill=0.0,
                            base=0, channel_multiplier=1).then_inc(s_const, 1)
            g.affine_select(out=upper[:], in_=ones[:], pattern=[[1, P]], compare_op=ALU.is_gt, fill=0.0,
                            base=0, channel_multiplier=-1).then_inc(s_const, 1)
            g.affine_select(out=lower[:], in_=ones[:], pattern=[[-1, P]], compare_op=ALU.is_gt, fill=0.0,
                            base=0, channel_multiplier=1).then_inc(s_const, 1)
            g.affine_select(out=shift[:], in_=ones[0:LO, :], pattern=[[-1, P]], compare_op=ALU.is_equal, fill=0.0,
                            base=LO, channel_multiplier=1).then_inc(s_const, 1)
            g.iota(iota_row[:], [[1, P]], base=0, channel_multiplier=0,
                   allow_small_or_imprecise_dtypes=True).then_inc(s_const, 1)
            g.iota(iota_slot[:], [[1, ELL]], base=0, channel_multiplier=0,
                   allow_small_or_imprecise_dtypes=True).then_inc(s_const, 1)
            g.memset(zeros_bf[:], 0.0).then_inc(s_const, 1)
            g.memset(tail_idx[:], 0).then_inc(s_const, 1)
            g.memset(null_row[:, 0:2 * D], 0.0).then_inc(s_const, 1)
            g.memset(null_row[:, 2 * D:ROW], NEG).then_inc(s_const, 1)
            g.iota(meta_nat[:, :, M_ID], [[P, T]], base=0, channel_multiplier=1,
                   allow_small_or_imprecise_dtypes=True).then_inc(s_const, 1)
            g.memset(meta_nat[:, 0:T - 1, 3], 0.0).then_inc(s_const, 1)
            pool.wait_ge(s_const, CONSTS)
            pool.dma_start(table[0][NULL:NULL + 1, :], null_row[0:1, :]).then_inc(s_stored, 16)
            pool.dma_start(table[1][NULL:NULL + 1, :], null_row[0:1, :]).then_inc(s_out, 16)
            pool.dma_start(edge_rows[E:E + ELL, :].rearrange("(o c) k -> o (c k)", o=1), tail_idx[0:1, :]
                           ).then_inc(s_edge_saved, 16)
            pool.wait_ge(s_edge_rows, 1)
            pool.dma_start(edge_rows[0:E, :].rearrange("(p c) o -> p (c o)", p=EP), src_i[:]
                           ).then_inc(s_edge_saved, 16)
            pool.wait_ge(s_uns, 1)
            pool.wait_ge(s_edge_saved, 32)
            bad = pool.value_load(unsorted_i[0:1, 0:1], min_val=0, max_val=1)
            with pool.If(bad > 0):
                pool.wait_ge(s_edge_rows, 2)
                pool.dma_start(edge_cells[:].rearrange("(p c) o -> p (c o)", p=EP), typ_i[:]
                               ).then_inc(s_edge_saved, 16)
                pool.wait_ge(s_edge_saved, 48)
                pool.dma_start(cursors[:].rearrange("(p t) o -> p (t o)", t=T), starts[:]).then_inc(s_cur, 16)
                pool.wait_ge(s_cur, 16)
                pool.dma_start(edge_rows_raw[:].rearrange("(p c) o -> p (c o)", p=EP),
                               edge_rows[0:E, :].rearrange("(p c) o -> p (c o)", p=EP)).then_inc(s_copy, 16)
                pool.wait_ge(s_copy, 16)
                n_ld, n_v, n_st = (counter(pool, f"pool_sort{i}", v) for i, v in enumerate((48, 1, 32)))
                n_cur = counter(pool, "pool_sort3", 16)
                with pool.Fori(0, EC) as c:
                    at = c * EP
                    pool.dma_start(sort_key[:], edge_cells[bass.ds(at, EP), :].bitcast(U32)).then_inc(s_sort_ld, 16)
                    pool.dma_start(sort_val[:], edge_rows_raw[bass.ds(at, EP), :]).then_inc(s_sort_ld, 16)
                    pool.dma_start(sort_keys[:], edge_cells[bass.ds(at, EP), :].bitcast(U32).rearrange("c o -> o c")
                                   .to_broadcast([EP, EP])).then_inc(s_sort_ld, 16)
                    pool.wait_ge(s_sort_ld, n_ld)
                    pool.reg_add(n_ld, n_ld, 48)
                    pool.indirect_dma_start(
                        out=sort_cur[:], out_offset=None, in_=cursors[:],
                        in_offset=bass.IndirectOffsetOnAxis(ap=sort_key[:], axis=0)
                    ).then_inc(s_sort_cur, 16)
                    pool.wait_ge(s_sort_cur, n_cur)
                    pool.reg_add(n_cur, n_cur, 16)
                    pool.wait_ge(s_sort_v, n_v)
                    pool.reg_add(n_v, n_v, 1)
                    pool.indirect_dma_start(
                        out=edge_rows[:], out_offset=bass.IndirectOffsetOnAxis(ap=sort_pos[:], axis=0),
                        in_=sort_val[:], in_offset=None).then_inc(s_sort_st, 16)
                    pool.indirect_dma_start(
                        out=cursors[:], out_offset=bass.IndirectOffsetOnAxis(ap=sort_cell[:], axis=0),
                        in_=sort_new[:], in_offset=None, bounds_check=NP_ - 1, oob_is_err=False
                    ).then_inc(s_sort_st, 16)
                    pool.wait_ge(s_sort_st, n_st)
                    pool.reg_add(n_st, n_st, 32)
            pool.wait_ge(s_rank, 1)
            pool.wait_ge(s_er, T + 1)
            pool.wait_ge(s_xload, 32)
            for t in range(T):
                pool.indirect_dma_start(
                    out=meta_ranked[:], out_offset=bass.IndirectOffsetOnAxis(ap=rank_u[:, t:t + 1], axis=0),
                    in_=meta_nat[:, t, :], in_offset=None).then_inc(s_scatter, 16)
            pool.wait_ge(s_scatter, 16 * T)
            by_rank = meta_ranked[:].rearrange("(t p) f -> p t f", p=P)
            pool.dma_start(meta[:, :, 0:M_ER], by_rank[:, :, 0:M_ER]).then_inc(s_meta_head, 16)
            pool.dma_start(meta[:, :, M_ER:META], by_rank[:, :, M_ER:META]).then_inc(s_meta, 16)
            pool.wait_ge(s_meta_cols, 3)
            for t in range(T):
                pool.indirect_dma_start(
                    out=ell[:, t, :], out_offset=None, in_=edge_rows[:],
                    in_offset=bass.IndirectOffsetOnAxis(ap=start_u[:, t:t + 1], axis=0)).then_inc(s_ell, 16)
            pool.wait_ge(s_slots_col, 1)
            pool.dma_start(tile_slots_dram[:], tile_slots_col[:]).then_inc(s_slots_saved, 16)
            pool.wait_ge(s_slots_saved, 16)
            pool.dma_start(tile_slots[:], tile_slots_dram[:].rearrange("t o -> o t")).then_inc(s_slots, 16)
            pool.wait_ge(s_slots, 16)

            pool.wait_ge(s_ell_ok, 1)
            pool.wait_ge(s_stored, 16)
            pool.wait_ge(s_out, 16)
            n_staged = counter(pool, "pool_staged", 1)
            n_blk = counter(pool, "pool_blk", 1)
            n_stored_pool = counter(pool, "pool_stored", 16)
            n_out_pool = counter(pool, "pool_out", 16)
            n_free = {b: counter(pool, f"pool_free_{b}", 1) for b in GROUPS}
            n_epi = counter(pool, "pool_epi", 1)
            at = counter(pool, "pool_at", 0)
            at_now = counter(pool, "pool_at_now", 0)
            left = counter(pool, "pool_left", 0)
            ell_flat = ell[:].rearrange("p t j -> p (t j)")

            def free(b):
                pool.wait_ge(s_free[b], n_free[b])
                pool.reg_add(n_free[b], n_free[b], 1)

            def gather(l, b, indices):
                for k in range(GK[b]):
                    pool.indirect_dma_start(
                        out=slots[b][:, k, :], out_offset=None, in_=table[l % 2],
                        in_offset=bass.IndirectOffsetOnAxis(ap=indices[:, k:k + 1], axis=0)
                    ).then_inc(s_landed[b], 16)

            def gather_hub(l, b):
                K = GK[b]
                pool.reg_add(at_now, at, 0)
                here = pool.snap(at_now, min_val=0, max_val=(HUB + 1) * ELL - K)
                g.tensor_copy(stage_hub[b][:].bitcast(I32), ell_flat[:, bass.ds(here, K)]).then_inc(s_staged, 1)
                pool.reg_add(at, at, K)
                pool.wait_ge(s_staged, n_staged)
                pool.reg_add(n_staged, n_staged, 1)
                gather(l, b, stage_hub[b])

            def next_block(t, first):
                def done():
                    pool.wait_ge(s_blk, n_blk)
                    pool.reg_add(n_blk, n_blk, 1)

                with pool.If(first):
                    g.tensor_copy(blk_start[:], meta[:, bass.ds(t, 1), M_START]).then_inc(s_blk, 1)
                    done()
                    g.tensor_copy(blk_left[:], meta[:, bass.ds(t, 1), M_CNT]).then_inc(s_blk, 1)
                    done()
                g.tensor_scalar(blk_start[:], blk_start[:], float(BLOCK), float(E), ALU.add, ALU.min
                                ).then_inc(s_blk, 1)
                done()
                g.tensor_scalar(blk_left[:], blk_left[:], -float(BLOCK), None, ALU.add).then_inc(s_blk, 1)
                done()
                g.tensor_copy(blk_start_u[:], blk_start[:]).then_inc(s_blk, 1)
                done()
                pool.indirect_dma_start(
                    out=ell[:, HUB, :], out_offset=None, in_=edge_rows[:],
                    in_offset=bass.IndirectOffsetOnAxis(ap=blk_start_u[:], axis=0)).then_inc(s_blk_ld, 16)
                pool.wait_ge(s_blk_ld, 16)
                pool.wait_ge(s_free["A"], n_free["A"])
                pool.wait_ge(s_free["B"], n_free["B"])
                pool.wait_ge(s_stored, n_stored_pool)
                pool.wait_ge(s_out, n_out_pool)
                pool.inc_swdge_sem([s_landed["A"], s_landed["B"], s_blk_ld], [LOWER_BY, LOWER_BY, 16], mode="sub")
                pool.sem_inc(s_lowered, 1)
                g.tensor_scalar(blk_f[:, 0], iota_slot[:], blk_left[:], None, ALU.is_lt).then_inc(s_blk, 1)
                done()
                g.tensor_scalar(blk_f[:, 1], ell[:, HUB, :], -float(NULL), None, ALU.add).then_inc(s_blk, 1)
                done()
                g.tensor_tensor(blk_f[:, 0], blk_f[:, 0], blk_f[:, 1], ALU.mult).then_inc(s_blk, 1)
                done()
                g.tensor_scalar(ell[:, HUB, :], blk_f[:, 0], float(NULL), None, ALU.add).then_inc(s_blk, 1)
                done()

            def store_tile(l, last):
                if l < L - 1:
                    pool.wait_ge(s_rows, n_rows_pool)
                    pool.reg_add(n_rows_pool, n_rows_pool, 1)
                else:
                    pool.wait_ge(s_yo, T if last else n_yo)
                    pool.reg_add(n_yo, n_yo, 1)
                pool.wait_ge(s_id, n_epi)
                pool.reg_add(n_epi, n_epi, 1)
                if l < L - 1:
                    pool.indirect_dma_start(
                        out=table[(l + 1) % 2][0:NP_ * R, :].rearrange("(n r) f -> n (r f)", r=R),
                        out_offset=bass.IndirectOffsetOnAxis(ap=stage_id[last][:], axis=0),
                        in_=rows[last][:].rearrange("p r f -> p (r f)"), in_offset=None).then_inc(s_stored, 16)
                    pool.reg_add(n_stored_pool, n_stored_pool, 16)
                else:
                    pool.indirect_dma_start(
                        out=out, out_offset=bass.IndirectOffsetOnAxis(ap=stage_id[last][:], axis=0),
                        in_=yo[last][:], in_offset=None, bounds_check=N - 1, oob_is_err=False).then_inc(s_out, 16)
                    pool.reg_add(n_out_pool, n_out_pool, 16)

            n_rows_pool = counter(pool, "pool_rows", T + 2)
            n_yo = counter(pool, "pool_yo", 1)

            def tile(l, t):
                n, pairs, in_first = load_slots(pool, t)
                pool.wait_ge(s_head, n_head)
                pool.reg_add(n_head, n_head, 1)
                free("A")
                gather(l, "A", stage_head[:, 0:8])
                if not isinstance(t, int):
                    with pool.If(t > 1):
                        store_tile(l, last=False)
                free("B")
                gather(l, "B", stage_head[:, 8:16])
                with pool.If(in_first > 1):
                    with pool.Fori(1, in_first):
                        for b in ("A", "B"):
                            pool.wait_ge(s_mid[b], n_mid[b])
                            pool.reg_add(n_mid[b], n_mid[b], 1)
                            free(b)
                            gather(l, b, stage_mid[b])
                for b in ("A", "B"):
                    pool.reg_add(n_mid[b], n_mid[b], 1)
                with pool.If(pairs > BLOCK // PAIR):
                    now = counter(pool, f"pool_now{nc.next_id()}", 0)
                    blocks = counter(pool, f"pool_blocks{nc.next_id()}", 0)
                    pool.reg_sub(left, pairs, BLOCK // PAIR)
                    pool.reg_sub(blocks, pairs, 1)
                    pool.reg_alu(blocks, blocks, (BLOCK // PAIR).bit_length() - 1, ALU.logical_shift_right)
                    with pool.Fori(0, pool.snap(blocks, min_val=1, max_val=E // BLOCK)) as b:
                        next_block(t, b < 1)
                        pool.reg_mov(at, HUB * ELL)
                        pool.reg_alu(now, left, BLOCK // PAIR, ALU.min)
                        pool.reg_sub(left, left, now)
                        with pool.Fori(0, pool.snap(now, min_val=1, max_val=BLOCK // PAIR)):
                            for b in ("A", "B"):
                                free(b)
                                gather_hub(l, b)
                pool.wait_ge(s_tail, n_tail)
                pool.reg_add(n_tail, n_tail, 1)
                for is_hub, run in ((pairs > BLOCK // PAIR, lambda b: gather_hub(l, b)),
                                    (pairs <= BLOCK // PAIR, lambda b: gather(l, b, stage_tail[b]))):
                    with pool.If(is_hub):
                        tail_groups(pool, n, lambda b: (free(b), pieces(pool, n, run) if b == "t7" else run(b)))

            n_head = counter(pool, "pool_head", 1)
            n_mid = {b: counter(pool, f"pool_mid_{b}", 2) for b in "AB"}
            n_tail = counter(pool, "pool_tail", 2)

            for l in range(L):
                if l == 0:
                    for k, j in ((0, 0), (0, 1), (1, 0), (1, 1)):
                        pool.wait_ge(s_saved[k][j], 16 * (T // 2 + 2 - k))
                else:
                    pool.wait_ge(s_stored, 16 * (1 + l * T))
                tile(l, 0)
                with pool.Fori(1, T) as t:
                    tile(l, t)
                store_tile(l, last=False)
                store_tile(l, last=True)
            pool.wait_ge(s_out, 16 * (1 + T))

        @block.scalar
        def _(act):
            s = nc.scalar
            n_tab = counter(act, "act_tab", 1)
            n_saved = [counter(act, f"act_saved{k}", 16) for k in range(2)]

            def evacuate_chunk(k, c):
                act.wait_ge(s_chunk[c], n_tab)
                s.activation(rows[k][:, c * RC:(c + 1) * RC, 0:D],
                             ps_tab[c % 2][:].rearrange("p (r f) -> p r f", r=RC), ACT.Copy
                             ).then_inc(s_bank[(c + 2) % 4], 1)

            def evacuate_rest(k, meta_col):
                for c in range(2, 4):
                    evacuate_chunk(k, c)
                s.activation(meta_col, ps_z[:, D + H:ZW].rearrange("p (o f) -> p o f", o=1), ACT.Copy
                             ).then_inc(s_rows, 1)
                act.reg_add(n_tab, n_tab, 1)

            act.sem_inc(s_bank[0], 1)
            act.sem_inc(s_bank[1], 1)
            act.sem_inc(s_rows, 1)
            act.sem_inc(s_er, 1)
            n_xT = counter(act, "act_xT", 1)
            n_er = counter(act, "act_er", 1)

            def transposed_x(k):
                act.wait_ge(s_xT_ps, n_xT)
                s.activation(hT[k][:], ps_xT[k], ACT.Copy).then_inc(s_hT[k], 1)
                act.reg_add(n_xT, n_xT, 1)

            def natural_er(t, k):
                transposed_x(k)
                act.wait_ge(s_er_ps, n_er)
                s.activation(meta_nat[:, bass.ds(t, 1), M_ER:M_X],
                             ps_gat[:, 0:H + D].rearrange("p (o f) -> p o f", o=1), ACT.Copy).then_inc(s_er, 1)
                act.reg_add(n_er, n_er, 1)

            def natural_rows(k, next_x=False):
                for j in range(2):
                    if j == 1 and next_x:
                        transposed_x(3 - k)
                    act.wait_ge(s_saved[k][j], n_saved[k])
                    for c in (2 * j, 2 * j + 1):
                        evacuate_chunk(k, c)
                    if j == 0:
                        act.wait_ge(s_z_ps, n_tab)
                    s.activation(rows[k][:, j * R // 2:(j + 1) * R // 2, D:ROW], bc(ps_z[:, 0:D + H], R // 2),
                                 ACT.Copy).then_inc((s_half, s_rows)[j], 1)
                act.reg_add(n_saved[k], n_saved[k], 16)
                act.reg_add(n_tab, n_tab, 1)

            def round_(i, k):
                natural_er(2 * i + ER_AHEAD, 1)
                transposed_x(2 + k)
                natural_er(2 * i + ER_AHEAD + 1, 0)
                natural_rows(k)

            for k in range(2):
                for j in range(2):
                    act.sem_inc(s_saved[k][j], 16)
            act.wait_ge(s_const, CONSTS)
            for t in range(ER_AHEAD):
                natural_er(t, t % 2)
            with act.Fori(0, (ROUNDS - 1) // 2) as i:
                round_(2 * i, 0)
                round_(2 * i + 1, 1)
            round_(ROUNDS - 1, 0)
            transposed_x(3)
            with act.Fori(0, (T - ROUNDS - 2) // 2):
                natural_rows(1, next_x=True)
                natural_rows(0, next_x=True)
            natural_rows(1, next_x=True)
            natural_rows(0)

            n_g = counter(act, "act_group", 1)
            n_e = counter(act, "act_epi", 1)

            def group(K):
                act.wait_ge(s_logit, n_g)
                s.activation(zx[:, 8 - K:9, :, DH], logit[:, 8 - K:9, :], ACT.Exp).then_inc(s_wgt, 1)
                act.reg_add(n_g, n_g, 1)

            def transposed(l):
                act.wait_ge(s_T_ps, n_e)
                s.activation(hrT[:], mix[0], ACT.Identity, bias=brel[:, l:l + 1])
                s.activation(hgT[:], mix[1], ACT.Identity, bias=bgat[:, l:l + 1]).then_inc(s_T, 1)

            def fused(l):
                if l < L - 1:
                    act.wait_ge(s_fuse, n_e)
                if l == 0:
                    s.activation(hc[:], mix[2], ACT.Identity, bias=bfuse[:]).then_inc(s_hc, 1)
                elif l < L - 1:
                    s.activation(hT[0][:], mix[2], ACT.Relu, bias=bfuse[:]).then_inc(s_hT[0], 1)

            def gate_and_half_table(l, last=False):
                if l == 0:
                    act.wait_ge(s_gate_ps, n_e0)
                    s.activation(th[:], mix[3], ACT.Tanh, bias=gate_bias[:], scale=0.5).then_inc(s_th, 1)
                    act.reg_add(n_e0, n_e0, 1)
                if l < L - 1:
                    if not last:
                        act.wait_ge(s_stored, n_stored)
                    act.reg_add(n_stored, n_stored, 16)
                    act.wait_ge(s_z_ps, n_tab)
                    s.activation(rows[last][:, :, D:ROW], bc(ps_z[:, 0:D + H], R), ACT.Copy)
                    for c in range(2):
                        evacuate_chunk(last, c)
                act.reg_add(n_e, n_e, 1)

            def rest_of_table(l, t, last=False):
                if l < L - 1:
                    evacuate_rest(last, meta[:, bass.ds(t, 1), M_ER:M_X])

            n_e0 = counter(act, "act_epi0", 1)
            n_stored = counter(act, "act_stored", 16)

            def tile(l, t, previous):
                n, pairs, _ = load_slots(act, t)
                group(8)
                if previous is not None:
                    transposed(l)
                    fused(l)
                group(8)
                split = previous is not None and l < L - 1
                if previous is not None:
                    gate_and_half_table(l)
                if split:
                    with act.If(pairs > 1):
                        group(8)
                    rest_of_table(l, previous)
                    with act.If(pairs > 1):
                        group(8)
                first = 2 if split else 1
                with act.If(pairs > first):
                    with act.Fori(first, pairs):
                        group(8)
                        group(8)
                tail_groups(act, n, lambda b: group(GK[b]))

            act.wait_ge(s_bload, 16 * (5 + 3 * L))
            act.wait_ge(s_slots, 16)
            act.wait_ge(s_gbias, 1)
            for k in range(2):
                for j in range(2):
                    act.wait_ge(s_saved[k][j], 16 * (T // 2 + 2 - k))
            act.wait_ge(s_meta, 16)
            for l in range(L):
                tile(l, 0, None)
                with act.Fori(1, T) as t:
                    tile(l, t, t - 1)
                transposed(l)
                fused(l)
                gate_and_half_table(l, last=True)
                rest_of_table(l, T - 1, last=True)

        @block.tensor
        def _(pe):
            n_tab = counter(pe, "pe_tab", 1)

            def z_product(l, k, width):
                pe.wait_ge(s_rows, n_tab)
                pe.matmul(ps_z[:, 0:width], hT[k][:], wz[:, l, 0:width], start=True, stop=True).then_inc(s_z_ps, 1)

            def table_products(l, k, hT_count, width=ZW, mid=None, chunks=range(4)):
                if chunks[0] == 0:
                    pe.wait_ge(s_hT[k], hT_count)
                    if l:
                        z_product(l, k, width)
                for c in chunks:
                    pe.wait_ge(s_bank[c], n_tab)
                    pe.matmul(ps_tab[c % 2][:], hT[k][:], wrel[:, l, c * RC * D:(c + 1) * RC * D],
                              start=True, stop=True).then_inc(s_chunk[c], 1)
                    if c == 0 and l == 0:
                        z_product(l, k, width)
                    if c == 1 and mid:
                        mid()
                if chunks[-1] == 3:
                    pe.reg_add(n_tab, n_tab, 1)

            pe.wait_ge(s_const, CONSTS)
            pe.wait_ge(s_wload, 16 * 4)
            pe.wait_ge(s_wz, 1)
            n_xin = [counter(pe, f"pe_xin{k}", 16) for k in range(4)]
            n_hT = [counter(pe, f"pe_hT{k}", 1) for k in range(4)]
            n_er = counter(pe, "pe_er", 1)

            def transpose_x(k):
                pe.wait_ge(s_xin[k], n_xin[k])
                pe.reg_add(n_xin[k], n_xin[k], 16)
                pe.transpose(ps_xT[k], xin[k][:], ident[:]).then_inc(s_xT_ps, 1)

            def transposed_x(k):
                pe.wait_ge(s_hT[k], n_hT[k])
                pe.sem_inc(s_xin_used[k], 1)

            def natural_er(k):
                transposed_x(k)
                pe.wait_ge(s_er, n_er)
                pe.reg_add(n_er, n_er, 1)
                pe.matmul(ps_gat[:, 0:H + D], hT[k][:], wz[:, 0, D + H:ZW], start=True, stop=True
                          ).then_inc(s_er_ps, 1)
                pe.reg_add(n_hT[k], n_hT[k], 1)

            def natural_rows(k, next_x=False):
                transposed_x(2 + k)
                table_products(0, 2 + k, n_hT[2 + k], D + H, mid=(lambda: transpose_x(3 - k)) if next_x else None)
                pe.reg_add(n_hT[2 + k], n_hT[2 + k], 1)

            for j in range(3):
                pe.sem_inc(s_oh_used[j], 1)
            hist = ps_cnt[0:LO, 0:HI]
            pe.matmul(hist, zeros_bf[0:EP, 0:LO], zeros_bf[0:EP, 0:HI], start=True, stop=False,
                      skip_group_check=True)
            n_oh = counter(pe, "pe_oh", 1)

            def count_batch(j):
                pe.wait_ge(s_oh[j], n_oh)
                for c in range(HB):
                    mm = pe.matmul(hist, oh[j][0:EP, 0:LO, c], oh[j][0:EP, LO:LO + HI, c], start=False,
                                   stop=False, skip_group_check=True)
                mm.then_inc(s_oh_used[j], 1)

            for t in range(ER_AHEAD):
                transpose_x(t % 2)
                natural_er(t % 2)
            pe.wait_ge(s_wrload, 16)

            def round_(k):
                transpose_x(1)
                count_batch(0)
                natural_er(1)
                transpose_x(2 + k)
                transpose_x(0)
                count_batch(1)
                natural_er(0)
                natural_rows(k)
                count_batch(2)
                pe.reg_add(n_oh, n_oh, 1)

            with pe.Fori(0, (ROUNDS - 1) // 2):
                round_(0)
                round_(1)
            round_(0)
            transpose_x(3)
            pe.matmul(hist, zeros_bf[0:EP, 0:LO], zeros_bf[0:EP, 0:HI], start=False, stop=True,
                      skip_group_check=True).then_inc(s_hist, 1)
            pe.wait_ge(s_cnt, 1)
            halves = counts[:].rearrange("p (t o) -> p o t", o=2)
            pe.matmul(ps_rel[:, 0:T], ident[0:LO, :], halves[:, 0], start=True, stop=False)
            pe.matmul(ps_rel[:, 0:T], shift[:], halves[:, 1], start=False, stop=True).then_inc(s_deg_nat, 1)
            pe.wait_ge(s_cls, 1)
            pe.wait_ge(s_er, T + 1)
            for t in range(T):
                mm = pe.matmul(ps_gat[:, t:t + 1], oh_cls[:, :, t], values[:, 1, 0:1], start=True, stop=True)
            mm.then_inc(s_cls_ps, 1)
            natural_rows(1, next_x=True)
            pe.wait_ge(s_deg, 1)
            pe.matmul(ps_cnt[:, 128:128 + T], upper[:], degree[:], start=True, stop=False)
            pe.matmul(ps_cnt[:, 128:128 + T], ones[:], before[:], start=False, stop=True)
            pe.wait_ge(s_cls_cum, 1)
            pe.matmul(ps_gat[:, 64:65], lower[:], cls_cum[:, T - 1:T], start=True, stop=True
                      ).then_inc(s_above_ps, 1)
            pe.wait_ge(s_uns_in, 1)
            pe.matmul(ps_cnt[:, 256:257], ones[0:EP, :], unsorted_f[0:EP, :], start=True, stop=True)
            pe.wait_ge(s_tws, 1)
            pe.matmul(ps_cnt[:, 260:261], ones[0:EP, :], wsum[0:EP, 0:1], start=True, stop=True
                      ).then_inc(s_start_ps, 1)
            natural_rows(0, next_x=True)
            for c in range(-(-T // 4)):
                tiles = range(4 * c, min(4 * c + 4, T))
                place = (ps_rel, ps_gat)[c % 2][:, 0:len(tiles) * CLS].rearrange("p (t v) -> p t v", v=CLS)
                pe.wait_ge(s_diag, c + 1)
                if c >= 2:
                    pe.wait_ge(s_picked, c - 1)
                pe.matmul(place, upper_bf[:], oh_cls[:, :, tiles[0]:tiles[-1] + 1].rearrange("p v t -> p t v"),
                          start=True, stop=False, skip_group_check=True)
                pe.matmul(place, ones[:], diag[c % 2][:, 0:len(tiles)], start=False, stop=True,
                          skip_group_check=True).then_inc(s_place_ps, 1)
            LAST = 4
            with pe.Fori(0, (T - ROUNDS - 2 - LAST) // 2):
                natural_rows(1, next_x=True)
                natural_rows(0, next_x=True)
            pe.wait_ge(s_meta_cols, 3)
            pe.transpose(ps_cnt[0:T, 0:P], cnt_r[:], ident[:]).then_inc(s_deg_ps, 1)
            with pe.Fori(0, (LAST - 2) // 2):
                natural_rows(1, next_x=True)
                natural_rows(0, next_x=True)
            natural_rows(1, next_x=True)
            natural_rows(0)

            pe.wait_ge(s_bload, 16 * (5 + 3 * L))
            pe.wait_ge(s_slots, 16)
            n_land = {b: counter(pe, f"pe_land_{b}", 16 * GK[b]) for b in GA}
            n_g = counter(pe, "pe_group", 1)
            n_e = counter(pe, "pe_epi", 1)
            n_e0 = counter(pe, "pe_epi0", 1)
            n_lowered = counter(pe, "pe_lowered", 1)
            for b in GROUPS:
                pe.sem_inc(s_free[b], 1)

            def group(b, first=False, mid=None, n_slots=None):
                K = GK[b]

                def relation_sum(b):
                    pe.wait_ge(s_landed[b], n_land[b])
                    pe.reg_add(n_land[b], n_land[b], 16 * GK[b])
                    if first:
                        pe.wait_ge(s_h2, n_h)
                    for k in range(GK[b]):
                        pe.matmul(ps_rel[:, 0:D], ident[:], slots[b][:, k, 0:D], start=first and k == 0,
                                  stop=True, skip_group_check=True)

                if b == "t7":
                    pieces(pe, n_slots, relation_sum)
                else:
                    relation_sum(b)
                if mid:
                    mid()
                pe.wait_ge(s_zx, n_g)
                zs = zx[:].rearrange("p k h e -> p k (h e)")
                W = H * EX
                for k in range(K):
                    mm = pe.matmul(ps_gat[:, 0:W], ident[:], zs[:, 8 - K + k, :], start=(k == 0),
                                   stop=(k == K - 1))
                    if k == 0:
                        mm.then_inc(s_free[b], 1)
                mm.then_inc(s_gat, 1)
                pe.reg_add(n_g, n_g, 1)

            def transpose_sums(l):
                pe.wait_ge(s_h2, n_h)
                pe.transpose(mix[0], hr[:], ident[:])
                pe.transpose(mix[1], hg[:].rearrange("p h c -> p (h c)"), ident[:]).then_inc(s_T_ps, 1)

            def fuse(l):
                pe.wait_ge(s_T, n_e)
                if l < L - 1:
                    pe.matmul(mix[2], wfuse[:, 0], hrT[:], start=True, stop=False)
                    pe.matmul(mix[2], wfuse[:, 1], hgT[:], start=False, stop=True).then_inc(s_fuse, 1)
                else:
                    pe.matmul(mix[2], ones[0:1, :], bfuse_row[:], start=True, stop=False)
                    pe.matmul(mix[2], hrT[:], wfuse[:, 0], start=False, stop=False)
                    pe.matmul(mix[2], hgT[:], wfuse[:, 1], start=False, stop=True).then_inc(s_fuse, 1)

            def gate(l):
                if l == 0:
                    pe.wait_ge(s_hc, n_e0)
                    pe.matmul(mix[3], wgate[:], hc[:], start=True, stop=True).then_inc(s_gate_ps, 1)

            def half_table(l):
                if l < L - 1:
                    table_products(l + 1, 0, n_hT[0], chunks=range(2))

            def rest_of_table(l):
                if l < L - 1:
                    table_products(l + 1, 0, n_hT[0], chunks=range(2, 4))
                    pe.reg_add(n_hT[0], n_hT[0], 1)
                if l == 0:
                    pe.reg_add(n_e0, n_e0, 1)
                pe.reg_add(n_e, n_e, 1)

            n_h = counter(pe, "pe_h2", 1)

            def tile(l, t, previous):
                n, pairs, in_first = load_slots(pe, t)
                split = previous and l < L - 1
                if previous:
                    group("A", first=True, mid=lambda: transpose_sums(l))
                    fuse(l)
                    group("B", mid=lambda: gate(l))
                    half_table(l)
                    if split:
                        with pe.If(in_first > 1):
                            group("A")
                    rest_of_table(l)
                    if split:
                        with pe.If(in_first > 1):
                            group("B")
                else:
                    group("A", first=True)
                    group("B")
                pair_loops(pe, 2 if split else 1, pairs, in_first, n_lowered, n_land,
                           lambda hub: (group("A"), group("B")))
                tail_groups(pe, n, lambda b: group(b, n_slots=n))
                pe.reg_add(n_h, n_h, 1)

            for l in range(L):
                tile(l, 0, False)
                with pe.Fori(1, T) as t:
                    tile(l, t, True)
                transpose_sums(l)
                fuse(l)
                gate(l)
                half_table(l)
                rest_of_table(l)

        @block.vector
        def _(dve):
            v = nc.vector
            done = 0

            def step(ins):
                nonlocal done
                done += 1
                ins.then_inc(s_v, 1)
                dve.wait_ge(s_v, done)

            dve.wait_ge(s_const, CONSTS)
            v.tensor_copy(upper_bf[:], upper[:])
            v.tensor_copy(values[:], bc_last(iota_row[:], HB))
            dve.wait_ge(s_dload, 16)
            v.tensor_scalar(lo_i[:], dst_i[:], LO - 1, None, ALU.bitwise_and)
            step(v.tensor_scalar(hi_i[:], dst_i[:], LO.bit_length() - 1, None, ALU.logical_shift_right))
            v.tensor_copy(lo_bf[:], lo_i[:])
            step(v.tensor_copy(hi_bf[:], hi_i[:]))

            n = counter(dve, "v_oh", 1)

            def onehots(batch, j):
                dve.wait_ge(s_oh_used[j], n)
                at = batch * HB
                v.tensor_tensor(oh[j][0:EP, LO:LO + HI, :], bc(hi_bf[:, bass.ds(at, HB)], HI), values[0:EP, 0:HI, :],
                                ALU.is_equal)
                v.tensor_tensor(oh[j][0:EP, 0:LO, :], bc(lo_bf[:, bass.ds(at, HB)], LO), values[0:EP, 0:LO, :],
                                ALU.is_equal).then_inc(s_oh[j], 1)

            def fold(l):
                nonlocal folded
                for i in range(2):
                    folded += 1
                    v.tensor_tensor(attn_tmp[:], wz[:, l, 0:D], attn[:, i, l], ALU.mult).then_inc(s_fold, 1)
                    dve.wait_ge(s_fold, folded)
                    r = v.tensor_reduce(wz[:, l, D + i * H:D + (i + 1) * H],
                                        attn_tmp[:].rearrange("p (h c) -> p h c", h=H), AX.X, ALU.add)
                    if i == 0:
                        folded += 1
                        r.then_inc(s_fold, 1)
                        dve.wait_ge(s_fold, folded)
                    else:
                        r.then_inc(s_wz, 1)
                        dve.wait_ge(s_wz, l + 1)

            folded = 0
            dve.wait_ge(s_wload, 16 * 4)
            fold(0)
            with dve.Fori(0, EC // (3 * HB)) as i:
                for j in range(3):
                    onehots(i * 3 + j, j)
                dve.reg_add(n, n, 1)

            dve.wait_ge(s_hist, 1)
            v.tensor_copy(counts[:], ps_cnt[0:LO, 0:HI]).then_inc(s_cnt, 1)
            dve.wait_ge(s_eload, 16 * 5)
            v.scalar_tensor_tensor(src_i[:], src_i[:], float(R), typ_i[:], ALU.mult, ALU.add).then_inc(s_edge_rows, 1)
            dve.wait_ge(s_deg_nat, 1)
            step(v.tensor_copy(degree[:], ps_rel[:, 0:T]))
            step(v.tensor_scalar(cls[:], degree[:], float(CLS - 1), None, ALU.min))
            v.tensor_tensor(oh_cls, bc(cls[:], CLS), values[:, :, 0:T], ALU.is_equal).then_inc(s_cls, 1)
            v.memset(before[:, 0:1], 0.0)
            v.tensor_tensor_scan(before[:, 1:T], ones[:, 0:T - 1], degree[:, 0:T - 1], 0.0, ALU.mult, ALU.add
                                 ).then_inc(s_deg, 1)
            v.tensor_copy(meta_nat[:, :, M_CNT], degree[:])
            step(v.tensor_tensor(dst_next[:], dst_i[:], dst_next[:], ALU.is_gt))
            v.tensor_reduce(unsorted_f[0:EP, :], dst_next[:], AX.X, ALU.add).then_inc(s_uns_in, 1)

            dve.wait_ge(s_cls_ps, 1)
            step(v.tensor_copy(cls_count[:], ps_gat[:, 0:T]))
            v.tensor_tensor_scan(cls_cum[:], ones[:, 0:T], cls_count[:], 0.0, ALU.mult, ALU.add
                                 ).then_inc(s_cls_cum, 1)
            dve.wait_ge(s_ewload, 16)
            v.tensor_reduce(wsum[0:EP, 0:1], ew[:], AX.X, ALU.add).then_inc(s_tws, 1)
            dve.wait_ge(s_above_ps, 1)
            step(v.tensor_copy(cls_above[:], ps_gat[:, 64:65]))
            v.tensor_copy(cls_base[:, 0:1], cls_above[:])
            step(v.tensor_scalar(cls_base[:, 1:T], cls_cum[:, 0:T - 1], cls_above[:], None, ALU.add))

            chunks = [range(4 * c, min(4 * c + 4, T)) for c in range(-(-T // 4))]

            def diagonals(c):
                tiles = chunks[c]
                v.tensor_tensor(diag[c % 2][:, 0:len(tiles)], bc(ident[:], len(tiles)),
                                bc_last(cls_base[:, tiles[0]:tiles[-1] + 1], CLS), ALU.mult).then_inc(s_diag, 1)

            diagonals(0)
            diagonals(1)
            for c, tiles in enumerate(chunks):
                dve.wait_ge(s_place_ps, c + 1)
                place = (ps_rel, ps_gat)[c % 2][:, 0:len(tiles) * CLS].rearrange("p (t v) -> p t v", v=CLS)
                v.tensor_tensor(picked[c % 2][:, 0:len(tiles)], place,
                                oh_cls[:, :, tiles[0]:tiles[-1] + 1].rearrange("p v t -> p t v"), ALU.mult
                                ).then_inc(s_picked, 1)
                if c + 2 < len(chunks):
                    diagonals(c + 2)
                dve.wait_ge(s_picked, c + 1)
                step(v.tensor_reduce(rank[:, tiles[0]:tiles[-1] + 1], picked[c % 2][:, 0:len(tiles)], AX.X, ALU.add))
            dve.wait_ge(s_start_ps, 1)
            step(v.tensor_copy(starts[:], ps_cnt[:, 128:128 + T]))
            v.tensor_copy(meta_nat[:, :, M_START], starts[:])
            v.tensor_copy(rank_u[:], rank[:]).then_inc(s_rank, 1)

            v.tensor_scalar(unsorted_i[:], ps_cnt[0:1, 256:257], 1.0, None, ALU.min).then_inc(s_uns, 1)
            step(v.tensor_scalar(tw_mean[:], ps_cnt[:, 260:261], 1.0 / E, None, ALU.mult))
            dve.wait_ge(s_bload, 16 * (5 + 3 * L))
            step(v.tensor_scalar(gate_bias[:], bgate[:, 1:2], tw_mean[:], bgate[:, 0:1], ALU.mult, ALU.add))
            v.tensor_scalar(gate_bias[:], gate_bias[:], 0.5, None, ALU.mult).then_inc(s_gbias, 1)
            for l in range(1, L):
                fold(l)

            dve.wait_ge(s_uns, 1)
            bad = dve.value_load(unsorted_i[0:1, 0:1], min_val=0, max_val=1)
            with dve.If(bad > 0):
                n_ld = counter(dve, "v_sort_ld", 48)
                n_cur = counter(dve, "v_sort_cur", 16)
                n_c = counter(dve, "v_sort_c", 1)

                def sort_step(ins):
                    ins.then_inc(s_sort_c, 1)
                    dve.wait_ge(s_sort_c, n_c)
                    dve.reg_add(n_c, n_c, 1)

                sort_step(v.tensor_scalar(lo_i[:], dst_i[:], P - 1, None, ALU.bitwise_and))
                sort_step(v.tensor_scalar(hi_i[:], dst_i[:], P.bit_length() - 1, None, ALU.logical_shift_right))
                dve.wait_ge(s_edge_rows, 1)
                v.scalar_tensor_tensor(typ_i[:], lo_i[:], float(T), hi_i[:], ALU.mult, ALU.add
                                       ).then_inc(s_edge_rows, 1)

                with dve.Fori(0, EC):
                    dve.wait_ge(s_sort_ld, n_ld)
                    dve.wait_ge(s_sort_cur, n_cur)
                    dve.reg_add(n_ld, n_ld, 48)
                    dve.reg_add(n_cur, n_cur, 16)
                    sort_step(v.tensor_copy(sort_f[:, 0:1], sort_key[:]))
                    sort_step(v.tensor_scalar(sort_eq[:, 0], sort_keys[:], sort_f[:, 0:1], None, ALU.is_equal))
                    sort_step(v.tensor_tensor(sort_eq[:, 1], sort_eq[:, 0], upper[0:EP, 0:EP], ALU.mult))
                    v.tensor_reduce(sort_f[:, 2:3], sort_eq[:, 1], AX.X, ALU.add)
                    sort_step(v.tensor_reduce(sort_f[:, 1:2], sort_eq[:, 0], AX.X, ALU.add))
                    sort_step(v.tensor_tensor(sort_f[:, 1:2], sort_f[:, 1:2], sort_f[:, 2:3], ALU.subtract))
                    sort_step(v.tensor_tensor(sort_new[:], sort_f[:, 1:2], sort_cur[:], ALU.add))
                    v.tensor_scalar(sort_pos[:], sort_new[:], -1.0, None, ALU.add)
                    sort_step(v.tensor_scalar(sort_f[:, 3:4], sort_f[:, 2:3], 0.0, float(NP_), ALU.is_gt, ALU.mult))
                    v.tensor_tensor(sort_cell[:], sort_f[:, 3:4], sort_f[:, 0:1], ALU.add).then_inc(s_sort_v, 1)

            dve.wait_ge(s_meta_head, 16)
            v.tensor_copy(start_u[:], meta[:, :, M_START]).then_inc(s_meta_cols, 1)
            v.tensor_copy(id_u[:], meta[:, :, M_ID]).then_inc(s_meta_cols, 1)
            v.tensor_copy(cnt_r[:], meta[:, :, M_CNT]).then_inc(s_meta_cols, 1)
            dve.wait_ge(s_deg_ps, 1)
            step(v.tensor_reduce(tile_slots_f[:], ps_cnt[0:T, 0:P], AX.X, ALU.max))
            v.tensor_scalar(tile_slots_col[:], tile_slots_f[:], float(PAIR), None, ALU.max).then_inc(s_slots_col, 1)
            dve.wait_ge(s_meta_cols, 3)
            step(v.tensor_tensor(ell_valid, bc(iota_slot[:], T), bc_last(cnt_r[:], ELL), ALU.is_lt))
            dve.wait_ge(s_ell, 16 * T)
            step(v.scalar_tensor_tensor(ell_valid, ell[:, 0:T], -float(NULL), ell_valid, ALU.add, ALU.mult))
            v.tensor_scalar(ell[:, 0:T], ell_valid, float(NULL), None, ALU.add).then_inc(s_ell_ok, 1)
            dve.wait_ge(s_ell_ok, 1)
            v.tensor_copy(ell[:, T], ell[:, 0]).then_inc(s_ell_ok, 1)
            v.tensor_copy(stage_head[:].bitcast(I32), ell[:, 0, 0:PAIR]).then_inc(s_head, 1)
            for b in "AB":
                v.memset(stage_mid[b][:].bitcast(I32), 0).then_inc(s_mid[b], 1)
            for b in TAIL[1:]:
                v.memset(stage_tail[b][:].bitcast(I32), 0)
            v.memset(slots["t7"], 0.0)
            v.memset(stage_tail["t8"][:].bitcast(I32), 0).then_inc(s_tail, 1)
            dve.wait_ge(s_ell_ok, 2)

            v.memset(acc[:], 0.0).then_inc(s_acc, 1)
            dve.wait_ge(s_slots, 16)
            dve.wait_ge(s_meta, 16)
            dve.sem_inc(s_h2, 1)
            n_land = {b: counter(dve, f"v_land_{b}", 16 * GK[b]) for b in GA}
            n_g = counter(dve, "v_group", 1)
            n_t = counter(dve, "v_tile", 1)
            n_lowered = counter(dve, "v_lowered", 1)
            n_norm = counter(dve, "v_norm", 1)
            n_e = counter(dve, "v_epi", 1)
            n_out = counter(dve, "v_out", 16)

            ell_flat = ell[:].rearrange("p t j -> p (t j)")
            n_head = counter(dve, "v_head", 1)
            n_mid = {b: counter(dve, f"v_mid_{b}", 1) for b in "AB"}
            n_tail = counter(dve, "v_tail_staged", 1)
            n_stored = counter(dve, "v_stored", 16)
            n_id_out = counter(dve, "v_id_out", 16)
            mid_at = counter(dve, "v_mid_at", 0)
            piece_at = counter(dve, "v_piece_at", 0)

            def copy_indices(to, at, K):
                here = dve.snap(at, min_val=0, max_val=(T + 1) * ELL - K)
                return v.tensor_copy(to.bitcast(I32), ell_flat[:, bass.ds(here, K)])

            def stage_mids(b):
                dve.wait_ge(s_mid[b], n_mid[b])
                dve.reg_add(n_mid[b], n_mid[b], 1)
                copy_indices(stage_mid[b][:], mid_at, 8).then_inc(s_mid[b], 1)
                dve.reg_add(mid_at, mid_at, 8)

            def stage_tails(t, n, in_first):
                dve.wait_ge(s_tail, n_tail)
                dve.reg_add(n_tail, n_tail, 1)
                for b, K in [(b, GK[b]) for b in TAIL]:
                    dve.reg_alu(piece_at, n, PAIR - 2 * K, ALU.bitwise_and)
                    dve.reg_alu(piece_at, piece_at, dve.snap(in_first * PAIR + t * ELL), ALU.add)
                    copy_indices(stage_tail[b][:], piece_at, K)
                ins = v.memset(slots["t7"][:, :, 2 * D:ROW], LEAST)
                ins.then_inc(s_tail, 1)

            def stage_next_head(t):
                dve.wait_ge(s_head, n_head)
                dve.reg_add(n_head, n_head, 1)
                v.tensor_copy(stage_head[:].bitcast(I32), ell_flat[:, bass.ds((t + 1) * ELL, PAIR)]).then_inc(s_head, 1)

            def stage_ids(l, t, last=False):
                if not last:
                    dve.wait_ge(s_stored, n_stored)
                if l < L - 1:
                    dve.reg_add(n_stored, n_stored, 16)
                elif not last:
                    dve.wait_ge(s_out, n_id_out)
                    dve.reg_add(n_id_out, n_id_out, 16)
                v.tensor_copy(stage_id[last][:].bitcast(I32), id_u[:, bass.ds(t, 1)].bitcast(I32)).then_inc(s_id, 1)

            def group(b, stage=False, n_slots=None, meanwhile=None):
                K = GK[b]
                lo = 8 - K

                def landed(b):
                    dve.wait_ge(s_landed[b], n_land[b])
                    dve.reg_add(n_land[b], n_land[b], 16 * GK[b])

                if b == "t7":
                    dve.wait_ge(s_tail, n_tail)
                    pieces(dve, n_slots, landed)
                else:
                    landed(b)
                if stage:
                    stage_mids(b)
                dve.wait_ge(s_acc, n_g)
                v.tensor_tensor(raw[:, lo:8], slots[b][:, :, 2 * D:ROW], er_cur[:].to_broadcast([P, K, H]), ALU.add
                                ).then_inc(s_raw, 1)
                dve.wait_ge(s_raw, n_g)
                v.tensor_reduce(top[:, 0], raw[:, lo:9].rearrange("p k h -> p h k"), AX.X, ALU.max
                                ).then_inc(s_top, 1)
                v.scalar_tensor_tensor(leaky[:, lo:9], raw[:, lo:9], SLOPE, raw[:, lo:9], ALU.mult, ALU.max
                                       ).then_inc(s_leaky, 1)
                dve.wait_ge(s_top, n_g)
                v.scalar_tensor_tensor(peak[:], top[:], SLOPE, top[:], ALU.mult, ALU.max).then_inc(s_peak, 1)
                dve.wait_ge(s_leaky, n_g)
                v.tensor_copy(raw[:, 8:9], top[:]).then_inc(s_keep, 1)
                dve.wait_ge(s_peak, n_g)
                v.tensor_tensor(logit[:, lo:9], leaky[:, lo:9], peak[:].to_broadcast([P, K + 1, H]), ALU.subtract
                                ).then_inc(s_logit, 1)
                dve.wait_ge(s_keep, n_g)
                dve.wait_ge(s_wgt, n_g)
                v.tensor_tensor(zx[:, lo:8, :, 0:DH], slots[b][:, :, D:2 * D].rearrange("p k (h c) -> p k h c", h=H),
                                zx[:, lo:8, :, DH:EX].to_broadcast([P, K, H, DH]), ALU.mult).then_inc(s_zx, 1)
                v.tensor_tensor(acc[:], acc[:], zx[:, 8, :, DH:EX].to_broadcast([P, H, EX]), ALU.mult
                                ).then_inc(s_scaled, 1)
                if meanwhile:
                    meanwhile()
                dve.wait_ge(s_scaled, n_g)
                dve.wait_ge(s_gat, n_g)
                v.tensor_tensor(acc[:], acc[:], ps_gat[:, 0:H * EX].rearrange("p (h e) -> p h e", h=H), ALU.add
                                ).then_inc(s_acc, 1)
                dve.reg_add(n_g, n_g, 1)

            def start_tile(t):
                v.tensor_copy(er_cur[:], meta[:, bass.ds(t, 1), M_ER:M_LOOP])
                v.memset(raw[:, 8:9], LEAST).then_inc(s_tile, 1)
                dve.wait_ge(s_tile, n_t)
                dve.reg_add(n_t, n_t, 1)

            def end_tile(t):
                dve.wait_ge(s_acc, n_g)
                v.reciprocal(rden[:], acc[:, :, DH:EX]).then_inc(s_rden, 1)
                v.tensor_tensor(hr[:], ps_rel[:, 0:D], meta[:, bass.ds(t, 1), M_LOOP:M_X].rearrange("p o f -> p (o f)"),
                                ALU.add)
                dve.wait_ge(s_rden, n_rd)
                dve.reg_add(n_rd, n_rd, 1)
                v.tensor_tensor(hg[:], acc[:, :, 0:DH], rden[:].to_broadcast([P, H, DH]), ALU.mult
                                ).then_inc(s_h2, 1)

            n_rd = counter(dve, "v_rden", 1)

            def norm_step(ins):
                ins.then_inc(s_norm, 1)
                dve.wait_ge(s_norm, n_norm)
                dve.reg_add(n_norm, n_norm, 1)

            def epilogue(l, t, last=False):
                if l == 0:
                    dve.wait_ge(s_th, n_e)
                    v.scalar_tensor_tensor(th[:], th[:], 1.0, hc[:], ALU.add, ALU.mult).then_inc(s_gated, 1)
                    dve.wait_ge(s_gated, n_e)
                    v.tensor_scalar(hT[0][:], th[:], 0.5, 0.0, ALU.mult, ALU.max).then_inc(s_hT[0], 1)
                    dve.reg_add(n_e, n_e, 1)
                elif l == L - 1:
                    for _ in range(3):
                        norm_step(v.tensor_scalar(nv[:, 1:2], nv[:, 0:1], nv[:, 0:1], ve[:], ALU.mult, ALU.mult))
                        norm_step(v.tensor_scalar(nv[:, 1:2], nv[:, 1:2], -0.5, 1.5, ALU.mult, ALU.add))
                        norm_step(v.tensor_tensor(nv[:, 0:1], nv[:, 0:1], nv[:, 1:2], ALU.mult))
                    if not last:
                        dve.wait_ge(s_out, n_out)
                        dve.reg_add(n_out, n_out, 16)
                    v.tensor_scalar(yo[last][:], y[:], mv[:, 0:1], nv[:, 0:1], ALU.subtract, ALU.mult).then_inc(s_yo, 1)

            def norm_statistics(l, t):
                if l == L - 1:
                    dve.wait_ge(s_fuse, n_f)
                    dve.reg_add(n_f, n_f, 1)
                    norm_step(v.scalar_tensor_tensor(y[:], mix[2], 0.0, meta[:, bass.ds(t, 1), M_X:META]
                                                     .rearrange("p o f -> p (o f)"), ALU.max, ALU.add))
                    norm_step(v.bn_stats(stats[:], y[:]))
                    norm_step(v.bn_aggr(mv[:], stats[:]))
                    norm_step(v.tensor_scalar(ve[:], mv[:, 1:2], EPS, None, ALU.add))
                    norm_step(v.tensor_scalar(nv_i[:], ve[:].bitcast(I32), 1, None, ALU.logical_shift_right))
                    norm_step(v.tensor_scalar(nv[:, 0:1].bitcast(I32), nv_i[:], -1.0, float(0x5f3759df),
                                              ALU.mult, ALU.add))

            n_f = counter(dve, "v_fuse", (L - 1) * T + 1)

            def between(l, t, previous):
                stage_next_head(t)
                if previous is not None:
                    stage_ids(l, previous)
                    norm_statistics(l, previous)

            def tile(l, t, previous):
                n, pairs, in_first = load_slots(dve, t)
                start_tile(t)
                dve.reg_mov(mid_at, t * ELL + PAIR)
                group("A", stage=True, meanwhile=lambda: stage_tails(t, n, in_first))
                group("B", stage=True, meanwhile=lambda: between(l, t, previous))
                if previous is not None:
                    epilogue(l, previous)
                pair_loops(dve, 1, pairs, in_first, n_lowered, n_land,
                           lambda hub: (group("A", not hub), group("B", not hub)))
                tail_groups(dve, n, lambda b: group(b, n_slots=n))
                end_tile(t)

            for l in range(L):
                if l:
                    dve.wait_ge(s_rows, T + 1 + l * T)
                tile(l, 0, None)
                with dve.Fori(1, T) as t:
                    tile(l, t, t - 1)
                stage_ids(l, T - 1, last=True)
                norm_statistics(l, T - 1)
                epilogue(l, T - 1, last=True)


_INS = ['x', 'src', 'dst', 'edge_type_16', 'edge_weight', 'L0_gnn_W_rel', 'L0_gnn_b_rel', 'L0_gnn_W_loop',
        'L0_gnn_W_gat', 'L0_gnn_attn_l', 'L0_gnn_attn_r', 'L0_gnn_b_gat', 'L0_gnn_W_fuse', 'L0_gnn_b_fuse',
        'L0_gnn_W_gate', 'L0_gnn_b_gate']


def kernel(**inputs):
    import numpy as _np
    import concourse.bacc as _bacc
    from concourse.bass_utils import run_bass_kernel_spmd as _run

    nc = _bacc.Bacc("TRN2", target_bir_lowering=False, num_devices=1)
    arrays, args = {}, []
    for name in _INS:
        a = _np.ascontiguousarray(inputs[name])
        arrays[f"in_{name}"] = a
        args.append(nc.dram_tensor(f"in_{name}", a.shape, mybir.dt.from_np(a.dtype), kind="ExternalInput").ap())
    out = nc.dram_tensor("out", inputs["x"].shape, F32, kind="ExternalOutput").ap()
    gnn_kernel(nc, *args, out)
    r = _run(nc, [arrays], core_ids=[0])
    return r.results[0]["out"]
```
